# Optimizing a Trainium2 kernel written in Bass

```python
import numpy as np
import jax
import jax.numpy as jnp

def _softmax(x, axis=-1):
    return jax.nn.softmax(x, axis=axis)

def _gelu(x):
    return jax.nn.gelu(x, approximate=True)

def _silu(x):
    return jax.nn.silu(x)

def _sigmoid(x):
    return jax.nn.sigmoid(x)

def _layernorm(x, axis=-1, eps=1e-05):
    m = jnp.mean(x, axis=axis, keepdims=True)
    v = jnp.var(x, axis=axis, keepdims=True)
    return (x - m) / jnp.sqrt(v + eps)

def _scatter_add(tgt, idx, src, axis=0):
    return tgt.at[idx].add(src)

def _segment_sum(src, seg, n):
    return jax.ops.segment_sum(src, seg, n)
kernel_name = 'mk_adj_ffn_d4_adj_r2_6a4dfa'

def setup_inputs(seed: int=0):
    np.random.seed(seed)
    _w = jnp.asarray

    def _rec_inputs():
        import jax
        import jax.numpy as jnp
        _gk = jax.random.key(seed)
        x = 7.22e-05 + 1 * jax.random.normal(jax.random.fold_in(_gk, 1), (64, 128, 128), jnp.float32)
        _a = jax.random.bernoulli(jax.random.fold_in(_gk, 2), 0.125, (64, 128, 128))
        _a = jnp.logical_or(_a, jnp.swapaxes(_a, -1, -2))
        _a = jnp.logical_or(_a, jnp.eye(128, dtype=bool))
        _af = _a.astype(jnp.float32)
        adj = _af
        return (x, adj)
    x, adj = _rec_inputs()

    def _L0_gnn_setup():
        import jax, jax.numpy as jnp
        import numpy as np
        from jax import lax
        DIM = 128
        EPS = 1e-05

        def _bn(h, g, b, m, v):
            scale = g / jnp.sqrt(v + EPS)
            return h * scale[None, :, None] + (b - m * scale)[None, :, None]

        def _conv1d(h, w, pad):
            return lax.conv_general_dilated(h, w, window_strides=(1,), padding=[(pad, pad)], dimension_numbers=('NCH', 'OIH', 'NCH'))
        key = jax.random.key(seed)
        ks = jax.random.split(key, 16)
        bs, n, d = (16, 1024, DIM)
        s = 0.05
        return {'x': jax.random.normal(ks[0], (bs, n, d), jnp.float32), 'mask': jnp.ones((bs, n, n), jnp.float32), 'w_se': jax.random.normal(ks[1], (3, d), jnp.float32) * s, 'b_se': jnp.zeros((3,), jnp.float32), 'conv1_w': jax.random.normal(ks[2], (d, d, 1), jnp.float32) * s, 'bn1_g': jnp.ones((d,), jnp.float32), 'bn1_b': jnp.zeros((d,), jnp.float32), 'bn1_m': jnp.zeros((d,), jnp.float32), 'bn1_v': jnp.ones((d,), jnp.float32), 'conv2_w': jax.random.normal(ks[3], (d, d, 17), jnp.float32) * s, 'bn2_g': jnp.ones((d,), jnp.float32), 'bn2_b': jnp.zeros((d,), jnp.float32), 'bn2_m': jnp.zeros((d,), jnp.float32), 'bn2_v': jnp.ones((d,), jnp.float32), 'w_msg': jax.random.normal(ks[4], (d, d), jnp.float32) * s, 'b_msg': jnp.zeros((d,), jnp.float32), 'w_ih': jax.random.normal(ks[5], (3 * d, 2 * d), jnp.float32) * s, 'b_ih': jnp.zeros((3 * d,), jnp.float32), 'w_hh': jax.random.normal(ks[6], (3 * d, d), jnp.float32) * s, 'b_hh': jnp.zeros((3 * d,), jnp.float32)}
    _L0_gnn_all = _L0_gnn_setup()
    _L0_gnn_in = {k: v for k, v in _L0_gnn_all.items() if k in ('w_se', 'b_se', 'conv1_w', 'bn1_g', 'bn1_b', 'bn1_m', 'bn1_v', 'conv2_w', 'bn2_g', 'bn2_b', 'bn2_m', 'bn2_v', 'w_msg', 'b_msg', 'w_ih', 'b_ih', 'w_hh', 'b_hh')}
    del _L0_gnn_all

    def _L0_ffn_setup():
        import jax, jax.numpy as jnp
        import numpy as np
        B, S, D, E, H, K = (4, 2048, 128, 8, 256, 2)
        key = jax.random.key(seed)
        ks = jax.random.split(key, 6)
        x = jax.random.normal(ks[0], (B, S, D), jnp.float32)
        Wg = jax.random.normal(ks[1], (D, E), jnp.float32) * 0.02
        bg = jnp.zeros((E,), jnp.float32)
        W1 = jax.random.normal(ks[2], (E, D, H), jnp.float32) * 0.02
        b1 = jnp.zeros((E, H), jnp.float32)
        W2 = jax.random.normal(ks[3], (E, H, D), jnp.float32) * 0.02
        b2 = jnp.zeros((E, D), jnp.float32)
        return {'x': x, 'Wg': Wg, 'bg': bg, 'W1': W1, 'b1': b1, 'W2': W2, 'b2': b2}
    _L0_ffn_all = _L0_ffn_setup()
    _L0_ffn_in = {k: v for k, v in _L0_ffn_all.items() if k in ('Wg', 'bg', 'W1', 'b1', 'W2', 'b2')}
    del _L0_ffn_all

    def _L1_gnn_setup():
        import jax, jax.numpy as jnp
        import numpy as np
        B, N, D = (8, 1024, 128)
        NEG = -9000000000000000.0
        key = jax.random.key(seed)
        ks = jax.random.split(key, 8)
        x = jax.random.normal(ks[0], (B, N, D), dtype=jnp.float32)
        adj = jax.random.randint(ks[1], (B, N, N), 0, 2).astype(jnp.float32)
        s = 1.0 / np.sqrt(D)
        W_w = jax.random.uniform(ks[2], (D, D), jnp.float32, -s, s)
        W_b = jax.random.uniform(ks[3], (D,), jnp.float32, -s, s)
        A = jax.random.normal(ks[4], (D, D), dtype=jnp.float32) * 0.02
        sg = 1.0 / np.sqrt(2 * D)
        gate_w = jax.random.uniform(ks[5], (1, 2 * D), jnp.float32, -sg, sg)
        gate_b = jax.random.uniform(ks[6], (1,), jnp.float32, -sg, sg)
        return {'x': x, 'adj': adj, 'W_w': W_w, 'W_b': W_b, 'A': A, 'gate_w': gate_w, 'gate_b': gate_b, 'use_adj': 1}
    _L1_gnn_all = _L1_gnn_setup()
    _L1_gnn_in = {k: v for k, v in _L1_gnn_all.items() if k in ('W_w', 'W_b', 'A', 'gate_w', 'gate_b')}
    del _L1_gnn_all

    def _L1_ffn_setup():
        import jax, jax.numpy as jnp
        import numpy as np
        E, D, H, TOP_K = (6, 128, 128, 2)
        ROUTER_H = D // 2
        key = jax.random.key(seed)
        ks = jax.random.split(key, 12)
        s = 1.0 / np.sqrt(D)
        sh = 1.0 / np.sqrt(H)
        sr = 1.0 / np.sqrt(ROUTER_H)
        return {'features': jax.random.normal(ks[0], (8, 2048, D), dtype=jnp.float32), 'router_w1': jax.random.uniform(ks[1], (D, ROUTER_H), jnp.float32, -s, s), 'router_b1': jnp.zeros((ROUTER_H,), jnp.float32), 'router_w2': jax.random.uniform(ks[2], (ROUTER_H, E), jnp.float32, -sr, sr), 'router_b2': jnp.zeros((E,), jnp.float32), 'expert_w1': jax.random.uniform(ks[3], (E, D, H), jnp.float32, -s, s), 'expert_b1': jnp.zeros((E, H), jnp.float32), 'expert_w2': jax.random.uniform(ks[4], (E, H, H), jnp.float32, -sh, sh), 'expert_b2': jnp.zeros((E, H), jnp.float32), 'expert_w3': jax.random.uniform(ks[5], (E, H, D), jnp.float32, -sh, sh), 'expert_b3': jnp.zeros((E, D), jnp.float32)}
    _L1_ffn_all = _L1_ffn_setup()
    _L1_ffn_in = {k: v for k, v in _L1_ffn_all.items() if k in ('router_w1', 'router_b1', 'router_w2', 'router_b2', 'expert_w1', 'expert_b1', 'expert_w2', 'expert_b2', 'expert_w3', 'expert_b3')}
    del _L1_ffn_all

    def _L2_gnn_setup():
        import jax, jax.numpy as jnp
        import numpy as np
        NEG = 9000000000000000.0
        key = jax.random.key(seed)
        ks = jax.random.split(key, 7)
        B, N, DIN, H, DOUT = (128, 256, 128, 128, 128)
        x = jax.random.normal(ks[0], (B, N, DIN), dtype=jnp.float32)
        mask = (jax.random.uniform(ks[1], (B, N, N)) > 0.5).astype(jnp.float32)

        def lin(k, fan_in, fan_out):
            kw, kb = jax.random.split(k)
            bound = 1.0 / np.sqrt(fan_in)
            W = jax.random.uniform(kw, (fan_in, fan_out), minval=-bound, maxval=bound, dtype=jnp.float32)
            b = jax.random.uniform(kb, (fan_out,), minval=-bound, maxval=bound, dtype=jnp.float32)
            return (W, b)
        Wv, bv = lin(ks[2], DIN, H)
        Wk, bk = lin(ks[3], DIN, H)
        Wq, bq = lin(ks[4], DIN, H)
        Wo, bo = lin(ks[5], H, DOUT)
        return {'x': x, 'mask': mask, 'Wv': Wv, 'bv': bv, 'Wk': Wk, 'bk': bk, 'Wq': Wq, 'bq': bq, 'Wo': Wo, 'bo': bo}
    _L2_gnn_all = _L2_gnn_setup()
    _L2_gnn_in = {k: v for k, v in _L2_gnn_all.items() if k in ('Wv', 'bv', 'Wk', 'bk', 'Wq', 'bq', 'Wo', 'bo')}
    del _L2_gnn_all

    def _L2_ffn_setup():
        import jax, jax.numpy as jnp
        import numpy as np
        DIM = 128
        HEADS = 8
        NUM_KEYS = 128
        NUM_KV = NUM_KEYS ** 2
        PK_TOPK = 16
        FINAL_TOPK = 16
        DIM_KEY = DIM // 2
        P = 2

        def _pk(x, Wq_pk, pk_keys):
            b, n, _ = x.shape
            q = (x @ Wq_pk).reshape(b, n, P, HEADS, DIM_KEY).transpose(2, 0, 1, 3, 4)
            sim = jnp.einsum('pbnhd,pkhd->pbnhk', q, pk_keys)
            scores, idx = jax.lax.top_k(sim, PK_TOPK)
            idx0 = idx[0]
            idx1 = idx[1] * NUM_KEYS
            index = (idx0[..., :, None] + idx1[..., None, :]).reshape(b, n, HEADS, PK_TOPK * PK_TOPK)
            score = (scores[0][..., :, None] + scores[1][..., None, :]).reshape(b, n, HEADS, PK_TOPK * PK_TOPK)
            final_scores, pk_idx = jax.lax.top_k(score, FINAL_TOPK)
            final_indices = jnp.take_along_axis(index, pk_idx, axis=-1)
            final_scores = jax.nn.softmax(final_scores, axis=-1)
            return (final_scores, final_indices)
        key = jax.random.key(seed)
        ks = jax.random.split(key, 7)
        b, n = (2, 512)
        std = 0.02
        x = jax.random.normal(ks[0], (b, n, DIM), dtype=jnp.float32)
        Wq_pk = jax.random.normal(ks[1], (DIM, P * HEADS * DIM_KEY), dtype=jnp.float32) * std
        pk_keys = jax.random.normal(ks[2], (P, NUM_KEYS, HEADS, DIM_KEY), dtype=jnp.float32) * std
        Wq = jax.random.normal(ks[3], (DIM, HEADS * DIM), dtype=jnp.float32) * std
        keys_table = jax.random.normal(ks[4], (NUM_KV * HEADS, DIM), dtype=jnp.float32) * std
        values_table = jax.random.normal(ks[5], (NUM_KV * HEADS, DIM), dtype=jnp.float32) * std
        Wo = jax.random.normal(ks[6], (DIM * HEADS, DIM), dtype=jnp.float32) * std
        return {'x': x, 'Wq_pk': Wq_pk, 'pk_keys': pk_keys, 'Wq': Wq, 'keys_table': keys_table, 'values_table': values_table, 'Wo': Wo}
    _L2_ffn_all = _L2_ffn_setup()
    _L2_ffn_in = {k: v for k, v in _L2_ffn_all.items() if k in ('Wq_pk', 'pk_keys', 'Wq', 'keys_table', 'values_table', 'Wo')}
    del _L2_ffn_all

    def _L3_gnn_setup():
        import jax, jax.numpy as jnp
        import numpy as np
        D_IN = 128
        D_HID = 256
        key = jax.random.key(seed)
        k1, k2, k3, k4, k5, k6 = jax.random.split(key, 6)
        x = jax.random.normal(k1, (8, 2048, D_IN), dtype=jnp.float32)
        adj = jax.random.uniform(k2, (8, 2048, 2048), dtype=jnp.float32)
        s1 = 1.0 / np.sqrt(D_IN)
        s2 = 1.0 / np.sqrt(D_HID)
        W1 = jax.random.uniform(k3, (D_IN, D_HID), dtype=jnp.float32, minval=-s1, maxval=s1)
        b1 = jax.random.uniform(k4, (D_HID,), dtype=jnp.float32, minval=-s1, maxval=s1)
        W2 = jax.random.uniform(k5, (D_HID, D_IN), dtype=jnp.float32, minval=-s2, maxval=s2)
        b2 = jax.random.uniform(k6, (D_IN,), dtype=jnp.float32, minval=-s2, maxval=s2)
        eps = jnp.zeros((1,), dtype=jnp.float32)
        return {'x': x, 'adj': adj, 'eps': eps, 'W1': W1, 'b1': b1, 'W2': W2, 'b2': b2}
    _L3_gnn_all = _L3_gnn_setup()
    _L3_gnn_in = {k: v for k, v in _L3_gnn_all.items() if k in ('eps', 'W1', 'b1', 'W2', 'b2')}
    del _L3_gnn_all

    def _L3_ffn_setup():
        import jax, jax.numpy as jnp
        import numpy as np
        TOP_K = 2
        LN_EPS = 1e-05
        key = jax.random.key(seed)
        ks = jax.random.split(key, 8)
        B, S, D, E, H = (16, 512, 128, 8, 512)
        x = jax.random.normal(ks[0], (B, S, D), dtype=jnp.float32)
        Wr = jax.random.normal(ks[1], (D, E), dtype=jnp.float32) * 0.1
        br = jnp.zeros((E,), dtype=jnp.float32)
        ln_g = jnp.ones((E, D), dtype=jnp.float32)
        ln_b = jnp.zeros((E, D), dtype=jnp.float32)
        W1 = jax.random.normal(ks[2], (E, D, H), dtype=jnp.float32) * (1.0 / np.sqrt(D))
        b1 = jnp.zeros((E, H), dtype=jnp.float32)
        W2 = jax.random.normal(ks[3], (E, H, D), dtype=jnp.float32) * (1.0 / np.sqrt(H))
        b2 = jnp.zeros((E, D), dtype=jnp.float32)
        return {'x': x, 'Wr': Wr, 'br': br, 'ln_g': ln_g, 'ln_b': ln_b, 'W1': W1, 'b1': b1, 'W2': W2, 'b2': b2}
    _L3_ffn_all = _L3_ffn_setup()
    _L3_ffn_in = {k: v for k, v in _L3_ffn_all.items() if k in ('Wr', 'br', 'ln_g', 'ln_b', 'W1', 'b1', 'W2', 'b2')}
    del _L3_ffn_all
    return {'x': x, 'adj': adj, 'L0_gnn_w_se': _L0_gnn_in['w_se'], 'L0_gnn_b_se': _L0_gnn_in['b_se'], 'L0_gnn_conv1_w': _L0_gnn_in['conv1_w'], 'L0_gnn_bn1_g': _L0_gnn_in['bn1_g'], 'L0_gnn_bn1_b': _L0_gnn_in['bn1_b'], 'L0_gnn_bn1_m': _L0_gnn_in['bn1_m'], 'L0_gnn_bn1_v': _L0_gnn_in['bn1_v'], 'L0_gnn_conv2_w': _L0_gnn_in['conv2_w'], 'L0_gnn_bn2_g': _L0_gnn_in['bn2_g'], 'L0_gnn_bn2_b': _L0_gnn_in['bn2_b'], 'L0_gnn_bn2_m': _L0_gnn_in['bn2_m'], 'L0_gnn_bn2_v': _L0_gnn_in['bn2_v'], 'L0_gnn_w_msg': _L0_gnn_in['w_msg'], 'L0_gnn_b_msg': _L0_gnn_in['b_msg'], 'L0_gnn_w_ih': _L0_gnn_in['w_ih'], 'L0_gnn_b_ih': _L0_gnn_in['b_ih'], 'L0_gnn_w_hh': _L0_gnn_in['w_hh'], 'L0_gnn_b_hh': _L0_gnn_in['b_hh'], 'L0_ffn_Wg': _L0_ffn_in['Wg'], 'L0_ffn_bg': _L0_ffn_in['bg'], 'L0_ffn_W1': _L0_ffn_in['W1'], 'L0_ffn_b1': _L0_ffn_in['b1'], 'L0_ffn_W2': _L0_ffn_in['W2'], 'L0_ffn_b2': _L0_ffn_in['b2'], 'L1_gnn_W_w': _L1_gnn_in['W_w'], 'L1_gnn_W_b': _L1_gnn_in['W_b'], 'L1_gnn_A': _L1_gnn_in['A'], 'L1_gnn_gate_w': _L1_gnn_in['gate_w'], 'L1_gnn_gate_b': _L1_gnn_in['gate_b'], 'L1_ffn_router_w1': _L1_ffn_in['router_w1'], 'L1_ffn_router_b1': _L1_ffn_in['router_b1'], 'L1_ffn_router_w2': _L1_ffn_in['router_w2'], 'L1_ffn_router_b2': _L1_ffn_in['router_b2'], 'L1_ffn_expert_w1': _L1_ffn_in['expert_w1'], 'L1_ffn_expert_b1': _L1_ffn_in['expert_b1'], 'L1_ffn_expert_w2': _L1_ffn_in['expert_w2'], 'L1_ffn_expert_b2': _L1_ffn_in['expert_b2'], 'L1_ffn_expert_w3': _L1_ffn_in['expert_w3'], 'L1_ffn_expert_b3': _L1_ffn_in['expert_b3'], 'L2_gnn_Wv': _L2_gnn_in['Wv'], 'L2_gnn_bv': _L2_gnn_in['bv'], 'L2_gnn_Wk': _L2_gnn_in['Wk'], 'L2_gnn_bk': _L2_gnn_in['bk'], 'L2_gnn_Wq': _L2_gnn_in['Wq'], 'L2_gnn_bq': _L2_gnn_in['bq'], 'L2_gnn_Wo': _L2_gnn_in['Wo'], 'L2_gnn_bo': _L2_gnn_in['bo'], 'L2_ffn_Wq_pk': _L2_ffn_in['Wq_pk'], 'L2_ffn_pk_keys': _L2_ffn_in['pk_keys'], 'L2_ffn_Wq': _L2_ffn_in['Wq'], 'L2_ffn_keys_table': _L2_ffn_in['keys_table'], 'L2_ffn_values_table': _L2_ffn_in['values_table'], 'L2_ffn_Wo': _L2_ffn_in['Wo'], 'L3_gnn_eps': _L3_gnn_in['eps'], 'L3_gnn_W1': _L3_gnn_in['W1'], 'L3_gnn_b1': _L3_gnn_in['b1'], 'L3_gnn_W2': _L3_gnn_in['W2'], 'L3_gnn_b2': _L3_gnn_in['b2'], 'L3_ffn_Wr': _L3_ffn_in['Wr'], 'L3_ffn_br': _L3_ffn_in['br'], 'L3_ffn_ln_g': _L3_ffn_in['ln_g'], 'L3_ffn_ln_b': _L3_ffn_in['ln_b'], 'L3_ffn_W1': _L3_ffn_in['W1'], 'L3_ffn_b1': _L3_ffn_in['b1'], 'L3_ffn_W2': _L3_ffn_in['W2'], 'L3_ffn_b2': _L3_ffn_in['b2']}

def reference(x, adj, L0_gnn_w_se, L0_gnn_b_se, L0_gnn_conv1_w, L0_gnn_bn1_g, L0_gnn_bn1_b, L0_gnn_bn1_m, L0_gnn_bn1_v, L0_gnn_conv2_w, L0_gnn_bn2_g, L0_gnn_bn2_b, L0_gnn_bn2_m, L0_gnn_bn2_v, L0_gnn_w_msg, L0_gnn_b_msg, L0_gnn_w_ih, L0_gnn_b_ih, L0_gnn_w_hh, L0_gnn_b_hh, L0_ffn_Wg, L0_ffn_bg, L0_ffn_W1, L0_ffn_b1, L0_ffn_W2, L0_ffn_b2, L1_gnn_W_w, L1_gnn_W_b, L1_gnn_A, L1_gnn_gate_w, L1_gnn_gate_b, L1_ffn_router_w1, L1_ffn_router_b1, L1_ffn_router_w2, L1_ffn_router_b2, L1_ffn_expert_w1, L1_ffn_expert_b1, L1_ffn_expert_w2, L1_ffn_expert_b2, L1_ffn_expert_w3, L1_ffn_expert_b3, L2_gnn_Wv, L2_gnn_bv, L2_gnn_Wk, L2_gnn_bk, L2_gnn_Wq, L2_gnn_bq, L2_gnn_Wo, L2_gnn_bo, L2_ffn_Wq_pk, L2_ffn_pk_keys, L2_ffn_Wq, L2_ffn_keys_table, L2_ffn_values_table, L2_ffn_Wo, L3_gnn_eps, L3_gnn_W1, L3_gnn_b1, L3_gnn_W2, L3_gnn_b2, L3_ffn_Wr, L3_ffn_br, L3_ffn_ln_g, L3_ffn_ln_b, L3_ffn_W1, L3_ffn_b1, L3_ffn_W2, L3_ffn_b2):
    import jax
    import jax.numpy as jnp

    def _L0_gnn_ref(x, mask, w_se, b_se, conv1_w, bn1_g, bn1_b, bn1_m, bn1_v, conv2_w, bn2_g, bn2_b, bn2_m, bn2_v, w_msg, b_msg, w_ih, b_ih, w_hh, b_hh):
        import jax, jax.numpy as jnp
        import numpy as np
        from jax import lax
        DIM = 128
        EPS = 1e-05

        def _bn(h, g, b, m, v):
            scale = g / jnp.sqrt(v + EPS)
            return h * scale[None, :, None] + (b - m * scale)[None, :, None]

        def _conv1d(h, w, pad):
            return lax.conv_general_dilated(h, w, window_strides=(1,), padding=[(pad, pad)], dimension_numbers=('NCH', 'OIH', 'NCH'))
        d = x.shape[-1]
        xc = jnp.transpose(x, (0, 2, 1))
        h = _bn(_conv1d(xc, conv1_w, 0), bn1_g, bn1_b, bn1_m, bn1_v)
        h = jax.nn.relu(h)
        h = _bn(_conv1d(h, conv2_w, 8), bn2_g, bn2_b, bn2_m, bn2_v)
        x_conv = jnp.transpose(jax.nn.relu(h + xc), (0, 2, 1))
        s = x @ w_se.T + b_se
        sq = jnp.sum(s * s, axis=-1)
        dist = sq[:, :, None] + sq[:, None, :] - 2.0 * jnp.einsum('bnd,bmd->bnm', s, s)
        A = jnp.exp(-dist) * mask
        msg = jax.nn.relu(x @ w_msg.T + b_msg)
        x_nmp = jnp.einsum('bnm,bmd->bnd', A, msg)
        x_in = jnp.concatenate([x_conv, x_nmp], axis=-1)
        gi = x_in @ w_ih.T + b_ih
        gh = x @ w_hh.T + b_hh
        gi_r, gi_z, gi_n = (gi[..., :d], gi[..., d:2 * d], gi[..., 2 * d:])
        gh_r, gh_z, gh_n = (gh[..., :d], gh[..., d:2 * d], gh[..., 2 * d:])
        r = jax.nn.sigmoid(gi_r + gh_r)
        z = jax.nn.sigmoid(gi_z + gh_z)
        nn_ = jnp.tanh(gi_n + r * gh_n)
        return (1.0 - z) * nn_ + z * x

    def _L0_ffn_ref(x, Wg, bg, W1, b1, W2, b2):
        import jax, jax.numpy as jnp
        import numpy as np
        B, S, D, E, H, K = (4, 2048, 128, 8, 256, 2)
        Bv, Sv, Dv = x.shape
        gate_scores = x @ Wg + bg
        _, idx = jax.lax.top_k(gate_scores, K)
        mask = jax.nn.one_hot(idx, E, dtype=x.dtype).sum(axis=-2)
        xf = x.reshape(-1, Dv)
        mf = mask.reshape(-1, E)
        h = jax.nn.gelu(jnp.einsum('td,edh->teh', xf, W1) + b1[None], approximate=False)
        y = jnp.einsum('teh,ehd->ted', h, W2) + b2[None]
        out = jnp.einsum('ted,te->td', y, mf)
        return out.reshape(Bv, Sv, Dv)

    def _L1_gnn_ref(x, adj, W_w, W_b, A, gate_w, gate_b, use_adj):
        import jax, jax.numpy as jnp
        import numpy as np
        B, N, D = (8, 1024, 128)
        NEG = -9000000000000000.0
        h = jnp.einsum('bnf,of->bno', x, W_w) + W_b
        e = jnp.einsum('bjl,bkl->bjk', jnp.einsum('bnd,de->bne', h, A), h)
        e = e + jnp.swapaxes(e, 1, 2)
        if use_adj:
            att = jnp.where(adj > 0, e, jnp.full_like(e, NEG))
            att = jax.nn.softmax(att, axis=1)
            att = att * adj
        else:
            att = e
        h_prime = jax.nn.relu(jnp.einsum('bij,bjk->bik', att, h))
        gate_in = jnp.concatenate([x, h_prime], axis=-1)
        coeff = jax.nn.sigmoid(jnp.einsum('bnf,of->bno', gate_in, gate_w) + gate_b)
        return coeff * x + (1.0 - coeff) * h_prime

    def _L1_ffn_ref(features, router_w1, router_b1, router_w2, router_b2, expert_w1, expert_b1, expert_w2, expert_b2, expert_w3, expert_b3):
        import jax, jax.numpy as jnp
        import numpy as np
        E, D, H, TOP_K = (6, 128, 128, 2)
        ROUTER_H = D // 2
        rh = jax.nn.relu(features @ router_w1 + router_b1)
        expert_logits = jax.nn.softmax(rh @ router_w2 + router_b2, axis=-1)
        top_w, top_i = jax.lax.top_k(expert_logits, TOP_K)
        routing_weights = jax.nn.softmax(top_w, axis=-1)
        h1 = jax.nn.relu(jnp.einsum('bsd,edh->bseh', features, expert_w1) + expert_b1)
        h2 = jax.nn.relu(jnp.einsum('bseh,ehf->bsef', h1, expert_w2) + expert_b2)
        expert_out = jnp.einsum('bsef,efo->bseo', h2, expert_w3) + expert_b3
        sel = jnp.take_along_axis(expert_out, top_i[:, :, :, None], axis=2)
        combined = jnp.sum(sel * routing_weights[..., None], axis=2)
        return combined

    def _L2_gnn_ref(x, mask, Wv, bv, Wk, bk, Wq, bq, Wo, bo):
        import jax, jax.numpy as jnp
        import numpy as np
        NEG = 9000000000000000.0
        v = jax.nn.relu(jnp.einsum('bnd,dh->bnh', x, Wv) + bv)
        q = jax.nn.relu(jnp.einsum('bnd,dh->bnh', x, Wq) + bq)
        k = jax.nn.relu(jnp.einsum('bnd,dh->bnh', x, Wk) + bk)
        scores = jnp.einsum('bnh,bmh->bnm', q, k)
        att = jax.nn.softmax(scores * mask - NEG * (1.0 - mask), axis=2)
        out = jnp.einsum('bnm,bmh->bnh', att, v)
        out = jax.nn.relu(jnp.einsum('bnh,ho->bno', out, Wo) + bo)
        return out

    def _L2_ffn_ref(x, Wq_pk, pk_keys, Wq, keys_table, values_table, Wo):
        import jax, jax.numpy as jnp
        import numpy as np
        DIM = 128
        HEADS = 8
        NUM_KEYS = 128
        NUM_KV = NUM_KEYS ** 2
        PK_TOPK = 16
        FINAL_TOPK = 16
        DIM_KEY = DIM // 2
        P = 2

        def _pk(x, Wq_pk, pk_keys):
            b, n, _ = x.shape
            q = (x @ Wq_pk).reshape(b, n, P, HEADS, DIM_KEY).transpose(2, 0, 1, 3, 4)
            sim = jnp.einsum('pbnhd,pkhd->pbnhk', q, pk_keys)
            scores, idx = jax.lax.top_k(sim, PK_TOPK)
            idx0 = idx[0]
            idx1 = idx[1] * NUM_KEYS
            index = (idx0[..., :, None] + idx1[..., None, :]).reshape(b, n, HEADS, PK_TOPK * PK_TOPK)
            score = (scores[0][..., :, None] + scores[1][..., None, :]).reshape(b, n, HEADS, PK_TOPK * PK_TOPK)
            final_scores, pk_idx = jax.lax.top_k(score, FINAL_TOPK)
            final_indices = jnp.take_along_axis(index, pk_idx, axis=-1)
            final_scores = jax.nn.softmax(final_scores, axis=-1)
            return (final_scores, final_indices)
        b, n, d = x.shape
        q = (x @ Wq).reshape(b, n, HEADS, DIM) * DIM ** (-0.5)
        kv_scores, indices = _pk(x, Wq_pk, pk_keys)
        offsets = jnp.arange(HEADS, dtype=indices.dtype) * NUM_KV
        ind = indices + offsets[None, None, :, None]
        k = jnp.einsum('bnhk,bnhkd->bnhd', kv_scores, keys_table[ind])
        v = jnp.einsum('bnhk,bnhkd->bnhd', kv_scores, values_table[ind])
        sim = jnp.einsum('bihd,bjhd->bhij', q, k)
        neg = -jnp.finfo(sim.dtype).max
        causal = jnp.tril(jnp.ones((n, n), dtype=bool))
        sim = jnp.where(causal, sim, neg)
        attn = jax.nn.softmax(sim, axis=-1)
        out = jnp.einsum('bhij,bjhd->bhid', attn, v)
        out = out.transpose(0, 2, 1, 3).reshape(b, n, HEADS * DIM)
        return out @ Wo

    def _L3_gnn_ref(x, adj, eps, W1, b1, W2, b2):
        import jax, jax.numpy as jnp
        import numpy as np
        D_IN = 128
        D_HID = 256
        aggregated = jnp.einsum('bnm,bmd->bnd', adj, x)
        h = (1.0 + eps) * x + aggregated
        h = jax.nn.relu(h @ W1 + b1)
        return h @ W2 + b2

    def _L3_ffn_ref(x, Wr, br, ln_g, ln_b, W1, b1, W2, b2):
        import jax, jax.numpy as jnp
        import numpy as np
        TOP_K = 2
        LN_EPS = 1e-05
        B, S, D = x.shape
        N = B * S
        xt = x.reshape(N, D)
        logits = xt @ Wr + br
        probs = jax.nn.softmax(logits, axis=-1)
        top_p, top_idx = jax.lax.top_k(probs, TOP_K)
        weights = top_p / top_p.sum(axis=-1, keepdims=True)
        mu = xt.mean(axis=-1, keepdims=True)
        var = ((xt - mu) ** 2).mean(axis=-1, keepdims=True)
        xn = (xt - mu) * jax.lax.rsqrt(var + LN_EPS)
        xe = xn[None, :, :] * ln_g[:, None, :] + ln_b[:, None, :]
        h = jax.nn.gelu(jnp.einsum('end,edh->enh', xe, W1) + b1[:, None, :], approximate=False)
        y = jnp.einsum('enh,ehd->end', h, W2) + b2[:, None, :]
        y_tok = jnp.transpose(y, (1, 0, 2))
        sel = jnp.take_along_axis(y_tok, top_idx[:, :, None], axis=1)
        out = (weights[:, :, None] * sel).sum(axis=1)
        return out.reshape(B, S, D)
    x = x + _L0_gnn_ref(_layernorm(x, axis=-1), adj, L0_gnn_w_se, L0_gnn_b_se, L0_gnn_conv1_w, L0_gnn_bn1_g, L0_gnn_bn1_b, L0_gnn_bn1_m, L0_gnn_bn1_v, L0_gnn_conv2_w, L0_gnn_bn2_g, L0_gnn_bn2_b, L0_gnn_bn2_m, L0_gnn_bn2_v, L0_gnn_w_msg, L0_gnn_b_msg, L0_gnn_w_ih, L0_gnn_b_ih, L0_gnn_w_hh, L0_gnn_b_hh)
    x = x + _L0_ffn_ref(_layernorm(x, axis=-1), L0_ffn_Wg, L0_ffn_bg, L0_ffn_W1, L0_ffn_b1, L0_ffn_W2, L0_ffn_b2)
    x = x + _L1_gnn_ref(_layernorm(x, axis=-1), adj, L1_gnn_W_w, L1_gnn_W_b, L1_gnn_A, L1_gnn_gate_w, L1_gnn_gate_b, 1)
    x = x + _L1_ffn_ref(_layernorm(x, axis=-1), L1_ffn_router_w1, L1_ffn_router_b1, L1_ffn_router_w2, L1_ffn_router_b2, L1_ffn_expert_w1, L1_ffn_expert_b1, L1_ffn_expert_w2, L1_ffn_expert_b2, L1_ffn_expert_w3, L1_ffn_expert_b3)
    x = x + _L2_gnn_ref(_layernorm(x, axis=-1), adj, L2_gnn_Wv, L2_gnn_bv, L2_gnn_Wk, L2_gnn_bk, L2_gnn_Wq, L2_gnn_bq, L2_gnn_Wo, L2_gnn_bo)
    x = x + _L2_ffn_ref(_layernorm(x, axis=-1), L2_ffn_Wq_pk, L2_ffn_pk_keys, L2_ffn_Wq, L2_ffn_keys_table, L2_ffn_values_table, L2_ffn_Wo)
    x = x + _L3_gnn_ref(_layernorm(x, axis=-1), adj, L3_gnn_eps, L3_gnn_W1, L3_gnn_b1, L3_gnn_W2, L3_gnn_b2)
    x = x + _L3_ffn_ref(_layernorm(x, axis=-1), L3_ffn_Wr, L3_ffn_br, L3_ffn_ln_g, L3_ffn_ln_b, L3_ffn_W1, L3_ffn_b1, L3_ffn_W2, L3_ffn_b2)
    return x

_drawn_inputs = setup_inputs


def setup_inputs(seed=0):
    import zlib

    import numpy as np

    out = dict(_drawn_inputs(seed))
    spreads = {'L0_gnn_b_se': (0.0, 2.0),
     'L0_gnn_bn1_g': (1.0, 0.2),
     'L0_gnn_bn1_b': (0.0, 0.288),
     'L0_gnn_bn1_m': (0.0, 0.1),
     'L0_gnn_bn1_v': (1.0, 0.6),
     'L0_gnn_bn2_g': (1.0, 0.2),
     'L0_gnn_bn2_b': (0.0, 0.374),
     'L0_gnn_bn2_m': (0.0, 0.333),
     'L0_gnn_bn2_v': (1.0, 0.6),
     'L0_gnn_b_msg': (0.0, 0.1),
     'L0_gnn_b_ih': (0.0, 0.1),
     'L0_gnn_b_hh': (0.0, 0.1),
     'L0_ffn_bg': (0.0, 0.1),
     'L0_ffn_b1': (0.0, 0.279),
     'L0_ffn_b2': (0.0, 0.1),
     'L1_ffn_router_b1': (0.0, 0.1),
     'L1_ffn_router_b2': (0.0, 0.358),
     'L1_ffn_expert_b1': (0.0, 0.749),
     'L1_ffn_expert_b2': (0.0, 0.331),
     'L1_ffn_expert_b3': (0.0, 0.1),
     'L3_ffn_br': (0.0, 0.1),
     'L3_ffn_ln_g': (1.0, 0.2),
     'L3_ffn_ln_b': (0.0, 0.447),
     'L3_ffn_b1': (0.0, 0.469),
     'L3_ffn_b2': (0.0, 0.337)}
    factors = {'L1_gnn_W_b': 2.689,
     'L2_gnn_bv': 4.382,
     'L2_gnn_bk': 8.0,
     'L2_gnn_bq': 8.0,
     'L2_ffn_Wq_pk': 8.0,
     'L2_ffn_pk_keys': 8.0,
     'L2_ffn_Wq': 64.0,
     'L2_ffn_keys_table': 64.0,
     'L2_ffn_values_table': 8.0,
     'L2_ffn_Wo': 8.0,
     'L3_gnn_b1': 5.635,
     'L3_gnn_b2': 2.823}
    for name, (base, spread) in spreads.items():
        noise = np.random.default_rng([zlib.crc32(name.encode()), seed]).standard_normal(out[name].shape)
        drawn = base * np.exp(spread * noise) if base else spread * noise
        out[name] = jnp.asarray(drawn.astype(out[name].dtype))
    for name, factor in factors.items():
        out[name] = (out[name] * factor).astype(out[name].dtype)
    return out
```

```python
from contextlib import ExitStack

import concourse.bass as bass
from concourse import mybir

F32 = mybir.dt.float32
U32 = mybir.dt.uint32
ALU = mybir.AluOpType
ACT = mybir.ActivationFunctionType
AXX = mybir.AxisListType.X

P = 128
B = 64
GRAPHS = 4
T = GRAPHS * P
GROUPS = B // GRAPHS
TAPS = 17
PAD = TAPS // 2
HEADS = 8
TOPK = 16
NUM_KEYS = 128
NUM_KV = NUM_KEYS ** 2
DK = 64
RING = 20
PER_TILE = HEADS * TOPK
NEG = 9.0e15
LOW = -3.0e38
ROW_AT = 32
EPS = 1e-5
ROW_LEN = [TOPK // (i + 1) for i in range(TOPK)]
ROW_OFF = [sum(ROW_LEN[:i]) for i in range(TOPK)]
CAND = sum(ROW_LEN)
CODE = 2 * NUM_KV

WEIGHTS = [("c1", P), ("c2", TAPS * P), ("wse", 3), ("wmsg", P), ("wih", 6 * P), ("whh", 3 * P),
           ("f0wg", 8), ("f0w1", 8 * 256), ("f0w2", 16 * P), ("g1w", P), ("g1a", P), ("f1r1", 64), ("f1r2", 6),
           ("f1w1", 6 * P), ("f1w2", 6 * P), ("f1w3", 6 * P), ("g2v", P), ("g2k", P), ("g2q", P), ("g2o", P),
           ("pkq", 1024), ("keys", 1024), ("wq", 1024), ("wo", 1024), ("g3w1", 256), ("g3w2", 256),
           ("f3wr", 8), ("f3w1", 8 * 512), ("f3w2", 32 * P)]
COLS = [("bn1", 4), ("bn2", 4), ("bih", 3), ("bhh", 3), ("bse", 1), ("f0b1", 16), ("g1b", 1), ("f1rb1", 1),
        ("f1b1", 6), ("f1b2", 6), ("g2bk", 1), ("g2bq", 1), ("g3eps", 1), ("g3b1", 2), ("lng", 8), ("lnb", 8),
        ("f3b1", 32), ("gateb", 1), ("gatew", 256)]
ROWS = [("bmsg", P), ("bg", 8), ("g1b", P), ("rb2", 6), ("bv", P), ("bo", P), ("g3b2", P), ("br", 8)]


def offsets(parts):
    at, out = 0, {}
    for name, n in parts:
        out[name] = (at, n)
        at += n
    return out, at


class Steps:

    def __init__(self, sem, names):
        self.sem = sem
        self.value = {n: k + 1 for k, n in enumerate(names)}
        self.count = len(names)

    def at(self, name, turn=0):
        return self.value[name] + turn * self.count


def build(nc, x_d, adj_d, table_d, wbig_d, cols_d, rows_d, b2_d, out_d):
    woff, wn = offsets(WEIGHTS)
    coff, cn = offsets(COLS)
    roff, rn = offsets(ROWS)
    with ExitStack() as ctx:
        def sb(name, shape, dt=F32):
            return ctx.enter_context(nc.sbuf_tensor(name, shape, dt))[:]

        sems = []

        def sem(name):
            sems.append(ctx.enter_context(nc.semaphore(name)))
            return sems[-1]

        wbig = sb("wbig", [P, wn])
        cols = sb("cols", [P, cn])
        b2 = sb("b2", [8, 3 * P])
        ident = sb("ident", [P, P])
        causal = sb("causal", [P, P])
        iota8 = sb("iota8", [P, 8])
        rank_code = sb("rank_code", [P, CAND])
        head_base = sb("head_base", [P, HEADS])
        ones = sb("ones", [P, P])
        rows_buf = sb("rows_buf", [ROW_AT + 1, 8 * P])
        expert_row = rows_buf[0:8, :]
        rows = rows_buf[ROW_AT:ROW_AT + 1, 0:rn]
        eps_col = sb("eps_col", [P, 1])
        bn_scale = sb("bn_scale", [P, 2])
        bn_shift = sb("bn_shift", [P, 2])
        gru_bias = sb("gru_bias", [P, 2])
        eps1 = sb("eps1", [P, 1])

        def W(name, a=0, n=None):
            o, size = woff[name]
            return wbig[:, o + a:o + (size if n is None else a + n)]

        def C(name, k=0, n=1):
            return cols[:, coff[name][0] + k:coff[name][0] + k + n]

        def R(name):
            o, n = roff[name]
            return rows[:, o:o + n]

        x_cur = sb("x_cur", [P, T])
        x_mid = sb("x_mid", [P, T])
        x_old = sb("x_old", [P, T])
        adj_row = sb("adj_row", [P, T])
        adjT = sb("adjT", [P, T])
        adjT_mid = sb("adjT_mid", [P, T])
        adjT_old = sb("adjT_old", [P, T])
        xn = sb("xn", [P, T])
        xnT = sb("xnT", [P, T])
        xnT_mid = sb("xnT_mid", [P, T])
        idx_new = sb("idx_new", [P, GRAPHS * PER_TILE], U32)
        idx_cur = sb("idx_cur", [P, GRAPHS * PER_TILE], U32)
        wgt_new = sb("wgt_new", [P, GRAPHS * PER_TILE])
        wgt_cur = sb("wgt_cur", [P, GRAPHS * PER_TILE])
        ring = sb("ring", [P, RING, 2 * P])
        kv = sb("kv", [P, 2, HEADS, 2 * P])
        bn_st = sb("bn_st", [P, GRAPHS, 6])
        bn_mv = sb("bn_mv", [P, GRAPHS, 2])
        std = sb("std", [P, GRAPHS])
        rstd = sb("rstd", [P, GRAPHS])
        tmps = sb("tmps", [P, 7 * T])
        tmp = [tmps[:, k * T:(k + 1) * T] for k in range(7)]
        h1pad = sb("h1pad", [P, GRAPHS, P + 2 * PAD])
        sml = [sb(f"sml{k}", [P, GRAPHS, 8]) for k in range(5)]
        idx8 = sb("idx8", [P, GRAPHS, 8], U32)
        col4 = [sb(f"col4{k}", [P, GRAPHS]) for k in range(4)]
        maskT = sb("maskT", [8, T])
        three = [tmp[k][0:3, :] for k in (5, 6, 4)]
        sq_row = three[1][0:1, :]
        simb = sb("simb", [P, 2, 8, P])
        simr = tmps[:, 2 * T:4 * T].rearrange("p (u k) -> p u k", u=8)
        score = sb("score", [P, GRAPHS, 2, HEADS, TOPK])
        place = sb("place", [P, GRAPHS, 2, HEADS, TOPK], U32)
        placef = place.bitcast(F32)
        cand, code = (tmp[k][:, 0:HEADS * CAND].rearrange("p (h c) -> p h c", h=HEADS) for k in (4, 5))
        fscore, pos, posf, fidx = (tmp[6][:, k * PER_TILE:(k + 1) * PER_TILE].rearrange("p (h k) -> p h k", h=HEADS)
                                   for k in range(4))
        pos = pos.bitcast(U32)
        wsum = sb("wsum", [P, HEADS])
        look = simb.rearrange("p a b c -> p (a b c)")[:, 0:2 * TOPK * CAND].rearrange(
            "p (h k c) -> p h k c", h=2, k=TOPK)
        candr = simr.rearrange("p a b -> p (a b)")[:, 0:HEADS * CAND].rearrange("p (h c) -> p h c", h=HEADS)
        at_q = sb("at_q", [P, T])
        at_k = sb("at_k", [P, T])
        at_s = sb("at_s", [P, T])
        at_max = sb("at_max", [P, 4])
        at_sum = sb("at_sum", [P, 4])

        ps = [ctx.enter_context(nc.psum_tensor(f"ps{k}", [P, 512], F32))[:] for k in range(8)]

        setup_in = sem("setup_in")
        setup_pool = sem("setup_pool")
        x_in = sem("x_in")
        adj_in = sem("adj_in")
        x_out = sem("x_out")
        dve_chain = sem("dve_chain")
        act_chain = sem("act_chain")
        ring_full = [sem(f"ring_full{k}") for k in range(RING)]
        sums_done = sem("sums_done")
        dve_end = sem("dve_end")

        def steps(stage, pe, act, dve):
            return tuple(Steps(sem(f"{stage}_{e}"), n) for e, n in (("pe", pe), ("act", act), ("dve", dve)))

        LN_P, LN_A, LN_D = ["xnT"], ["std", "xnT"], ["var", "xn"]
        G0 = steps("l0gnn", ["adjT", *LN_P, "h1", "s", "sq", "conv", "dist", "msg", "nmp", "gh", "r", "z", "gi", "o"],
                   ["adjT", *LN_A, "h1", "s", "sq", "xconv", "exp", "msg", "nmp", "r", "z", "n"],
                   [*LN_D, "s2", "conv", "A", "pre_n", "o", "x"])

        def moe_steps(stage, route_pe, route_act, route_dve, experts, blocks, layers):
            ks = [(e, b) for e in range(experts) for b in range(blocks)]
            pe = [("route", r) for r in route_pe] + ["wT"]
            act = [("route", r) for r in route_act] + ["wT"]
            dve = [("route", r) for r in route_dve] + ["w"]
            if layers == 2:
                order = pe_order(experts, blocks)
                act += [("act", *k) for k in ks]
            else:
                order = pe_order3(experts)
                act += act_order3(experts)
            pe += order + ["y", "xT"]
            act += ["y"]
            dve += dve_order(experts, blocks, stage == "l3ffn") + ["x"]
            return steps(stage, [*LN_P, *pe], [*LN_A, *act], [*LN_D, *dve])

        def pe_order(experts, blocks):
            out, ks = [], [(e, b) for e in range(experts) for b in range(blocks)]
            for n, (e, b) in enumerate(ks):
                out.append(("h", e, b))
                if b == 0:
                    out.append(("bc", e))
                if n >= 2:
                    out.append(("acc", *ks[n - 2]))
            return out + [("acc", *k) for k in ks[-2:]]

        def pe_order3(experts):
            out = []
            for n in range(experts + 2):
                if n < experts:
                    out += [("h1", n), ("bc", n)]
                if 1 <= n <= experts:
                    out.append(("h2", n - 1))
                if n >= 2:
                    out.append(("acc", n - 2, 0))
            return out

        def act_order3(experts):
            out = []
            for n in range(experts + 1):
                if n < experts:
                    out.append(("act1", n))
                if n >= 1:
                    out.append(("act", n - 1, 0))
            return out

        def dve_order(experts, blocks, normed):
            out = [("xe", 0), ("xe", 1)] if normed else []
            for e in range(experts):
                out += [("mul", e, b) for b in range(blocks)]
                if normed and e + 2 < experts:
                    out.append(("xe", e + 2))
            return out

        F0 = moe_steps("l0ffn", ["gate"], [], [], 8, 2, 2)
        F1 = moe_steps("l1ffn", ["rh", "gate"], ["rh", "exp", "exp2"], ["max", "gap"], 6, 1, 3)
        F3 = moe_steps("l3ffn", ["gate", "xn2T"], ["exp", "std2", "xn2T"], ["max", "var2", "xn2"], 8, 4, 2)
        G1 = steps("l1gnn", [*LN_P, "hT", "h", "hA", "e", "hp"], [*LN_A, "hT", "h", "hA", "exp", "hp", "coeff"],
                   [*LN_D, "e", "att", "logit", "x"])
        G2 = steps("l2gnn", [*LN_P, "v", "q", "k", "s", "pT", "oT", "y"], [*LN_A, "v", "q", "k", "exp", "pT", "oT"],
                   [*LN_D, "s", "p", "x"])
        blk = range(8)
        PK = steps("search", [*LN_P, *[n for b in blk for n in (("q", b), ("sim", b, 0), ("sim", b, 1))]],
                   [*LN_A, *[n for b in blk for n in (("q", b), ("sim", b))], *[("w", g) for g in range(GRAPHS)]],
                   [*LN_D, *[("top", b) for b in blk], *[n for g in range(GRAPHS) for n in (("gap", g), ("idx", g))]])
        AT = steps("attend", ["q0", "k0", "s0", "pT0", "o0", "y0", "q1", "k1", "s1", "pT1", "o1", "y1"],
                   ["q0", "k0", "e0", "pT0", "o0", "q1", "k1", "e1", "pT1", "o1"],
                   ["s0", "p0", "x0", "s1", "p1", "x1"])
        G3 = steps("l3gnn", [*LN_P, "agg", "h0", "h1", "y"], [*LN_A, "h0", "h1"], [*LN_D, "h", "x"])

        def v4(ap):
            return ap.rearrange("p (g d) -> p g d", g=GRAPHS)

        def tok(ap, g):
            return ap[:, g * P:(g + 1) * P]

        class Chain:

            def __init__(self, eng, s):
                self.eng, self.sem, self.n = eng, s, 0

            def link(self, ins):
                ins.then_inc(self.sem, 1)
                self.n += 1
                self.eng.wait_ge(self.sem, self.n)

        def ln_dve(dve, ch, S, x, out, names=("var", "xn", "std")):
            Pe, A, D = S
            for g in range(GRAPHS):
                ins = nc.vector.bn_stats(bn_st[:, g, :], tok(x, g))
            ch.link(ins)
            for g in range(GRAPHS):
                ins = nc.vector.bn_aggr(bn_mv[:, g, :], bn_st[:, g, :])
            ins.then_inc(D.sem, 1)
            dve.wait_ge(A.sem, A.at(names[2]))
            ch.link(nc.vector.reciprocal(rstd, std))
            for g in range(GRAPHS):
                ins = nc.vector.tensor_scalar(tok(out, g), tok(x, g), bn_mv[:, g, 0:1], rstd[:, g:g + 1],
                                              ALU.subtract, ALU.mult)
            ins.then_inc(D.sem, 1)
            dve.wait_ge(D.sem, D.at(names[1]))

        def ln_act(act, S, var="var"):
            Pe, A, D = S
            act.wait_ge(D.sem, D.at(var))
            nc.scalar.activation(std, bn_mv[:, :, 1], ACT.Sqrt, bias=eps_col[:, 0:1]).then_inc(A.sem, 1)

        def xnT_act(act, S):
            Pe, A, D = S
            act.wait_ge(Pe.sem, Pe.at("xnT"))
            nc.scalar.copy(xnT, ps[0]).then_inc(A.sem, 1)

        def ln_pe(pe, S):
            Pe, A, D = S
            pe.wait_ge(D.sem, D.at("xn"))
            for g in range(GRAPHS):
                ins = nc.tensor.transpose(tok(ps[0], g), tok(xn, g), ident)
            ins.then_inc(Pe.sem, 1)

        def mm(out, lhsT, rhs, start, stop):
            return nc.tensor.matmul(out, lhsT, rhs, start=start, stop=stop, skip_group_check=True)

        def bias_row(out, row, n):
            return mm(out, ones[ROW_AT:ROW_AT + 1, :], row.unsqueeze(1).to_broadcast([1, GRAPHS, n]), True, False)

        def chunk(ap, k, n=P):
            return ap[:, k * n:(k + 1) * n]

        def l0gnn_pe(pe):
            Pe, A, D = G0
            pe.wait_ge(adj_in, 16)
            for g in range(GRAPHS):
                ins = nc.tensor.transpose(tok(ps[1], g), tok(adj_row, g), ident)
            ins.then_inc(Pe.sem, 1)
            ln_pe(pe, G0)
            pe.wait_ge(A.sem, A.at("xnT"))
            mm(ps[1], W("c1"), xnT, True, True).then_inc(Pe.sem, 1)
            mm(ps[3][0:3, :], W("wse"), xnT, True, True).then_inc(Pe.sem, 1)
            pe.wait_ge(D.sem, D.at("s2"))
            mm(ps[4][0:1, :], ones[0:3, 0:1], three[2], True, True).then_inc(Pe.sem, 1)
            pe.wait_ge(A.sem, A.at("h1"))
            for k in range(TAPS):
                ins = mm(ps[2], chunk(W("c2"), k), h1pad[:, :, k:k + P], k == 0, k == TAPS - 1)
            ins.then_inc(Pe.sem, 1)
            pe.wait_ge(A.sem, A.at("sq"))
            for g in range(GRAPHS):
                mm(tok(ps[0], g), tok(sq_row, g), ones[0:1, :], True, False)
                mm(tok(ps[0], g), ones[0:1, :], tok(sq_row, g), False, False)
                ins = mm(tok(ps[0], g), tok(maskT[0:3, :], g), tok(three[0], g), False, True)
            ins.then_inc(Pe.sem, 1)
            bias_row(ps[1], R("bmsg"), P)
            for g in range(GRAPHS):
                ins = mm(tok(ps[1], g), tok(xnT, g), W("wmsg"), False, g == GRAPHS - 1)
            ins.then_inc(Pe.sem, 1)
            pe.wait_ge(D.sem, D.at("A"))
            pe.wait_ge(A.sem, A.at("msg"))
            for g in range(GRAPHS):
                ins = mm(tok(ps[3], g), tok(tmp[2], g), tok(tmp[1], g), True, True)
            ins.then_inc(Pe.sem, 1)
            mm(ps[4], chunk(W("whh"), 2), xnT, True, True).then_inc(Pe.sem, 1)
            pe.wait_ge(A.sem, A.at("nmp"))
            for k, bank in enumerate((0, 1, 2)):
                mm(ps[bank], chunk(W("wih"), k), tmp[0], True, False)
                ins = mm(ps[bank], chunk(W("wih"), 3 + k), tmp[3], False, k == 2)
                if k < 2:
                    ins = mm(ps[bank], chunk(W("whh"), k), xnT, False, True)
                ins.then_inc(Pe.sem, 1)
            pe.wait_ge(D.sem, D.at("o"))
            for g in range(GRAPHS):
                ins = nc.tensor.transpose(tok(ps[3], g), tok(tmp[4], g), ident)
            ins.then_inc(Pe.sem, 1)

        def l0gnn_act(act, ch):
            Pe, A, D = G0
            act.wait_ge(Pe.sem, Pe.at("adjT"))
            nc.scalar.copy(adjT, ps[1]).then_inc(A.sem, 1)
            ln_act(act, G0)
            xnT_act(act, G0)
            act.wait_ge(Pe.sem, Pe.at("h1"))
            nc.scalar.activation(h1pad[:, :, PAD:PAD + P], v4(ps[1]), ACT.Relu, bias=bn_shift[:, 0:1],
                                 scale=bn_scale[:, 0:1]).then_inc(A.sem, 1)
            act.wait_ge(Pe.sem, Pe.at("s"))
            nc.scalar.activation(three[0], ps[3][0:3, :], ACT.Identity, bias=C("bse")[0:3, :]).then_inc(A.sem, 1)
            act.wait_ge(Pe.sem, Pe.at("sq"))
            nc.scalar.copy(sq_row, ps[4][0:1, :]).then_inc(A.sem, 1)
            act.wait_ge(D.sem, D.at("conv"))
            nc.scalar.activation(tmp[0], tmp[0], ACT.Relu, bias=bn_shift[:, 1:2]).then_inc(A.sem, 1)
            act.wait_ge(Pe.sem, Pe.at("dist"))
            nc.scalar.activation(tmp[1], ps[0], ACT.Exp, scale=-1.0).then_inc(A.sem, 1)
            act.wait_ge(Pe.sem, Pe.at("msg"))
            nc.scalar.activation(tmp[2], ps[1], ACT.Relu).then_inc(A.sem, 1)
            act.wait_ge(Pe.sem, Pe.at("nmp"))
            nc.scalar.copy(tmp[3], ps[3]).then_inc(A.sem, 1)
            for k, name in enumerate("rz"):
                act.wait_ge(Pe.sem, Pe.at(name))
                nc.scalar.activation(tmp[4 + k], ps[k], ACT.Sigmoid, bias=gru_bias[:, k:k + 1])\
                    .then_inc(A.sem, 1)
            act.wait_ge(D.sem, D.at("pre_n"))
            nc.scalar.activation(tmp[6], tmp[6], ACT.Tanh, bias=C("bih", 2)).then_inc(A.sem, 1)

        def l0gnn_dve(dve, ch, fill):
            Pe, A, D = G0
            dve.wait_ge(x_in, 16)
            ln_dve(dve, ch, G0, x_cur, xn)
            fill(6)
            dve.wait_ge(A.sem, A.at("s"))
            nc.vector.tensor_scalar(maskT[0:3, :], three[0], -2.0, None, ALU.mult)
            nc.vector.tensor_tensor(three[2], three[0], three[0], ALU.mult).then_inc(D.sem, 1)
            fill(16)
            dve.wait_ge(Pe.sem, Pe.at("conv"))
            nc.vector.scalar_tensor_tensor(tmp[0], ps[2], bn_scale[:, 1:2], xnT, ALU.mult, ALU.add)\
                .then_inc(D.sem, 1)
            dve.wait_ge(A.sem, A.at("exp"))
            nc.vector.tensor_tensor(tmp[1], tmp[1], adjT, ALU.mult).then_inc(D.sem, 1)
            fill(6)
            dve.wait_ge(A.sem, A.at("r"))
            dve.wait_ge(Pe.sem, Pe.at("gh"))
            ch.link(nc.vector.scalar_tensor_tensor(tmp[6], ps[4], C("bhh", 2), tmp[4], ALU.add, ALU.mult))
            dve.wait_ge(Pe.sem, Pe.at("gi"))
            nc.vector.tensor_tensor(tmp[6], ps[2], tmp[6], ALU.add).then_inc(D.sem, 1)
            dve.wait_ge(A.sem, A.at("n"))
            ch.link(nc.vector.tensor_tensor(tmp[4], xnT, tmp[6], ALU.subtract))
            ch.link(nc.vector.tensor_tensor(tmp[4], tmp[5], tmp[4], ALU.mult))
            nc.vector.tensor_tensor(tmp[4], tmp[4], tmp[6], ALU.add).then_inc(D.sem, 1)
            fill(2)
            dve.wait_ge(Pe.sem, Pe.at("o"))
            nc.vector.tensor_tensor(x_cur, x_cur, ps[3], ALU.add).then_inc(D.sem, 1)
            dve.wait_ge(D.sem, D.at("x"))

        def gate_pe(w, n, row):
            mm(ps[1][:, 0:GRAPHS * n], ones[ROW_AT:ROW_AT + 1, :], row.unsqueeze(1).to_broadcast([1, GRAPHS, n]), True, False)
            for g in range(GRAPHS):
                ins = mm(ps[1][:, g * n:(g + 1) * n], w(g)[0], w(g)[1], False, g == GRAPHS - 1)
            return ins

        def wT_pe(pe, S):
            Pe, A, D = S
            pe.wait_ge(D.sem, D.at("w"))
            for g in range(GRAPHS):
                ins = nc.tensor.transpose(tok(ps[2][0:8, :], g), sml[4][:, g, :], ident)
            ins.then_inc(Pe.sem, 1)
            pe.wait_ge(A.sem, A.at("wT"))

        def wT_act(act, S):
            Pe, A, D = S
            act.wait_ge(Pe.sem, Pe.at("wT"))
            nc.scalar.copy(maskT, ps[2][0:8, :]).then_inc(A.sem, 1)

        def acc_end_pe(pe, S, which, experts):
            Pe, A, D = S
            mm(ps[4], b2[0:experts, which * P:(which + 1) * P], maskT[0:experts, :], False, True)\
                .then_inc(Pe.sem, 1)
            pe.wait_ge(A.sem, A.at("y"))
            for g in range(GRAPHS):
                ins = nc.tensor.transpose(tok(ps[0], g), tok(tmp[6], g), ident)
            ins.then_inc(Pe.sem, 1)

        def experts_pe(pe, S, experts, blocks, w1, w2, which, rhs):
            Pe, A, D = S
            ks = [(e, b) for e in range(experts) for b in range(blocks)]
            for item in pe_order(experts, blocks):
                if item[0] == "h":
                    _, e, b = item
                    n = ks.index((e, b))
                    if n >= 2:
                        pe.wait_ge(A.sem, A.at(("act", *ks[n - 2])))
                    if rhs is not None and b == 0:
                        pe.wait_ge(D.sem, D.at(("xe", e)))
                    mm(ps[n % 2], chunk(w1, n), xnT if rhs is None else rhs[e % 2], True, True)\
                        .then_inc(Pe.sem, 1)
                elif item[0] == "bc":
                    e = item[1]
                    if e >= 2:
                        pe.wait_ge(D.sem, D.at(("mul", e - 2, blocks - 1)))
                    mm(ps[2 + e % 2], chunk(expert_row[0:experts, :], e), maskT[0:experts, :], True, True)\
                        .then_inc(Pe.sem, 1)
                else:
                    _, e, b = item
                    n = ks.index((e, b))
                    pe.wait_ge(D.sem, D.at(("mul", e, b)))
                    mm(ps[4], chunk(w2, n), tmp[2 + n % 2], n == 0, False).then_inc(Pe.sem, 1)
            acc_end_pe(pe, S, which, experts)

        def experts_act(act, S, experts, blocks, bias):
            Pe, A, D = S
            ks = [(e, b) for e in range(experts) for b in range(blocks)]
            for n, (e, b) in enumerate(ks):
                act.wait_ge(Pe.sem, Pe.at(("h", e, b)))
                if n >= 2:
                    act.wait_ge(D.sem, D.at(("mul", *ks[n - 2])))
                nc.scalar.activation(tmp[n % 2], ps[n % 2], ACT.Gelu, bias=C(bias, n)).then_inc(A.sem, 1)
            y_act(act, S)

        def y_act(act, S):
            Pe, A, D = S
            act.wait_ge(Pe.sem, Pe.at("y"))
            nc.scalar.copy(tmp[6], ps[4]).then_inc(A.sem, 1)

        def experts_dve(dve, ch, S, experts, blocks, fill, per, x, xe=None):
            Pe, A, D = S
            ks = [(e, b) for e in range(experts) for b in range(blocks)]
            for item in dve_order(experts, blocks, xe is not None):
                if item[0] == "xe":
                    e = item[1]
                    if e >= 2:
                        dve.wait_ge(Pe.sem, Pe.at(("h", e - 2, blocks - 1)))
                    nc.vector.tensor_scalar(xe[e % 2], xnT, C("lng", e), C("lnb", e), ALU.mult, ALU.add)\
                        .then_inc(D.sem, 1)
                    continue
                _, e, b = item
                n = ks.index((e, b))
                dve.wait_ge(A.sem, A.at(("act", e, b)))
                dve.wait_ge(Pe.sem, Pe.at(("bc", e)))
                if n >= 2:
                    dve.wait_ge(Pe.sem, Pe.at(("acc", *ks[n - 2])))
                nc.vector.tensor_tensor(tmp[2 + n % 2], tmp[n % 2], ps[2 + e % 2], ALU.mult)\
                    .then_inc(D.sem, 1)
                fill(per)
            dve.wait_ge(Pe.sem, Pe.at("xT"))
            nc.vector.tensor_tensor(x, x, ps[0], ALU.add).then_inc(D.sem, 1)
            dve.wait_ge(D.sem, D.at("x"))

        def top2_dve(dve, ch, scores):
            for g in range(GRAPHS):
                ins = nc.vector.max(sml[1][:, g, :], scores[:, g, :])
            ch.link(ins)
            for g in range(GRAPHS):
                ins = nc.vector.max_index(idx8[:, g, :], sml[1][:, g, :], scores[:, g, :])
            ch.link(ins)
            ch.link(nc.vector.tensor_copy(sml[4], idx8))
            it = iota8.unsqueeze(1).to_broadcast([P, GRAPHS, 8])
            nc.vector.tensor_tensor(sml[2], sml[4][:, :, 0:1].to_broadcast([P, GRAPHS, 8]), it, ALU.is_equal)
            ch.link(nc.vector.tensor_tensor(sml[3], sml[4][:, :, 1:2].to_broadcast([P, GRAPHS, 8]), it, ALU.is_equal))

        def b8(ap):
            return ap.unsqueeze(2).to_broadcast([P, GRAPHS, 8])

        def l0ffn_pe(pe):
            Pe, A, D = F0
            ln_pe(pe, F0)
            pe.wait_ge(A.sem, A.at("xnT"))
            gate_pe(lambda g: (tok(xnT, g), W("f0wg")), 8, R("bg")).then_inc(Pe.sem, 1)
            wT_pe(pe, F0)
            experts_pe(pe, F0, 8, 2, W("f0w1"), W("f0w2"), 0, None)

        def l0ffn_act(act, ch):
            ln_act(act, F0)
            xnT_act(act, F0)
            wT_act(act, F0)
            experts_act(act, F0, 8, 2, "f0b1")

        def l0ffn_dve(dve, ch, fill):
            Pe, A, D = F0
            ln_dve(dve, ch, F0, x_cur, xn)
            fill(4)
            dve.wait_ge(Pe.sem, Pe.at(("route", "gate")))
            ch.link(nc.vector.tensor_copy(sml[0], ps[1][:, 0:32].rearrange("p (g e) -> p g e", g=GRAPHS)))
            top2_dve(dve, ch, sml[0])
            nc.vector.tensor_tensor(sml[4], sml[2], sml[3], ALU.add).then_inc(D.sem, 1)
            experts_dve(dve, ch, F0, 8, 2, fill, 2, x_cur)

        def l1ffn_pe(pe):
            Pe, A, D = F1
            ln_pe(pe, F1)
            pe.wait_ge(A.sem, A.at("xnT"))
            mm(ps[3][0:64, :], W("f1r1"), xnT, True, True).then_inc(Pe.sem, 1)
            pe.wait_ge(A.sem, A.at(("route", "rh")))
            gate_pe(lambda g: (tok(tmp[5][0:64, :], g), W("f1r2")[0:64, :]), 6, R("rb2")).then_inc(Pe.sem, 1)
            wT_pe(pe, F1)
            for item in pe_order3(6):
                e = item[1]
                if item[0] == "h1":
                    if e >= 1:
                        pe.wait_ge(A.sem, A.at(("act1", e - 1)))
                    mm(ps[0], chunk(W("f1w1"), e), xnT, True, True).then_inc(Pe.sem, 1)
                elif item[0] == "bc":
                    if e >= 2:
                        pe.wait_ge(D.sem, D.at(("mul", e - 2, 0)))
                    mm(ps[2 + e % 2], chunk(expert_row[0:6, :], e), maskT[0:6, :], True, True)\
                        .then_inc(Pe.sem, 1)
                elif item[0] == "h2":
                    pe.wait_ge(A.sem, A.at(("act1", e)))
                    if e >= 1:
                        pe.wait_ge(A.sem, A.at(("act", e - 1, 0)))
                    mm(ps[1], chunk(W("f1w2"), e), tmp[4 + e % 2], True, True).then_inc(Pe.sem, 1)
                else:
                    pe.wait_ge(D.sem, D.at(("mul", e, 0)))
                    mm(ps[4], chunk(W("f1w3"), e), tmp[2 + e % 2], e == 0, False).then_inc(Pe.sem, 1)
            acc_end_pe(pe, F1, 1, 6)

        def l1ffn_act(act, ch):
            Pe, A, D = F1
            ln_act(act, F1)
            xnT_act(act, F1)
            act.wait_ge(Pe.sem, Pe.at(("route", "rh")))
            nc.scalar.activation(tmp[5][0:64, :], ps[3][0:64, :], ACT.Relu, bias=C("f1rb1")[0:64, :])\
                .then_inc(A.sem, 1)
            act.wait_ge(D.sem, D.at(("route", "max")))
            nc.scalar.activation(sml[1][:, :, 0:6], sml[1][:, :, 0:6], ACT.Exp).then_inc(A.sem, 1)
            act.wait_ge(D.sem, D.at(("route", "gap")))
            nc.scalar.activation(col4[1], col4[0], ACT.Exp).then_inc(A.sem, 1)
            wT_act(act, F1)
            for item in act_order3(6):
                e = item[1]
                if item[0] == "act1":
                    act.wait_ge(Pe.sem, Pe.at(("h1", e)))
                    if e >= 2:
                        act.wait_ge(Pe.sem, Pe.at(("h2", e - 2)))
                    nc.scalar.activation(tmp[4 + e % 2], ps[0], ACT.Relu, bias=C("f1b1", e)).then_inc(A.sem, 1)
                else:
                    act.wait_ge(Pe.sem, Pe.at(("h2", e)))
                    if e >= 2:
                        act.wait_ge(D.sem, D.at(("mul", e - 2, 0)))
                    nc.scalar.activation(tmp[e % 2], ps[1], ACT.Relu, bias=C("f1b2", e)).then_inc(A.sem, 1)
            y_act(act, F1)

        def softmax6_dve(dve, ch, S, n, bank):
            Pe, A, D = S
            lg = bank[:, 0:GRAPHS * n].rearrange("p (g e) -> p g e", g=GRAPHS)
            nc.vector.memset(sml[0], -1.0)
            ch.link(nc.vector.tensor_reduce(col4[0], lg, AXX, ALU.max))
            nc.vector.tensor_tensor(sml[1][:, :, 0:n], lg, col4[0].unsqueeze(2).to_broadcast([P, GRAPHS, n]),
                                    ALU.subtract).then_inc(D.sem, 1)
            dve.wait_ge(A.sem, A.at(("route", "exp")))
            ch.link(nc.vector.tensor_reduce(col4[1], sml[1][:, :, 0:n], AXX, ALU.add))
            ch.link(nc.vector.reciprocal(col4[2], col4[1]))
            ch.link(nc.vector.tensor_tensor(sml[0][:, :, 0:n], sml[1][:, :, 0:n],
                                            col4[2].unsqueeze(2).to_broadcast([P, GRAPHS, n]), ALU.mult))

        def l1ffn_dve(dve, ch, fill):
            Pe, A, D = F1
            ln_dve(dve, ch, F1, x_cur, xn)
            fill(6)
            dve.wait_ge(Pe.sem, Pe.at(("route", "gate")))
            softmax6_dve(dve, ch, F1, 6, ps[1])
            top2_dve(dve, ch, sml[0])
            nc.vector.tensor_tensor(col4[0], sml[1][:, :, 1], sml[1][:, :, 0], ALU.subtract).then_inc(D.sem, 1)
            dve.wait_ge(A.sem, A.at(("route", "exp2")))
            ch.link(nc.vector.tensor_scalar(col4[2], col4[1], 1.0, None, ALU.add))
            ch.link(nc.vector.reciprocal(col4[3], col4[2]))
            ch.link(nc.vector.tensor_tensor(col4[1], col4[1], col4[3], ALU.mult))
            nc.vector.tensor_tensor(sml[2], sml[2], b8(col4[3]), ALU.mult)
            ch.link(nc.vector.tensor_tensor(sml[3], sml[3], b8(col4[1]), ALU.mult))
            nc.vector.tensor_tensor(sml[4], sml[2], sml[3], ALU.add).then_inc(D.sem, 1)
            experts_dve(dve, ch, F1, 6, 1, fill, 3, x_cur)

        def l3ffn_pe(pe):
            Pe, A, D = F3
            ln_pe(pe, F3)
            pe.wait_ge(A.sem, A.at("xnT"))
            gate_pe(lambda g: (tok(xnT, g), W("f3wr")), 8, R("br")).then_inc(Pe.sem, 1)
            pe.wait_ge(D.sem, D.at(("route", "xn2")))
            for g in range(GRAPHS):
                ins = nc.tensor.transpose(tok(ps[3], g), tok(tmp[5], g), ident)
            ins.then_inc(Pe.sem, 1)
            wT_pe(pe, F3)
            experts_pe(pe, F3, 8, 4, W("f3w1"), W("f3w2"), 2, [tmp[4], tmp[5]])

        def l3ffn_act(act, ch):
            Pe, A, D = F3
            ln_act(act, F3)
            xnT_act(act, F3)
            act.wait_ge(D.sem, D.at(("route", "max")))
            nc.scalar.activation(sml[1], sml[1], ACT.Exp).then_inc(A.sem, 1)
            act.wait_ge(D.sem, D.at(("route", "var2")))
            nc.scalar.activation(std, bn_mv[:, :, 1], ACT.Sqrt, bias=eps_col[:, 0:1]).then_inc(A.sem, 1)
            act.wait_ge(Pe.sem, Pe.at(("route", "xn2T")))
            nc.scalar.copy(xnT, ps[3]).then_inc(A.sem, 1)
            wT_act(act, F3)
            experts_act(act, F3, 8, 4, "f3b1")

        def l3ffn_dve(dve, ch, fill):
            Pe, A, D = F3
            ln_dve(dve, ch, F3, x_old, xn)
            fill(4)
            dve.wait_ge(Pe.sem, Pe.at(("route", "gate")))
            softmax6_dve(dve, ch, F3, 8, ps[1])
            top2_dve(dve, ch, sml[0])
            for g in range(GRAPHS):
                ins = nc.vector.bn_stats(bn_st[:, g, :], tok(xn, g))
            ch.link(ins)
            for g in range(GRAPHS):
                ins = nc.vector.bn_aggr(bn_mv[:, g, :], bn_st[:, g, :])
            ins.then_inc(D.sem, 1)
            ch.link(nc.vector.tensor_tensor(col4[0], sml[1][:, :, 0], sml[1][:, :, 1], ALU.add))
            ch.link(nc.vector.reciprocal(col4[1], col4[0]))
            ch.link(nc.vector.tensor_tensor(col4[2], sml[1][:, :, 0], col4[1], ALU.mult))
            ch.link(nc.vector.tensor_tensor(col4[3], sml[1][:, :, 1], col4[1], ALU.mult))
            dve.wait_ge(A.sem, A.at(("route", "std2")))
            ch.link(nc.vector.reciprocal(rstd, std))
            for g in range(GRAPHS):
                ins = nc.vector.tensor_scalar(tok(tmp[5], g), tok(xn, g), bn_mv[:, g, 0:1], rstd[:, g:g + 1],
                                              ALU.subtract, ALU.mult)
            ins.then_inc(D.sem, 1)
            nc.vector.tensor_tensor(sml[2], sml[2], b8(col4[2]), ALU.mult)
            ch.link(nc.vector.tensor_tensor(sml[3], sml[3], b8(col4[3]), ALU.mult))
            nc.vector.tensor_tensor(sml[4], sml[2], sml[3], ALU.add).then_inc(D.sem, 1)
            dve.wait_ge(A.sem, A.at(("route", "xn2T")))
            experts_dve(dve, ch, F3, 8, 4, fill, 2, x_old, xe=[tmp[4], tmp[5]])

        def l1gnn_pe(pe):
            Pe, A, D = G1
            ln_pe(pe, G1)
            pe.wait_ge(A.sem, A.at("xnT"))
            mm(ps[1], W("g1w"), xnT, True, True).then_inc(Pe.sem, 1)
            bias_row(ps[2], R("g1b"), P)
            for g in range(GRAPHS):
                ins = mm(tok(ps[2], g), tok(xnT, g), W("g1w"), False, g == GRAPHS - 1)
            ins.then_inc(Pe.sem, 1)
            pe.wait_ge(A.sem, A.at("hT"))
            mm(ps[3], W("g1a"), tmp[0], True, True).then_inc(Pe.sem, 1)
            pe.wait_ge(A.sem, A.at("hA"))
            for g in range(GRAPHS):
                mm(tok(ps[4], g), tok(tmp[2], g), tok(tmp[0], g), True, False)
                ins = mm(tok(ps[4], g), tok(tmp[0], g), tok(tmp[2], g), False, True)
            ins.then_inc(Pe.sem, 1)
            pe.wait_ge(D.sem, D.at("att"))
            for g in range(GRAPHS):
                ins = mm(tok(ps[1], g), tok(tmp[3], g), tok(tmp[1], g), True, True)
            ins.then_inc(Pe.sem, 1)

        def l1gnn_act(act, ch):
            Pe, A, D = G1
            ln_act(act, G1)
            xnT_act(act, G1)
            act.wait_ge(Pe.sem, Pe.at("hT"))
            nc.scalar.activation(tmp[0], ps[1], ACT.Identity, bias=C("g1b")).then_inc(A.sem, 1)
            act.wait_ge(Pe.sem, Pe.at("h"))
            nc.scalar.copy(tmp[1], ps[2]).then_inc(A.sem, 1)
            act.wait_ge(Pe.sem, Pe.at("hA"))
            nc.scalar.copy(tmp[2], ps[3]).then_inc(A.sem, 1)
            act.wait_ge(D.sem, D.at("e"))
            for g in range(GRAPHS):
                ins = nc.scalar.activation(tok(tmp[3], g), tok(tmp[4], g), ACT.Exp, bias=col4[0][:, g:g + 1],
                                           accum_out=col4[1][:, g:g + 1])
            ins.then_inc(A.sem, 1)
            act.wait_ge(Pe.sem, Pe.at("hp"))
            nc.scalar.activation(tmp[5], ps[1], ACT.Relu).then_inc(A.sem, 1)
            act.wait_ge(D.sem, D.at("logit"))
            nc.scalar.activation(col4[3], col4[2], ACT.Sigmoid, bias=C("gateb")).then_inc(A.sem, 1)

        def l1gnn_dve(dve, ch, fill):
            Pe, A, D = G1
            ln_dve(dve, ch, G1, x_cur, xn)
            fill(4)
            ch.link(nc.vector.tensor_scalar(tmp[6], adjT, 0.0, None, ALU.is_gt))
            ch.link(nc.vector.tensor_scalar(tmp[5], tmp[6], -1.0, NEG, ALU.add, ALU.mult))
            fill(4)
            dve.wait_ge(Pe.sem, Pe.at("e"))
            ch.link(nc.vector.tensor_tensor(tmp[4], ps[4], tmp[6], ALU.mult))
            ch.link(nc.vector.tensor_tensor(tmp[4], tmp[4], tmp[5], ALU.add))
            nc.vector.tensor_reduce(col4[0], v4(tmp[4]), AXX, ALU.max, negate=True).then_inc(D.sem, 1)
            fill(4)
            dve.wait_ge(A.sem, A.at("exp"))
            ch.link(nc.vector.reciprocal(col4[2], col4[1]))
            for g in range(GRAPHS):
                ins = nc.vector.scalar_tensor_tensor(tok(tmp[3], g), tok(tmp[3], g), col4[2][:, g:g + 1],
                                                     tok(adjT, g), ALU.mult, ALU.mult)
            ins.then_inc(D.sem, 1)
            gw = C("gatew", 0, 256)
            ch.link(nc.vector.tensor_tensor(v4(tmp[6]), v4(xn), gw[:, 0:P].unsqueeze(1).to_broadcast([P, GRAPHS, P]),
                                            ALU.mult))
            dve.wait_ge(A.sem, A.at("hp"))
            ch.link(nc.vector.tensor_tensor(v4(tmp[4]), v4(tmp[5]),
                                            gw[:, P:2 * P].unsqueeze(1).to_broadcast([P, GRAPHS, P]), ALU.mult))
            ch.link(nc.vector.tensor_tensor(tmp[4], tmp[4], tmp[6], ALU.add))
            nc.vector.tensor_reduce(col4[2], v4(tmp[4]), AXX, ALU.add).then_inc(D.sem, 1)
            ch.link(nc.vector.tensor_tensor(tmp[6], xn, tmp[5], ALU.subtract))
            fill(2)
            dve.wait_ge(A.sem, A.at("coeff"))
            for g in range(GRAPHS):
                ins = nc.vector.scalar_tensor_tensor(tok(tmp[6], g), tok(tmp[6], g), col4[3][:, g:g + 1],
                                                     tok(tmp[5], g), ALU.mult, ALU.add)
            ch.link(ins)
            nc.vector.tensor_tensor(x_cur, x_cur, tmp[6], ALU.add).then_inc(D.sem, 1)
            dve.wait_ge(D.sem, D.at("x"))

        def l2gnn_pe(pe):
            Pe, A, D = G2
            ln_pe(pe, G2)
            pe.wait_ge(A.sem, A.at("xnT"))
            bias_row(ps[1], R("bv"), P)
            for g in range(GRAPHS):
                ins = mm(tok(ps[1], g), tok(xnT, g), W("g2v"), False, g == GRAPHS - 1)
            ins.then_inc(Pe.sem, 1)
            mm(ps[2], W("g2q"), xnT, True, True).then_inc(Pe.sem, 1)
            mm(ps[3], W("g2k"), xnT, True, True).then_inc(Pe.sem, 1)
            pe.wait_ge(A.sem, A.at("k"))
            for g in range(GRAPHS):
                ins = mm(tok(ps[4], g), tok(tmp[1], g), tok(tmp[2], g), True, True)
            ins.then_inc(Pe.sem, 1)
            pe.wait_ge(D.sem, D.at("p"))
            for g in range(GRAPHS):
                ins = nc.tensor.transpose(tok(ps[1], g), tok(tmp[3], g), ident)
            ins.then_inc(Pe.sem, 1)
            pe.wait_ge(A.sem, A.at("pT"))
            for g in range(GRAPHS):
                ins = mm(tok(ps[2], g), tok(tmp[0], g), tok(tmp[4], g), True, True)
            ins.then_inc(Pe.sem, 1)
            bias_row(ps[3], R("bo"), P)
            pe.wait_ge(A.sem, A.at("oT"))
            for g in range(GRAPHS):
                ins = mm(tok(ps[3], g), tok(tmp[1], g), W("g2o"), False, g == GRAPHS - 1)
            ins.then_inc(Pe.sem, 1)

        def l2gnn_act(act, ch):
            Pe, A, D = G2
            ln_act(act, G2)
            xnT_act(act, G2)
            act.wait_ge(Pe.sem, Pe.at("v"))
            nc.scalar.activation(tmp[0], ps[1], ACT.Relu).then_inc(A.sem, 1)
            act.wait_ge(Pe.sem, Pe.at("q"))
            nc.scalar.activation(tmp[1], ps[2], ACT.Relu, bias=C("g2bq")).then_inc(A.sem, 1)
            act.wait_ge(Pe.sem, Pe.at("k"))
            nc.scalar.activation(tmp[2], ps[3], ACT.Relu, bias=C("g2bk")).then_inc(A.sem, 1)
            act.wait_ge(D.sem, D.at("s"))
            for g in range(GRAPHS):
                ins = nc.scalar.activation(tok(tmp[3], g), tok(tmp[5], g), ACT.Exp, bias=col4[0][:, g:g + 1],
                                           accum_out=col4[1][:, g:g + 1])
            ins.then_inc(A.sem, 1)
            act.wait_ge(Pe.sem, Pe.at("pT"))
            nc.scalar.copy(tmp[4], ps[1]).then_inc(A.sem, 1)
            act.wait_ge(Pe.sem, Pe.at("oT"))
            nc.scalar.copy(tmp[1], ps[2]).then_inc(A.sem, 1)

        def l2gnn_dve(dve, ch, fill):
            Pe, A, D = G2
            ln_dve(dve, ch, G2, x_cur, xn)
            fill(4)
            ch.link(nc.vector.tensor_scalar(tmp[6], adj_row, -1.0, NEG, ALU.add, ALU.mult))
            fill(4)
            dve.wait_ge(Pe.sem, Pe.at("s"))
            ch.link(nc.vector.tensor_tensor(tmp[5], ps[4], adj_row, ALU.mult))
            ch.link(nc.vector.tensor_tensor(tmp[5], tmp[5], tmp[6], ALU.add))
            nc.vector.tensor_reduce(col4[0], v4(tmp[5]), AXX, ALU.max, negate=True).then_inc(D.sem, 1)
            fill(3)
            dve.wait_ge(A.sem, A.at("exp"))
            ch.link(nc.vector.reciprocal(col4[2], col4[1]))
            nc.vector.tensor_tensor(v4(tmp[3]), v4(tmp[3]), col4[2].unsqueeze(2).to_broadcast([P, GRAPHS, P]),
                                    ALU.mult).then_inc(D.sem, 1)
            fill(8)
            dve.wait_ge(Pe.sem, Pe.at("y"))
            nc.vector.scalar_tensor_tensor(x_cur, ps[3], 0.0, x_cur, ALU.max, ALU.add).then_inc(D.sem, 1)
            dve.wait_ge(D.sem, D.at("x"))

        qpk = [tmp[0], tmp[1]]

        def search_pe(pe):
            Pe, A, D = PK
            ln_pe(pe, PK)
            pe.wait_ge(A.sem, A.at("xnT"))

            def queries(b):
                if b >= 2:
                    pe.wait_ge(A.sem, A.at(("q", b - 2)))
                mm(ps[b % 2], chunk(W("pkq"), b), xnT, True, True).then_inc(Pe.sem, 1)

            for b in range(8):
                queries(b)
                pe.wait_ge(A.sem, A.at(("q", b)))
                if b >= 1:
                    pe.wait_ge(A.sem, A.at(("sim", b - 1)))
                for g in range(GRAPHS):
                    for hh in range(2):
                        part = slice(hh * DK, (hh + 1) * DK)
                        ins = mm(chunk(ps[2 + hh], g), tok(qpk[b % 2], g)[part, :],
                                 chunk(W("keys"), b)[part, :], True, True)
                        if g == GRAPHS - 1:
                            ins.then_inc(Pe.sem, 1)

        def search_act(act, ch):
            Pe, A, D = PK
            ln_act(act, PK)
            xnT_act(act, PK)
            for b in range(8):
                act.wait_ge(Pe.sem, Pe.at(("q", b)))
                nc.scalar.copy(qpk[b % 2], ps[b % 2]).then_inc(A.sem, 1)
                if b >= 2:
                    act.wait_ge(D.sem, D.at(("top", b - 2)))
                for hh in range(2):
                    act.wait_ge(Pe.sem, Pe.at(("sim", b, hh)))
                    ins = nc.scalar.copy(simb[:, b % 2, 4 * hh:4 * hh + 4, :], v4(ps[2 + hh]))
                ins.then_inc(A.sem, 1)
            for g in range(GRAPHS):
                act.wait_ge(D.sem, D.at(("gap", g)))
                w = chunk(wgt_new, g, PER_TILE)
                nc.scalar.activation(w, w, ACT.Exp).then_inc(A.sem, 1)

        def search_dve(dve, ch, fill):
            Pe, A, D = PK
            ln_dve(dve, ch, PK, x_cur, xn)
            fill(3)
            for b in range(8):
                p, hp = b // 4, b % 4
                dve.wait_ge(A.sem, A.at(("sim", b)))
                units = [(hh * 4 + g, g, hp * 2 + hh) for g in range(GRAPHS) for hh in range(2)]
                src = simb[:, b % 2]
                for u, g, h in units:
                    ins = nc.vector.max(score[:, g, p, h, 0:8], src[:, u, :])
                ch.link(ins)
                for u, g, h in units:
                    ins = nc.vector.match_replace(simr[:, u, :], score[:, g, p, h, 0:8], src[:, u, :], LOW)
                fill(3)
                ch.link(ins)
                for u, g, h in units:
                    ins = nc.vector.max(score[:, g, p, h, 8:16], simr[:, u, :])
                fill(3)
                ch.link(ins)
                for u, g, h in units:
                    nc.vector.max_index(place[:, g, p, h, 0:8], score[:, g, p, h, 0:8], src[:, u, :])
                fill(3)
                for u, g, h in units:
                    ins = nc.vector.max_index(place[:, g, p, h, 8:16], score[:, g, p, h, 8:16], simr[:, u, :])
                ins.then_inc(D.sem, 1)
                fill(3)
            dve.wait_ge(D.sem, D.at(("top", 7)))
            nc.vector.tensor_copy(placef[:, :, 0], place[:, :, 0])
            ch.link(nc.vector.tensor_scalar(placef[:, :, 1], place[:, :, 1], float(NUM_KEYS), None, ALU.mult))
            for g in range(GRAPHS):
                for src, dst in ((score, cand), (placef, code)):
                    a, c = src[:, g, 0], src[:, g, 1]
                    for i in range(5):
                        n, o = ROW_LEN[i], ROW_OFF[i]
                        nc.vector.tensor_tensor(dst[:, :, o:o + n], a[:, :, i:i + 1].to_broadcast([P, HEADS, n]),
                                                c[:, :, 0:n], ALU.add)
                    o = ROW_OFF[5]
                    nc.vector.tensor_tensor(dst[:, :, o:o + 6].rearrange("p h (i j) -> p h i j", i=3),
                                            a[:, :, 5:8].unsqueeze(3).to_broadcast([P, HEADS, 3, 2]),
                                            c[:, :, 0:2].unsqueeze(2).to_broadcast([P, HEADS, 3, 2]), ALU.add)
                    o = ROW_OFF[8]
                    ins = nc.vector.tensor_tensor(dst[:, :, o:o + 8], a[:, :, 8:16],
                                                  c[:, :, 0:1].to_broadcast([P, HEADS, 8]), ALU.add)
                ch.link(ins)
                fill(2)
                nc.vector.tensor_tensor(code, code, rank_code.unsqueeze(1).to_broadcast([P, HEADS, CAND]), ALU.add)
                for h in range(HEADS):
                    ins = nc.vector.max(fscore[:, h, 0:8], cand[:, h, :])
                ch.link(ins)
                for h in range(HEADS):
                    ins = nc.vector.match_replace(candr[:, h, :], fscore[:, h, 0:8], cand[:, h, :], LOW)
                ch.link(ins)
                for h in range(HEADS):
                    ins = nc.vector.max(fscore[:, h, 8:16], candr[:, h, :])
                ch.link(ins)
                fill(2)
                nc.vector.tensor_tensor(chunk(wgt_new, g, PER_TILE).rearrange("p (h k) -> p h k", h=HEADS), fscore,
                                        fscore[:, :, 0:1].to_broadcast([P, HEADS, TOPK]), ALU.subtract)\
                    .then_inc(D.sem, 1)
                for h in range(HEADS):
                    nc.vector.max_index(pos[:, h, 0:8], fscore[:, h, 0:8], cand[:, h, :])
                    ins = nc.vector.max_index(pos[:, h, 8:16], fscore[:, h, 8:16], candr[:, h, :])
                ch.link(ins)
                fill(2)
                ch.link(nc.vector.tensor_scalar(posf, pos, float(CODE), None, ALU.mult))
                for q in range(HEADS // 2):
                    hs = slice(2 * q, 2 * q + 2)
                    ch.link(nc.vector.tensor_tensor(look, code[:, hs].unsqueeze(2).to_broadcast([P, 2, TOPK, CAND]),
                                                    posf[:, hs].unsqueeze(3).to_broadcast([P, 2, TOPK, CAND]),
                                                    ALU.subtract))
                    ch.link(nc.vector.tensor_reduce(fidx[:, hs], look, AXX, ALU.min, apply_absolute_value=True))
                    fill(3)
                nc.vector.tensor_tensor(chunk(idx_new, g, PER_TILE).rearrange("p (h k) -> p h k", h=HEADS), fidx,
                                        head_base.unsqueeze(2).to_broadcast([P, HEADS, TOPK]), ALU.add)\
                    .then_inc(D.sem, 1)
                w = chunk(wgt_new, g, PER_TILE).rearrange("p (h k) -> p h k", h=HEADS)
                dve.wait_ge(A.sem, A.at(("w", g)))
                ch.link(nc.vector.tensor_reduce(wsum, w, AXX, ALU.add))
                ch.link(nc.vector.reciprocal(wsum, wsum))
                ch.link(nc.vector.tensor_tensor(w, w, wsum.unsqueeze(2).to_broadcast([P, HEADS, TOPK]), ALU.mult))

        def gather_pool(pool):
            for n in range(GRAPHS * PER_TILE):
                t, k, h = n // PER_TILE, n % PER_TILE // HEADS, n % HEADS
                if n >= RING:
                    pool.wait_ge(sums_done, n - RING + 1)
                c = t * PER_TILE + h * TOPK + k
                pool.indirect_dma_start(ring[:, n % RING, :], None, table_d,
                                        bass.IndirectOffsetOnAxis(idx_cur[:, c:c + 1], 0))\
                    .then_inc(ring_full[n % RING], 16)
            pool.wait_ge(sums_done, GRAPHS * PER_TILE)
            pool.dma_reset(range(ring_full[0].num, ring_full[-1].num + 1))

        def sum_dve(dve, n):
            t, k, h = n // PER_TILE, n % PER_TILE // HEADS, n % HEADS
            c = t * PER_TILE + h * TOPK + k
            w = wgt_cur[:, c:c + 1]
            acc = kv[:, t % 2, h, :]
            dve.wait_ge(ring_full[n % RING], 16 * (n // RING + 1))
            if k == 0:
                if t >= 2:
                    dve.wait_ge(AT[0].sem, AT[0].at("o1", t - 2))
                nc.vector.tensor_scalar(acc, ring[:, n % RING, :], w, None, ALU.mult).then_inc(sums_done, 1)
            else:
                dve.wait_ge(sums_done, n - HEADS + 1)
                nc.vector.scalar_tensor_tensor(acc, ring[:, n % RING, :], w, acc, ALU.mult, ALU.add)\
                    .then_inc(sums_done, 1)

        def attend_pe(pe, t):
            Pe, A, D = AT
            pe.wait_ge(sums_done, (t + 1) * PER_TILE)
            for f in range(2):
                hs = [4 * f + j for j in range(4)]
                if f == 1 or t >= 1:
                    pe.wait_ge(A.sem, A.at("pT0", t) if f else A.at("pT1", t - 1))
                for j, h in enumerate(hs):
                    ins = mm(chunk(ps[5], j), chunk(W("wq"), h), tok(xnT_mid, t), True, True)
                ins.then_inc(Pe.sem, 1)
                if f == 1 or t >= 1:
                    pe.wait_ge(A.sem, A.at("o0", t) if f else A.at("o1", t - 1))
                for j, h in enumerate(hs):
                    ins = nc.tensor.transpose(chunk(ps[6], j), kv[:, t % 2, h, 0:P], ident)
                ins.then_inc(Pe.sem, 1)
                pe.wait_ge(A.sem, A.at(f"k{f}", t))
                if f == 1 or t >= 1:
                    pe.wait_ge(D.sem, D.at("x0", t) if f else D.at("x1", t - 1))
                for j, h in enumerate(hs):
                    ins = mm(chunk(ps[7], j), chunk(at_q, j), chunk(at_k, j), True, True)
                ins.then_inc(Pe.sem, 1)
                pe.wait_ge(D.sem, D.at(f"p{f}", t))
                for j, h in enumerate(hs):
                    ins = nc.tensor.transpose(chunk(ps[5], j), chunk(at_s, j), ident)
                ins.then_inc(Pe.sem, 1)
                pe.wait_ge(A.sem, A.at(f"pT{f}", t))
                for j, h in enumerate(hs):
                    ins = mm(chunk(ps[6], j), kv[:, t % 2, h, P:2 * P], chunk(at_q, j), True, True)
                ins.then_inc(Pe.sem, 1)
                pe.wait_ge(A.sem, A.at(f"o{f}", t))
                for j, h in enumerate(hs):
                    ins = mm(ps[7][:, 0:P], chunk(at_k, j), chunk(W("wo"), h), j == 0, j == 3)
                ins.then_inc(Pe.sem, 1)

        def attend_act(act, t):
            Pe, A, D = AT
            for f in range(2):
                act.wait_ge(Pe.sem, Pe.at(f"q{f}", t))
                nc.scalar.mul(at_q, ps[5], float(P) ** -0.5).then_inc(A.sem, 1)
                act.wait_ge(Pe.sem, Pe.at(f"k{f}", t))
                nc.scalar.copy(at_k, ps[6]).then_inc(A.sem, 1)
                act.wait_ge(D.sem, D.at(f"s{f}", t))
                for j in range(4):
                    ins = nc.scalar.activation(chunk(at_s, j), chunk(at_s, j), ACT.Exp, bias=at_max[:, j:j + 1],
                                               accum_out=at_sum[:, j:j + 1])
                ins.then_inc(A.sem, 1)
                act.wait_ge(Pe.sem, Pe.at(f"pT{f}", t))
                nc.scalar.copy(at_q, ps[5]).then_inc(A.sem, 1)
                act.wait_ge(Pe.sem, Pe.at(f"o{f}", t))
                nc.scalar.copy(at_k, ps[6]).then_inc(A.sem, 1)

        def attend_dve(dve, ch, t, fill):
            Pe, A, D = AT
            for f in range(2):
                dve.wait_ge(Pe.sem, Pe.at(f"s{f}", t))
                ch.link(nc.vector.tensor_tensor(v4(at_s), v4(ps[7]),
                                                causal.unsqueeze(1).to_broadcast([P, 4, P]), ALU.add))
                nc.vector.tensor_reduce(at_max, v4(at_s), AXX, ALU.max, negate=True).then_inc(D.sem, 1)
                fill(3)
                dve.wait_ge(A.sem, A.at(f"e{f}", t))
                ch.link(nc.vector.reciprocal(at_sum, at_sum))
                nc.vector.tensor_tensor(v4(at_s), v4(at_s), at_sum.unsqueeze(2).to_broadcast([P, 4, P]), ALU.mult)\
                    .then_inc(D.sem, 1)
                fill(8)
                dve.wait_ge(Pe.sem, Pe.at(f"y{f}", t))
                nc.vector.tensor_tensor(tok(x_mid, t), tok(x_mid, t), ps[7][:, 0:P], ALU.add).then_inc(D.sem, 1)
                dve.wait_ge(D.sem, D.at(f"x{f}", t))

        def l3gnn_pe(pe):
            Pe, A, D = G3
            ln_pe(pe, G3)
            for g in range(GRAPHS):
                ins = mm(tok(ps[1], g), tok(xn, g), tok(adjT_old, g), True, True)
            ins.then_inc(Pe.sem, 1)
            pe.wait_ge(D.sem, D.at("h"))
            for b in range(2):
                mm(ps[2 + b], chunk(W("g3w1"), b), tmp[0], True, True).then_inc(Pe.sem, 1)
            bias_row(ps[4], R("g3b2"), P)
            pe.wait_ge(A.sem, A.at("h1"))
            for g in range(GRAPHS):
                for b in range(2):
                    ins = mm(tok(ps[4], g), tok(tmp[1 + b], g), chunk(W("g3w2"), b), False,
                             g == GRAPHS - 1 and b == 1)
            ins.then_inc(Pe.sem, 1)

        def l3gnn_act(act, ch):
            Pe, A, D = G3
            ln_act(act, G3)
            xnT_act(act, G3)
            for b in range(2):
                act.wait_ge(Pe.sem, Pe.at(f"h{b}"))
                nc.scalar.activation(tmp[1 + b], ps[2 + b], ACT.Relu, bias=C("g3b1", b)).then_inc(A.sem, 1)

        def l3gnn_dve(dve, ch, fill):
            Pe, A, D = G3
            ln_dve(dve, ch, G3, x_old, xn)
            dve.wait_ge(A.sem, A.at("xnT"))
            dve.wait_ge(Pe.sem, Pe.at("agg"))
            nc.vector.scalar_tensor_tensor(tmp[0], xnT, eps1[:, 0:1], ps[1], ALU.mult, ALU.add)\
                .then_inc(D.sem, 1)
            fill(4)
            dve.wait_ge(Pe.sem, Pe.at("y"))
            nc.vector.tensor_tensor(x_old, x_old, ps[4], ALU.add).then_inc(D.sem, 1)
            dve.wait_ge(D.sem, D.at("x"))

        with nc.Block() as block:
            @block.sync
            def _(sp):
                sp.dma_start(cols, cols_d).then_inc(setup_in, 16)
                sp.dma_start(rows, rows_d).then_inc(setup_in, 16)
                sp.dma_start(b2, b2_d).then_inc(setup_in, 16)
                sp.dma_start(wbig, wbig_d).then_inc(setup_in, 16)
                sp.wait_ge(setup_in, 64)

            @block.gpsimd
            def _(pool):
                pool.memset(ident, 0.0)
                pool.memset(causal, 0.0).then_inc(setup_pool, 1)
                pool.wait_ge(setup_pool, 1)
                pool.affine_select(out=ident, in_=ident, compare_op=ALU.not_equal, fill=1.0, base=0,
                                   pattern=[[-1, P]], channel_multiplier=1)
                pool.affine_select(out=causal, in_=causal, compare_op=ALU.is_ge, fill=LOW, base=0,
                                   pattern=[[-1, P]], channel_multiplier=1)
                pool.iota(iota8, [[1, 8]], base=0, channel_multiplier=0, allow_small_or_imprecise_dtypes=True)
                pool.iota(rank_code, [[1, CAND]], base=0, channel_multiplier=0, allow_small_or_imprecise_dtypes=True)
                pool.iota(head_base, [[1, HEADS]], base=0, channel_multiplier=0,
                          allow_small_or_imprecise_dtypes=True)
                pool.memset(ones, 1.0)
                pool.memset(eps_col, EPS)
                pool.memset(h1pad, 0.0).then_inc(setup_pool, 1)

            @block.vector
            def _(dve):
                ch = Chain(dve, dve_chain)
                dve.wait_ge(setup_in, 64)
                dve.wait_ge(setup_pool, 2)
                ch.link(nc.vector.tensor_scalar(rank_code, rank_code, float(CODE), None, ALU.mult))
                ch.link(nc.vector.tensor_scalar(head_base, head_base, float(NUM_KV), None, ALU.mult))
                ch.link(nc.vector.tensor_copy(expert_row.rearrange("k (e m) -> k e m", e=8),
                                              ident[0:8, 0:8].unsqueeze(2).to_broadcast([8, 8, P])))
                ch.link(nc.vector.tensor_scalar(eps1, C("g3eps"), 1.0, None, ALU.add))
                nc.vector.tensor_tensor(gru_bias, C("bih", 0, 2), C("bhh", 0, 2), ALU.add).then_inc(dve_end, 1)
                dve.wait_ge(act_chain, 1)
                ch.link(nc.vector.reciprocal(bn_scale, bn_scale))
                for k, name in enumerate(("bn1", "bn2")):
                    s, d = bn_scale[:, k:k + 1], bn_shift[:, k:k + 1]
                    ch.link(nc.vector.tensor_tensor(s, s, C(name, 0), ALU.mult))
                    ch.link(nc.vector.tensor_tensor(d, s, C(name, 2), ALU.mult))
                    ch.link(nc.vector.tensor_tensor(d, C(name, 1), d, ALU.subtract))

            @block.scalar
            def _(act):
                act.wait_ge(setup_in, 64)
                act.wait_ge(setup_pool, 2)
                nc.scalar.activation(bn_scale[:, 0:1], C("bn1", 3), ACT.Sqrt, bias=eps_col[:, 0:1])
                nc.scalar.activation(bn_scale[:, 1:2], C("bn2", 3), ACT.Sqrt, bias=eps_col[:, 0:1])\
                    .then_inc(act_chain, 1)
        nums = [s.num for s in sems]
        assert max(nums) - min(nums) + 1 == len(nums)
        all_sems = range(min(nums), max(nums) + 1)
        nc.all_engine_barrier(sems_to_clear=all_sems)

        x_g = x_d.rearrange("(i g) n d -> i n g d", g=GRAPHS)
        adj_g = adj_d.rearrange("(i g) n m -> i n g m", g=GRAPHS)
        out_g = out_d.rearrange("(i g) n d -> i n g d", g=GRAPHS)

        def one_pass(i, front, gather, tail):
            order = []
            if tail:
                order += ["l3gnn", "l3ffn"]
            if front:
                order += ["l0gnn"]
            if gather:
                order += [("attend", 0)]
            if front:
                order += ["l0ffn", "l1gnn"]
            if gather:
                order += [("attend", 1)]
            if front:
                order += ["l1ffn", "l2gnn"]
            if gather:
                order += [("attend", 2)]
            if front:
                order += ["search"]
            if gather:
                order += [("attend", 3)]
            total = GRAPHS * PER_TILE if gather else 0

            with nc.Block() as block:
                @block.sync
                def _(sp):
                    if front:
                        sp.dma_start(v4(x_cur), x_g[i]).then_inc(x_in, 16)
                        sp.dma_start(v4(adj_row), adj_g[i]).then_inc(adj_in, 16)
                    if tail:
                        sp.wait_ge(F3[2].sem, F3[2].at("x"))
                        sp.dma_start(out_g[i - 2], v4(x_old)).then_inc(x_out, 16)
                        sp.wait_ge(x_out, 16)

                @block.gpsimd
                def _(pool):
                    if gather:
                        gather_pool(pool)

                @block.tensor
                def _(pe):
                    for st in order:
                        if st[0] == "attend":
                            attend_pe(pe, st[1])
                        else:
                            {"l3gnn": l3gnn_pe, "l3ffn": l3ffn_pe, "l0gnn": l0gnn_pe, "l0ffn": l0ffn_pe,
                             "l1gnn": l1gnn_pe, "l1ffn": l1ffn_pe, "l2gnn": l2gnn_pe, "search": search_pe}[st](pe)

                @block.scalar
                def _(act):
                    ch = Chain(act, act_chain)
                    for st in order:
                        if st[0] == "attend":
                            attend_act(act, st[1])
                        else:
                            {"l3gnn": l3gnn_act, "l3ffn": l3ffn_act, "l0gnn": l0gnn_act, "l0ffn": l0ffn_act,
                             "l1gnn": l1gnn_act, "l1ffn": l1ffn_act, "l2gnn": l2gnn_act,
                             "search": search_act}[st](act, ch)
                    act.wait_ge(dve_end, 1)
                    if gather:
                        ch.link(nc.scalar.copy(adjT_old, adjT_mid))
                    if front:
                        nc.scalar.copy(adjT_mid, adjT)
                        nc.scalar.copy(xnT_mid, xnT)

                @block.vector
                def _(dve):
                    ch = Chain(dve, dve_chain)
                    done = [0, 2]

                    def fill(n):
                        for _ in range(n):
                            if done[0] >= min(total, done[1] * PER_TILE):
                                return
                            sum_dve(dve, done[0])
                            done[0] += 1

                    for st in order:
                        if st[0] == "attend":
                            fill((st[1] + 1) * PER_TILE - done[0])
                            attend_dve(dve, ch, st[1], fill)
                            done[1] += 1
                        else:
                            {"l3gnn": l3gnn_dve, "l3ffn": l3ffn_dve, "l0gnn": l0gnn_dve, "l0ffn": l0ffn_dve,
                             "l1gnn": l1gnn_dve, "l1ffn": l1ffn_dve, "l2gnn": l2gnn_dve,
                             "search": search_dve}[st](dve, ch, fill)
                    if tail:
                        dve.wait_ge(x_out, 16)
                    if gather:
                        ch.link(nc.vector.tensor_copy(x_old, x_mid))
                    if front:
                        nc.vector.tensor_copy(x_mid, x_cur)
                        nc.vector.tensor_copy(idx_cur, idx_new)
                        nc.vector.tensor_copy(wgt_cur, wgt_new)
                    nc.vector.tensor_copy(rstd, std).then_inc(dve_end, 1)
            nc.all_engine_barrier(sems_to_clear=all_sems)

        one_pass(0, True, False, False)
        one_pass(1, True, True, False)
        with nc.Fori(2, GROUPS) as i:
            one_pass(i, True, True, True)
        one_pass(GROUPS, False, True, True)
        one_pass(GROUPS + 1, False, False, True)


def kernel(**inputs):
    import numpy as np
    import concourse.bacc as _bacc
    from concourse.bass_utils import run_bass_kernel_spmd as _run

    a = {k: np.asarray(v) for k, v in inputs.items()}

    def rows_first(w):
        e, k, n = w.shape
        return w.reshape(e, k // P, P, n).transpose(2, 0, 1, 3).reshape(P, -1)

    def pad(v, n=P):
        return np.concatenate([v, np.zeros((n - v.shape[0],) + v.shape[1:], v.dtype)])

    wih = a["L0_gnn_w_ih"].T
    parts = dict(
        c1=a["L0_gnn_conv1_w"][:, :, 0].T, c2=a["L0_gnn_conv2_w"].transpose(1, 2, 0).reshape(P, -1),
        wse=a["L0_gnn_w_se"].T, wmsg=a["L0_gnn_w_msg"].T, wih=np.concatenate([wih[:P], wih[P:]], 1),
        whh=a["L0_gnn_w_hh"].T, f0wg=a["L0_ffn_Wg"], f0w1=a["L0_ffn_W1"].transpose(1, 0, 2).reshape(P, -1),
        f0w2=rows_first(a["L0_ffn_W2"]), g1w=a["L1_gnn_W_w"].T, g1a=a["L1_gnn_A"], f1r1=a["L1_ffn_router_w1"],
        f1r2=pad(a["L1_ffn_router_w2"]), f1w1=rows_first(a["L1_ffn_expert_w1"]),
        f1w2=rows_first(a["L1_ffn_expert_w2"]), f1w3=rows_first(a["L1_ffn_expert_w3"]),
        g2v=a["L2_gnn_Wv"], g2k=a["L2_gnn_Wk"], g2q=a["L2_gnn_Wq"], g2o=a["L2_gnn_Wo"], pkq=a["L2_ffn_Wq_pk"],
        keys=a["L2_ffn_pk_keys"].transpose(0, 2, 3, 1).reshape(2, 4, 2, DK, P).transpose(2, 3, 0, 1, 4).reshape(P, -1),
        wq=a["L2_ffn_Wq"], wo=a["L2_ffn_Wo"].reshape(HEADS, P, P).transpose(1, 0, 2).reshape(P, -1),
        g3w1=a["L3_gnn_W1"], g3w2=rows_first(a["L3_gnn_W2"][None]), f3wr=a["L3_ffn_Wr"],
        f3w1=a["L3_ffn_W1"].transpose(1, 0, 2).reshape(P, -1), f3w2=rows_first(a["L3_ffn_W2"]))
    wbig = np.concatenate([parts[n] for n, _ in WEIGHTS], 1)
    colp = dict(
        bn1=np.stack([a[f"L0_gnn_bn1_{k}"] for k in "gbmv"], 1), bn2=np.stack([a[f"L0_gnn_bn2_{k}"] for k in "gbmv"], 1),
        bih=a["L0_gnn_b_ih"].reshape(3, P).T, bhh=a["L0_gnn_b_hh"].reshape(3, P).T,
        bse=pad(a["L0_gnn_b_se"])[:, None], f0b1=a["L0_ffn_b1"].reshape(16, P).T, g1b=a["L1_gnn_W_b"][:, None],
        f1rb1=pad(a["L1_ffn_router_b1"])[:, None], f1b1=a["L1_ffn_expert_b1"].T, f1b2=a["L1_ffn_expert_b2"].T,
        g2bk=a["L2_gnn_bk"][:, None], g2bq=a["L2_gnn_bq"][:, None],
        g3eps=np.broadcast_to(a["L3_gnn_eps"][None], (P, 1)), g3b1=a["L3_gnn_b1"].reshape(2, P).T,
        lng=a["L3_ffn_ln_g"].T, lnb=a["L3_ffn_ln_b"].T, f3b1=a["L3_ffn_b1"].reshape(32, P).T,
        gateb=np.broadcast_to(a["L1_gnn_gate_b"][None], (P, 1)), gatew=np.broadcast_to(a["L1_gnn_gate_w"], (P, 256)))
    cols = np.concatenate([colp[n] for n, _ in COLS], 1)
    rowp = dict(bmsg=a["L0_gnn_b_msg"], bg=a["L0_ffn_bg"], g1b=a["L1_gnn_W_b"], rb2=a["L1_ffn_router_b2"],
                bv=a["L2_gnn_bv"], bo=a["L2_gnn_bo"], g3b2=a["L3_gnn_b2"], br=a["L3_ffn_br"])
    rows = np.concatenate([rowp[n] for n, _ in ROWS])[None]
    b2 = np.concatenate([a["L0_ffn_b2"], pad(a["L1_ffn_expert_b3"], 8), a["L3_ffn_b2"]], 1)
    table = np.concatenate([a["L2_ffn_keys_table"], a["L2_ffn_values_table"]], 1)

    nc = _bacc.Bacc("TRN2", target_bir_lowering=False, num_devices=1)
    arrays, args = {}, []
    for name, arr in (("x", a["x"]), ("adj", a["adj"]), ("table", table), ("wbig", wbig), ("cols", cols),
                      ("rows", rows), ("b2", b2)):
        arr = np.ascontiguousarray(arr)
        arrays[f"in_{name}_dram"] = arr
        args.append(nc.dram_tensor(f"in_{name}_dram", arr.shape, mybir.dt.from_np(arr.dtype),
                                   kind="ExternalInput").ap())
    args.append(nc.dram_tensor("out_0_dram", a["x"].shape, F32, kind="ExternalOutput").ap())
    build(nc, *args)
    r = _run(nc, [arrays], core_ids=[0])
    return r.results[0]["out_0_dram"]
```

```python
from contextlib import ExitStack

import concourse.bass as bass
from concourse import mybir

F32 = mybir.dt.float32
U32 = mybir.dt.uint32
ALU = mybir.AluOpType
ACT = mybir.ActivationFunctionType
AXX = mybir.AxisListType.X

P = 128
B = 64
GRAPHS = 4
T = GRAPHS * P
GROUPS = B // GRAPHS
TAPS = 17
PAD = TAPS // 2
HEADS = 8
TOPK = 16
NUM_KEYS = 128
NUM_KV = NUM_KEYS ** 2
DK = 64
RING = 20
PER_TILE = HEADS * TOPK
NEG = 9.0e15
LOW = -3.0e38
PACE = 0.91
EPS = 1e-5
ROW_LEN = [TOPK // (i + 1) for i in range(TOPK)]
ROW_OFF = [sum(ROW_LEN[:i]) for i in range(TOPK)]
CAND = sum(ROW_LEN)
CODE = 2 * NUM_KV

WEIGHTS = [("c1", P), ("c2", TAPS * P), ("wse", 3), ("wmsg", P), ("wih", 6 * P), ("whh", 3 * P),
           ("f0wg", 8), ("f0w1", 8 * 256), ("f0w2", 16 * P), ("g1w", P), ("g1a", P), ("f1r1", 64), ("f1r2", 6),
           ("f1w1", 6 * P), ("f1w2", 6 * P), ("f1w3", 6 * P), ("g2v", P), ("g2k", P), ("g2q", P), ("g2o", P),
           ("pkq", 1024), ("keys", 1024), ("wq", 1024), ("wo", 1024), ("g3w1", 256), ("g3w2", 256),
           ("f3wr", 8), ("f3w1", 8 * 512), ("f3w2", 32 * P)]
COLS = [("bn1", 4), ("bn2", 4), ("bih", 3), ("bhh", 3), ("bse", 1), ("f0b1", 16), ("g1b", 1), ("f1rb1", 1),
        ("f1b1", 6), ("f1b2", 6), ("g2bk", 1), ("g2bq", 1), ("g3eps", 1), ("g3b1", 2), ("lng", 8), ("lnb", 8),
        ("f3b1", 32), ("gateb", 1), ("gatew", 256)]
ROWS = [("bmsg", P), ("bg", 8), ("g1b", P), ("rb2", 6), ("bv", P), ("bo", P), ("g3b2", P), ("br", 8)]


def offsets(parts):
    at, out = 0, {}
    for name, n in parts:
        out[name] = (at, n)
        at += n
    return out, at


class Steps:

    def __init__(self, sem, names):
        self.sem = sem
        self.value = {n: k + 1 for k, n in enumerate(names)}
        self.count = len(names)

    def at(self, name, turn=0):
        return self.value[name] + turn * self.count


def build(nc, x_d, adj_d, table_d, wbig_d, cols_d, rows_d, b2_d, out_d):
    woff, wn = offsets(WEIGHTS)
    coff, cn = offsets(COLS)
    roff, rn = offsets(ROWS)
    with ExitStack() as ctx:
        def sb(name, shape, dt=F32):
            return ctx.enter_context(nc.sbuf_tensor(name, shape, dt))[:]

        sems = []

        def sem(name):
            sems.append(ctx.enter_context(nc.semaphore(name)))
            return sems[-1]

        wbig = sb("wbig", [P, wn])
        cols = sb("cols", [P, cn])
        b2 = sb("b2", [8, 3 * P])
        ident = sb("ident", [P, P])
        causal = sb("causal", [P, P])
        iota8 = sb("iota8", [P, 8])
        rank_code = sb("rank_code", [P, CAND])
        head_base = sb("head_base", [P, HEADS])
        ones = sb("ones", [P, P])
        rows = sb("rows", [1, rn])
        eps_col = sb("eps_col", [P, 1])
        bn_scale = sb("bn_scale", [P, 2])
        bn_shift = sb("bn_shift", [P, 2])
        gru_bias = sb("gru_bias", [P, 2])
        eps1 = sb("eps1", [P, 1])

        def W(name, a=0, n=None):
            o, size = woff[name]
            return wbig[:, o + a:o + (size if n is None else a + n)]

        def C(name, k=0, n=1):
            return cols[:, coff[name][0] + k:coff[name][0] + k + n]

        def R(name):
            o, n = roff[name]
            return rows[:, o:o + n]

        x_cur = sb("x_cur", [P, T])
        x_mid = sb("x_mid", [P, T])
        x_old = sb("x_old", [P, T])
        adj_row = sb("adj_row", [P, T])
        adjT = sb("adjT", [P, T])
        adjT_mid = sb("adjT_mid", [P, T])
        adjT_old = sb("adjT_old", [P, T])
        xn = sb("xn", [P, T])
        xnT = sb("xnT", [P, T])
        xnT_mid = sb("xnT_mid", [P, T])
        idx_new = sb("idx_new", [P, GRAPHS * PER_TILE], U32)
        idx_cur = sb("idx_cur", [P, GRAPHS * PER_TILE], U32)
        wgt_new = sb("wgt_new", [P, GRAPHS * PER_TILE])
        wgt_cur = sb("wgt_cur", [P, GRAPHS * PER_TILE])
        ring = sb("ring", [P, RING, 2 * P])
        kv = sb("kv", [P, 2, HEADS, 2 * P])
        bn_st = sb("bn_st", [P, GRAPHS, 6])
        bn_mv = sb("bn_mv", [P, GRAPHS, 2])
        std = sb("std", [P, GRAPHS])
        rstd = sb("rstd", [P, GRAPHS])
        tmps = sb("tmps", [P, 7 * T])
        tmp = [tmps[:, k * T:(k + 1) * T] for k in range(7)]
        h1pad = sb("h1pad", [P, GRAPHS, P + 2 * PAD])
        sml = [sb(f"sml{k}", [P, GRAPHS, 8]) for k in range(5)]
        idx8 = sb("idx8", [P, GRAPHS, 8], U32)
        col4 = [sb(f"col4{k}", [P, GRAPHS]) for k in range(4)]
        maskT = sb("maskT", [8, T])
        three = [tmp[k][0:3, :] for k in (5, 6, 4)]
        sq_row = three[1][0:1, :]
        simb = sb("simb", [P, 2, 8, P])
        simr = tmps[:, 2 * T:4 * T].rearrange("p (u k) -> p u k", u=8)
        score = sb("score", [P, GRAPHS, 2, HEADS, TOPK])
        place = sb("place", [P, GRAPHS, 2, HEADS, TOPK], U32)
        placef = place.bitcast(F32)
        cand, code = (tmp[k][:, 0:HEADS * CAND].rearrange("p (h c) -> p h c", h=HEADS) for k in (4, 5))
        fscore, pos, posf, fidx = (tmp[6][:, k * PER_TILE:(k + 1) * PER_TILE].rearrange("p (h k) -> p h k", h=HEADS)
                                   for k in range(4))
        pos = pos.bitcast(U32)
        wsum = sb("wsum", [P, HEADS])
        look = simb.rearrange("p a b c -> p (a b c)")[:, 0:2 * TOPK * CAND].rearrange(
            "p (h k c) -> p h k c", h=2, k=TOPK)
        candr = simr.rearrange("p a b -> p (a b)")[:, 0:HEADS * CAND].rearrange("p (h c) -> p h c", h=HEADS)
        at_q = sb("at_q", [P, T])
        at_k = sb("at_k", [P, T])
        at_s = sb("at_s", [P, T])
        at_max = sb("at_max", [P, HEADS])
        at_sum = sb("at_sum", [P, HEADS])
        xq_last = sb("xq_last", [P, P])

        ps = [ctx.enter_context(nc.psum_tensor(f"ps{k}", [P, 512], F32))[:] for k in range(8)]

        setup_in = sem("setup_in")
        setup_pool = sem("setup_pool")
        x_in = sem("x_in")
        adj_in = sem("adj_in")
        x_out = sem("x_out")
        dve_chain = sem("dve_chain")
        act_chain = sem("act_chain")
        ring_full = [sem(f"ring_full{k}") for k in range(RING)]
        sums_done = sem("sums_done")
        dve_end = sem("dve_end")

        def steps(stage, pe, act, dve):
            return tuple(Steps(sem(f"{stage}_{e}"), n) for e, n in (("pe", pe), ("act", act), ("dve", dve)))

        LN_P, LN_A, LN_D = ["xnT"], ["std", "xnT"], ["var", "xn"]
        G0 = steps("l0gnn", ["adjT", *LN_P, "h1", "s", "sq", "conv", "dist", "msg", "nmp", "gh", "r", "z", "gi", "o"],
                   ["adjT", *LN_A, "h1", "s", "sq", "xconv", "exp", "msg", "nmp", "r", "z", "n"],
                   [*LN_D, "s2", "conv", "A", "pre_n", "o", "x"])

        def blocks_of(experts, blocks):
            return [(e, b) for e in range(experts) for b in range(blocks)]

        def moe_steps(stage, route_pe, route_act, route_dve, experts, blocks, layers):
            ks = blocks_of(experts, blocks)
            pe = [("route", r) for r in route_pe] + ["wT", "b"] + (pe_order(ks) if layers == 2 else pe_order3(experts))
            act = [("route", r) for r in route_act] + ["wT"]
            act += [("act", *k) for k in ks] if layers == 2 else act_order3(experts)
            dve = [("route", r) for r in route_dve] + ["w"] + [("xe", 0), ("xe", 1)] * (stage == "l3ffn") + ["b"] + dve_order(experts, stage == "l3ffn")
            return steps(stage, [*LN_P, *pe], [*LN_A, *act], [*LN_D, *dve])

        def pe_order(ks):
            out = []
            for n in range(len(ks) + 1):
                if n < len(ks):
                    out.append(("h", *ks[n]))
                if n >= 1:
                    out.append(("acc", *ks[n - 1]))
            return out

        def pe_order3(experts):
            out = []
            for n in range(experts + 2):
                if n < experts:
                    out.append(("h1", n))
                if 1 <= n <= experts:
                    out.append(("h2", n - 1))
                if n >= 2:
                    out.append(("acc", n - 2, 0))
            return out

        def act_order3(experts):
            out = []
            for n in range(experts + 1):
                if n < experts:
                    out.append(("act1", n))
                if n >= 1:
                    out.append(("act", n - 1, 0))
            return out

        def dve_order(experts, normed):
            out = []
            for e in range(experts):
                out += [x_of(e, experts)] + [("xe", e + 2)] * (normed and e + 2 < experts)
            return out

        def x_of(e, experts):
            return ("x", e) if e < experts - 1 else "x"

        F0 = moe_steps("l0ffn", ["gate"], [], [], 8, 2, 2)
        F1 = moe_steps("l1ffn", ["rh", "gate"], ["rh", "exp", "exp2"], ["max", "gap"], 6, 1, 3)
        F3 = moe_steps("l3ffn", ["gate", "xn2T"], ["exp", "std2", "xn2T"], ["max", "var2", "xn2"], 8, 4, 2)
        G1 = steps("l1gnn", [*LN_P, "hT", "h", "hA", "e", "hp"], [*LN_A, "hT", "h", "hA", "exp", "hp", "coeff"],
                   [*LN_D, "e", "att", "logit", "x"])
        G2 = steps("l2gnn", [*LN_P, "v", "q", "k", "s", "pT", "oT", "y"], [*LN_A, "v", "q", "k", "exp", "pT", "oT"],
                   [*LN_D, "s", "p", "x"])
        blk = range(8)
        PK = steps("search", [*LN_P, *[n for b in blk for n in (("q", b), ("sim", b, 0), ("sim", b, 1))]],
                   [*LN_A, *[n for b in blk for n in (("q", b), ("sim", b))], *[("w", g) for g in range(GRAPHS)]],
                   [*LN_D, *[("top", b) for b in blk], *[n for g in range(GRAPHS) for n in (("gap", g), ("idx", g))]])
        AT = steps("attend", ["q0", "q1", "k0", "k1", "s0", "s1", "pT0", "pT1", "o0", "o1", "y"],
                   ["q0", "q1", "k0", "k1", "e0", "e1", "pT0", "pT1", "o0", "o1"],
                   ["s0", "s1", "p0", "p1", "x"])
        G3 = steps("l3gnn", [*LN_P, "agg", "h0", "h1", "y"], [*LN_A, "h0", "h1"], [*LN_D, "h", "x"])

        def v4(ap):
            return ap.rearrange("p (g d) -> p g d", g=GRAPHS)

        def tok(ap, g):
            return ap[:, g * P:(g + 1) * P]

        class Chain:

            def __init__(self, eng, s):
                self.eng, self.sem, self.n = eng, s, 0

            def link(self, ins):
                ins.then_inc(self.sem, 1)
                self.n += 1
                self.eng.wait_ge(self.sem, self.n)

        def ln_dve(dve, ch, S, x, out, fill):
            Pe, A, D = S
            for g in range(GRAPHS):
                ins = nc.vector.bn_stats(bn_st[:, g, :], tok(x, g))
            ch.link(ins)
            for g in range(GRAPHS):
                ins = nc.vector.bn_aggr(bn_mv[:, g, :], bn_st[:, g, :])
            ins.then_inc(D.sem, 1)
            fill(4)
            dve.wait_ge(A.sem, A.at("std"))
            ch.link(nc.vector.reciprocal(rstd, std))
            for g in range(GRAPHS):
                ins = nc.vector.tensor_scalar(tok(out, g), tok(x, g), bn_mv[:, g, 0:1], rstd[:, g:g + 1],
                                              ALU.subtract, ALU.mult)
            ins.then_inc(D.sem, 1)
            dve.wait_ge(D.sem, D.at("xn"))

        def ln_act(act, S, var="var"):
            Pe, A, D = S
            act.wait_ge(D.sem, D.at(var))
            nc.scalar.activation(std, bn_mv[:, :, 1], ACT.Sqrt, bias=eps_col[:, 0:1]).then_inc(A.sem, 1)

        def xnT_act(act, S, to=xnT):
            Pe, A, D = S
            act.wait_ge(Pe.sem, Pe.at("xnT"))
            nc.scalar.copy(to, ps[0]).then_inc(A.sem, 1)

        def ln_pe(pe, S):
            Pe, A, D = S
            pe.wait_ge(D.sem, D.at("xn"))
            for g in range(GRAPHS):
                ins = nc.tensor.transpose(tok(ps[0], g), tok(xn, g), ident)
            ins.then_inc(Pe.sem, 1)

        def mm(out, lhsT, rhs, start, stop):
            return nc.tensor.matmul(out, lhsT, rhs, start=start, stop=stop, skip_group_check=True)

        def bias_row(out, row, n):
            return mm(out, ones[0:1, :], row.unsqueeze(1).to_broadcast([1, GRAPHS, n]), True, False)

        def chunk(ap, k, n=P):
            return ap[:, k * n:(k + 1) * n]

        def l0gnn_pe(pe):
            Pe, A, D = G0
            pe.wait_ge(adj_in, 16)
            for g in range(GRAPHS):
                ins = nc.tensor.transpose(tok(ps[1], g), tok(adj_row, g), ident)
            ins.then_inc(Pe.sem, 1)
            ln_pe(pe, G0)
            pe.wait_ge(A.sem, A.at("xnT"))
            mm(ps[1], W("c1"), xnT, True, True).then_inc(Pe.sem, 1)
            mm(ps[3][0:3, :], W("wse"), xnT, True, True).then_inc(Pe.sem, 1)
            pe.wait_ge(D.sem, D.at("s2"))
            mm(ps[4][0:1, :], ones[0:3, 0:1], three[2], True, True).then_inc(Pe.sem, 1)
            pe.wait_ge(A.sem, A.at("h1"))
            for k in range(TAPS):
                ins = mm(ps[2], chunk(W("c2"), k), h1pad[:, :, k:k + P], k == 0, k == TAPS - 1)
            ins.then_inc(Pe.sem, 1)
            pe.wait_ge(A.sem, A.at("sq"))
            for g in range(GRAPHS):
                mm(tok(ps[0], g), tok(sq_row, g), ones[0:1, :], True, False)
                mm(tok(ps[0], g), ones[0:1, :], tok(sq_row, g), False, False)
                ins = mm(tok(ps[0], g), tok(maskT[0:3, :], g), tok(three[0], g), False, True)
            ins.then_inc(Pe.sem, 1)
            bias_row(ps[1], R("bmsg"), P)
            for g in range(GRAPHS):
                ins = mm(tok(ps[1], g), tok(xnT, g), W("wmsg"), False, g == GRAPHS - 1)
            ins.then_inc(Pe.sem, 1)
            pe.wait_ge(D.sem, D.at("A"))
            pe.wait_ge(A.sem, A.at("msg"))
            for g in range(GRAPHS):
                ins = mm(tok(ps[3], g), tok(tmp[2], g), tok(tmp[1], g), True, True)
            ins.then_inc(Pe.sem, 1)
            mm(ps[4], chunk(W("whh"), 2), xnT, True, True).then_inc(Pe.sem, 1)
            pe.wait_ge(A.sem, A.at("nmp"))
            for k, bank in enumerate((0, 1, 2)):
                mm(ps[bank], chunk(W("wih"), k), tmp[0], True, False)
                ins = mm(ps[bank], chunk(W("wih"), 3 + k), tmp[3], False, k == 2)
                if k < 2:
                    ins = mm(ps[bank], chunk(W("whh"), k), xnT, False, True)
                ins.then_inc(Pe.sem, 1)
            pe.wait_ge(D.sem, D.at("o"))
            for g in range(GRAPHS):
                ins = nc.tensor.transpose(tok(ps[3], g), tok(tmp[4], g), ident)
            ins.then_inc(Pe.sem, 1)

        def l0gnn_act(act, ch):
            Pe, A, D = G0
            act.wait_ge(Pe.sem, Pe.at("adjT"))
            nc.scalar.copy(adjT, ps[1]).then_inc(A.sem, 1)
            ln_act(act, G0)
            xnT_act(act, G0)
            act.wait_ge(Pe.sem, Pe.at("h1"))
            nc.scalar.activation(h1pad[:, :, PAD:PAD + P], v4(ps[1]), ACT.Relu, bias=bn_shift[:, 0:1],
                                 scale=bn_scale[:, 0:1]).then_inc(A.sem, 1)
            act.wait_ge(Pe.sem, Pe.at("s"))
            nc.scalar.activation(three[0], ps[3][0:3, :], ACT.Identity, bias=C("bse")[0:3, :]).then_inc(A.sem, 1)
            act.wait_ge(Pe.sem, Pe.at("sq"))
            nc.scalar.copy(sq_row, ps[4][0:1, :]).then_inc(A.sem, 1)
            act.wait_ge(D.sem, D.at("conv"))
            nc.scalar.activation(tmp[0], tmp[0], ACT.Relu, bias=bn_shift[:, 1:2]).then_inc(A.sem, 1)
            act.wait_ge(Pe.sem, Pe.at("dist"))
            nc.scalar.activation(tmp[1], ps[0], ACT.Exp, scale=-1.0).then_inc(A.sem, 1)
            act.wait_ge(Pe.sem, Pe.at("msg"))
            nc.scalar.activation(tmp[2], ps[1], ACT.Relu).then_inc(A.sem, 1)
            act.wait_ge(Pe.sem, Pe.at("nmp"))
            nc.scalar.copy(tmp[3], ps[3]).then_inc(A.sem, 1)
            for k, name in enumerate("rz"):
                act.wait_ge(Pe.sem, Pe.at(name))
                nc.scalar.activation(tmp[4 + k], ps[k], ACT.Sigmoid, bias=gru_bias[:, k:k + 1])\
                    .then_inc(A.sem, 1)
            act.wait_ge(D.sem, D.at("pre_n"))
            nc.scalar.activation(tmp[6], tmp[6], ACT.Tanh, bias=C("bih", 2)).then_inc(A.sem, 1)

        def l0gnn_dve(dve, ch, fill):
            Pe, A, D = G0
            dve.wait_ge(x_in, 16)
            ln_dve(dve, ch, G0, x_cur, xn, fill)
            fill(6)
            dve.wait_ge(A.sem, A.at("s"))
            nc.vector.tensor_scalar(maskT[0:3, :], three[0], -2.0, None, ALU.mult)
            nc.vector.tensor_tensor(three[2], three[0], three[0], ALU.mult).then_inc(D.sem, 1)
            fill(18)
            dve.wait_ge(Pe.sem, Pe.at("conv"))
            nc.vector.scalar_tensor_tensor(tmp[0], ps[2], bn_scale[:, 1:2], xnT, ALU.mult, ALU.add)\
                .then_inc(D.sem, 1)
            fill(4)
            dve.wait_ge(A.sem, A.at("exp"))
            nc.vector.tensor_tensor(tmp[1], tmp[1], adjT, ALU.mult).then_inc(D.sem, 1)
            fill(12)
            dve.wait_ge(A.sem, A.at("r"))
            dve.wait_ge(Pe.sem, Pe.at("gh"))
            ch.link(nc.vector.scalar_tensor_tensor(tmp[6], ps[4], C("bhh", 2), tmp[4], ALU.add, ALU.mult))
            dve.wait_ge(Pe.sem, Pe.at("gi"))
            nc.vector.tensor_tensor(tmp[6], ps[2], tmp[6], ALU.add).then_inc(D.sem, 1)
            fill(3)
            dve.wait_ge(A.sem, A.at("n"))
            ch.link(nc.vector.tensor_tensor(tmp[4], xnT, tmp[6], ALU.subtract))
            ch.link(nc.vector.tensor_tensor(tmp[4], tmp[5], tmp[4], ALU.mult))
            nc.vector.tensor_tensor(tmp[4], tmp[4], tmp[6], ALU.add).then_inc(D.sem, 1)
            fill(4)
            dve.wait_ge(Pe.sem, Pe.at("o"))
            nc.vector.tensor_tensor(x_cur, x_cur, ps[3], ALU.add).then_inc(D.sem, 1)
            dve.wait_ge(D.sem, D.at("x"))

        def gate_pe(w, n, row):
            mm(ps[1][:, 0:GRAPHS * n], ones[0:1, :], row.unsqueeze(1).to_broadcast([1, GRAPHS, n]), True, False)
            for g in range(GRAPHS):
                ins = mm(ps[1][:, g * n:(g + 1) * n], w(g)[0], w(g)[1], False, g == GRAPHS - 1)
            return ins

        def wT_pe(pe, S):
            Pe, A, D = S
            pe.wait_ge(D.sem, D.at("w"))
            for g in range(GRAPHS):
                ins = nc.tensor.transpose(tok(ps[2][0:8, :], g), sml[4][:, g, :], ident)
            ins.then_inc(Pe.sem, 1)
            pe.wait_ge(A.sem, A.at("wT"))

        def wT_act(act, S):
            Pe, A, D = S
            act.wait_ge(Pe.sem, Pe.at("wT"))
            nc.scalar.copy(maskT, ps[2][0:8, :]).then_inc(A.sem, 1)

        def bias_pe(pe, S, which, experts):
            Pe, A, D = S
            for g in range(GRAPHS):
                ins = mm(tok(ps[4], g), tok(maskT[0:experts, :], g), b2[0:experts, which * P:(which + 1) * P],
                         True, True)
            ins.then_inc(Pe.sem, 1)

        def acc_pe(pe, S, e, b, blocks, hidden, w2, experts):
            Pe, A, D = S
            pe.wait_ge(A.sem, A.at(("act", e, b)))
            if b == 0 and e >= 2:
                pe.wait_ge(D.sem, D.at(x_of(e - 2, experts)))
            for g in range(GRAPHS):
                ins = mm(tok(ps[2 + e % 2], g), tok(hidden, g), w2, b == 0 and g == 0, b == blocks - 1)
            ins.then_inc(Pe.sem, 1)

        def experts_pe(pe, S, experts, blocks, w1, w2, hidden, rhs):
            Pe, A, D = S
            ks = blocks_of(experts, blocks)
            for kind, e, b in pe_order(ks):
                n = ks.index((e, b))
                if kind == "h":
                    if n >= 2:
                        pe.wait_ge(A.sem, A.at(("act", *ks[n - 2])))
                    if rhs is not None and b == 0:
                        pe.wait_ge(D.sem, D.at(("xe", e)))
                    mm(ps[n % 2], chunk(w1, n), xnT if rhs is None else rhs[e % 2], True, True)\
                        .then_inc(Pe.sem, 1)
                else:
                    acc_pe(pe, S, e, b, blocks, hidden[n % 3], chunk(w2, n), experts)

        def experts_act(act, S, experts, blocks, bias, hidden, some=None):
            Pe, A, D = S
            ks = blocks_of(experts, blocks)
            for n, (e, b) in enumerate(ks):
                if some is not None and e not in some:
                    continue
                act.wait_ge(Pe.sem, Pe.at(("h", e, b)))
                if n >= 3:
                    act.wait_ge(Pe.sem, Pe.at(("acc", *ks[n - 3])))
                nc.scalar.activation(hidden[n % 3], ps[n % 2], ACT.Gelu, bias=C(bias, n)).then_inc(A.sem, 1)

        def expert_dve(dve, S, e, experts, blocks, x, xe=None, xT=None):
            Pe, A, D = S
            if e == 0:
                dve.wait_ge(Pe.sem, Pe.at("b"))
                nc.vector.tensor_tensor(x, x, ps[4], ALU.add).then_inc(D.sem, 1)
            dve.wait_ge(Pe.sem, Pe.at(("acc", e, blocks - 1)))
            dve.wait_ge(D.sem, D.at(x_of(e - 1, experts)) if e else D.at("b"))
            for g in range(GRAPHS):
                ins = nc.vector.scalar_tensor_tensor(tok(x, g), tok(ps[2 + e % 2], g), sml[4][:, g, e:e + 1],
                                                     tok(x, g), ALU.mult, ALU.add)
            ins.then_inc(D.sem, 1)
            if xe is not None and e + 2 < experts:
                expert_in_dve(dve, S, e + 2, blocks, xe, xT)

        def expert_in_dve(dve, S, e, blocks, xe, xT):
            Pe, A, D = S
            if e >= 2:
                dve.wait_ge(Pe.sem, Pe.at(("h", e - 2, blocks - 1)))
            nc.vector.tensor_scalar(xe[e % 2], xT, C("lng", e), C("lnb", e), ALU.mult, ALU.add)\
                .then_inc(D.sem, 1)

        def experts_dve(dve, S, experts, blocks, fill, per, x):
            for e in range(experts):
                fill(per)
                expert_dve(dve, S, e, experts, blocks, x)
            dve.wait_ge(S[2].sem, S[2].at("x"))

        def top2_dve(dve, ch, scores):
            for g in range(GRAPHS):
                ins = nc.vector.max(sml[1][:, g, :], scores[:, g, :])
            ch.link(ins)
            for g in range(GRAPHS):
                ins = nc.vector.max_index(idx8[:, g, :], sml[1][:, g, :], scores[:, g, :])
            ch.link(ins)
            ch.link(nc.vector.tensor_copy(sml[4], idx8))
            it = iota8.unsqueeze(1).to_broadcast([P, GRAPHS, 8])
            nc.vector.tensor_tensor(sml[2], sml[4][:, :, 0:1].to_broadcast([P, GRAPHS, 8]), it, ALU.is_equal)
            ch.link(nc.vector.tensor_tensor(sml[3], sml[4][:, :, 1:2].to_broadcast([P, GRAPHS, 8]), it, ALU.is_equal))

        def b8(ap):
            return ap.unsqueeze(2).to_broadcast([P, GRAPHS, 8])

        def l0ffn_pe(pe):
            Pe, A, D = F0
            ln_pe(pe, F0)
            pe.wait_ge(A.sem, A.at("xnT"))
            gate_pe(lambda g: (tok(xnT, g), W("f0wg")), 8, R("bg")).then_inc(Pe.sem, 1)
            wT_pe(pe, F0)
            bias_pe(pe, F0, 0, 8)
            experts_pe(pe, F0, 8, 2, W("f0w1"), W("f0w2"), tmp, None)

        def l0ffn_act(act, ch):
            ln_act(act, F0)
            xnT_act(act, F0)
            wT_act(act, F0)
            experts_act(act, F0, 8, 2, "f0b1", tmp)

        def l0ffn_dve(dve, ch, fill):
            Pe, A, D = F0
            ln_dve(dve, ch, F0, x_cur, xn, fill)
            fill(8)
            dve.wait_ge(Pe.sem, Pe.at(("route", "gate")))
            ch.link(nc.vector.tensor_copy(sml[0], ps[1][:, 0:32].rearrange("p (g e) -> p g e", g=GRAPHS)))
            top2_dve(dve, ch, sml[0])
            nc.vector.tensor_tensor(sml[4], sml[2], sml[3], ALU.add).then_inc(D.sem, 1)
            fill(6)
            experts_dve(dve, F0, 8, 2, fill, 3.4, x_cur)

        def l1ffn_pe(pe):
            Pe, A, D = F1
            ln_pe(pe, F1)
            pe.wait_ge(A.sem, A.at("xnT"))
            mm(ps[3][0:64, :], W("f1r1"), xnT, True, True).then_inc(Pe.sem, 1)
            pe.wait_ge(A.sem, A.at(("route", "rh")))
            gate_pe(lambda g: (tok(tmp[5][0:64, :], g), W("f1r2")[0:64, :]), 6, R("rb2")).then_inc(Pe.sem, 1)
            wT_pe(pe, F1)
            bias_pe(pe, F1, 1, 6)
            for item in pe_order3(6):
                e = item[1]
                if item[0] == "h1":
                    if e >= 1:
                        pe.wait_ge(A.sem, A.at(("act1", e - 1)))
                    mm(ps[0], chunk(W("f1w1"), e), xnT, True, True).then_inc(Pe.sem, 1)
                elif item[0] == "h2":
                    pe.wait_ge(A.sem, A.at(("act1", e)))
                    if e >= 1:
                        pe.wait_ge(A.sem, A.at(("act", e - 1, 0)))
                    mm(ps[1], chunk(W("f1w2"), e), tmp[4 + e % 2], True, True).then_inc(Pe.sem, 1)
                else:
                    acc_pe(pe, F1, e, 0, 1, tmp[e % 2], chunk(W("f1w3"), e), 6)

        def l1ffn_act(act, ch):
            Pe, A, D = F1
            ln_act(act, F1)
            xnT_act(act, F1)
            act.wait_ge(Pe.sem, Pe.at(("route", "rh")))
            nc.scalar.activation(tmp[5][0:64, :], ps[3][0:64, :], ACT.Relu, bias=C("f1rb1")[0:64, :])\
                .then_inc(A.sem, 1)
            act.wait_ge(D.sem, D.at(("route", "max")))
            nc.scalar.activation(sml[1][:, :, 0:6], sml[1][:, :, 0:6], ACT.Exp).then_inc(A.sem, 1)
            act.wait_ge(D.sem, D.at(("route", "gap")))
            nc.scalar.activation(col4[1], col4[0], ACT.Exp).then_inc(A.sem, 1)
            wT_act(act, F1)
            for item in act_order3(6):
                e = item[1]
                if item[0] == "act1":
                    act.wait_ge(Pe.sem, Pe.at(("h1", e)))
                    if e >= 2:
                        act.wait_ge(Pe.sem, Pe.at(("h2", e - 2)))
                    nc.scalar.activation(tmp[4 + e % 2], ps[0], ACT.Relu, bias=C("f1b1", e)).then_inc(A.sem, 1)
                else:
                    act.wait_ge(Pe.sem, Pe.at(("h2", e)))
                    if e >= 2:
                        act.wait_ge(Pe.sem, Pe.at(("acc", e - 2, 0)))
                    nc.scalar.activation(tmp[e % 2], ps[1], ACT.Relu, bias=C("f1b2", e)).then_inc(A.sem, 1)
        def softmax6_dve(dve, ch, S, n, bank):
            Pe, A, D = S
            lg = bank[:, 0:GRAPHS * n].rearrange("p (g e) -> p g e", g=GRAPHS)
            nc.vector.memset(sml[0], -1.0)
            ch.link(nc.vector.tensor_reduce(col4[0], lg, AXX, ALU.max))
            nc.vector.tensor_tensor(sml[1][:, :, 0:n], lg, col4[0].unsqueeze(2).to_broadcast([P, GRAPHS, n]),
                                    ALU.subtract).then_inc(D.sem, 1)
            dve.wait_ge(A.sem, A.at(("route", "exp")))
            ch.link(nc.vector.tensor_reduce(col4[1], sml[1][:, :, 0:n], AXX, ALU.add))
            ch.link(nc.vector.reciprocal(col4[2], col4[1]))
            ch.link(nc.vector.tensor_tensor(sml[0][:, :, 0:n], sml[1][:, :, 0:n],
                                            col4[2].unsqueeze(2).to_broadcast([P, GRAPHS, n]), ALU.mult))

        def l1ffn_dve(dve, ch, fill):
            Pe, A, D = F1
            ln_dve(dve, ch, F1, x_cur, xn, fill)
            fill(8)
            dve.wait_ge(Pe.sem, Pe.at(("route", "gate")))
            softmax6_dve(dve, ch, F1, 6, ps[1])
            top2_dve(dve, ch, sml[0])
            nc.vector.tensor_tensor(col4[0], sml[1][:, :, 1], sml[1][:, :, 0], ALU.subtract).then_inc(D.sem, 1)
            dve.wait_ge(A.sem, A.at(("route", "exp2")))
            ch.link(nc.vector.tensor_scalar(col4[2], col4[1], 1.0, None, ALU.add))
            ch.link(nc.vector.reciprocal(col4[3], col4[2]))
            ch.link(nc.vector.tensor_tensor(col4[1], col4[1], col4[3], ALU.mult))
            nc.vector.tensor_tensor(sml[2], sml[2], b8(col4[3]), ALU.mult)
            ch.link(nc.vector.tensor_tensor(sml[3], sml[3], b8(col4[1]), ALU.mult))
            nc.vector.tensor_tensor(sml[4], sml[2], sml[3], ALU.add).then_inc(D.sem, 1)
            fill(20)
            experts_dve(dve, F1, 6, 1, fill, 2.6, x_cur)

        l3T, l3_hidden, l3_in = tmp[3], [tmp[0], tmp[1], at_s], [at_q, at_k]

        def l3route_pe(pe):
            Pe, A, D = F3
            ln_pe(pe, F3)
            pe.wait_ge(A.sem, A.at("xnT"))
            gate_pe(lambda g: (tok(l3T, g), W("f3wr")), 8, R("br")).then_inc(Pe.sem, 1)
            pe.wait_ge(D.sem, D.at(("route", "xn2")))
            for g in range(GRAPHS):
                ins = nc.tensor.transpose(tok(ps[3], g), tok(tmp[5], g), ident)
            ins.then_inc(Pe.sem, 1)
            wT_pe(pe, F3)

        def l3experts_pe(pe):
            bias_pe(pe, F3, 2, 8)
            experts_pe(pe, F3, 8, 4, W("f3w1"), W("f3w2"), l3_hidden, l3_in)

        def l3route_act(act, ch):
            Pe, A, D = F3
            ln_act(act, F3)
            xnT_act(act, F3, l3T)
            act.wait_ge(D.sem, D.at(("route", "max")))
            nc.scalar.activation(sml[1], sml[1], ACT.Exp).then_inc(A.sem, 1)
            act.wait_ge(D.sem, D.at(("route", "var2")))
            nc.scalar.activation(std, bn_mv[:, :, 1], ACT.Sqrt, bias=eps_col[:, 0:1]).then_inc(A.sem, 1)
            act.wait_ge(Pe.sem, Pe.at(("route", "xn2T")))
            nc.scalar.copy(l3T, ps[3]).then_inc(A.sem, 1)
            wT_act(act, F3)

        def l3experts_act(act, some=None):
            experts_act(act, F3, 8, 4, "f3b1", l3_hidden, some)

        def l3route_dve(dve, ch, fill):
            Pe, A, D = F3
            ln_dve(dve, ch, F3, x_old, xn, fill)
            fill(4)
            dve.wait_ge(Pe.sem, Pe.at(("route", "gate")))
            softmax6_dve(dve, ch, F3, 8, ps[1])
            top2_dve(dve, ch, sml[0])
            for g in range(GRAPHS):
                ins = nc.vector.bn_stats(bn_st[:, g, :], tok(xn, g))
            ch.link(ins)
            for g in range(GRAPHS):
                ins = nc.vector.bn_aggr(bn_mv[:, g, :], bn_st[:, g, :])
            ins.then_inc(D.sem, 1)
            ch.link(nc.vector.tensor_tensor(col4[0], sml[1][:, :, 0], sml[1][:, :, 1], ALU.add))
            ch.link(nc.vector.reciprocal(col4[1], col4[0]))
            ch.link(nc.vector.tensor_tensor(col4[2], sml[1][:, :, 0], col4[1], ALU.mult))
            ch.link(nc.vector.tensor_tensor(col4[3], sml[1][:, :, 1], col4[1], ALU.mult))
            dve.wait_ge(A.sem, A.at(("route", "std2")))
            ch.link(nc.vector.reciprocal(rstd, std))
            for g in range(GRAPHS):
                ins = nc.vector.tensor_scalar(tok(tmp[5], g), tok(xn, g), bn_mv[:, g, 0:1], rstd[:, g:g + 1],
                                              ALU.subtract, ALU.mult)
            ins.then_inc(D.sem, 1)
            nc.vector.tensor_tensor(sml[2], sml[2], b8(col4[2]), ALU.mult)
            ch.link(nc.vector.tensor_tensor(sml[3], sml[3], b8(col4[3]), ALU.mult))
            nc.vector.tensor_tensor(sml[4], sml[2], sml[3], ALU.add).then_inc(D.sem, 1)
            fill(4)
            dve.wait_ge(A.sem, A.at(("route", "xn2T")))
            for e in range(2):
                expert_in_dve(dve, F3, e, 4, l3_in, l3T)

        def l3expert_dve(dve, e):
            expert_dve(dve, F3, e, 8, 4, x_old, l3_in, l3T)

        def l3experts_dve(dve, ch, fill):
            for e in range(8):
                fill(6.8)
                l3expert_dve(dve, e)

        def l1gnn_pe(pe):
            Pe, A, D = G1
            ln_pe(pe, G1)
            pe.wait_ge(A.sem, A.at("xnT"))
            mm(ps[1], W("g1w"), xnT, True, True).then_inc(Pe.sem, 1)
            bias_row(ps[2], R("g1b"), P)
            for g in range(GRAPHS):
                ins = mm(tok(ps[2], g), tok(xnT, g), W("g1w"), False, g == GRAPHS - 1)
            ins.then_inc(Pe.sem, 1)
            pe.wait_ge(A.sem, A.at("hT"))
            mm(ps[3], W("g1a"), tmp[0], True, True).then_inc(Pe.sem, 1)
            pe.wait_ge(A.sem, A.at("hA"))
            for g in range(GRAPHS):
                mm(tok(ps[4], g), tok(tmp[2], g), tok(tmp[0], g), True, False)
                ins = mm(tok(ps[4], g), tok(tmp[0], g), tok(tmp[2], g), False, True)
            ins.then_inc(Pe.sem, 1)
            pe.wait_ge(D.sem, D.at("att"))
            for g in range(GRAPHS):
                ins = mm(tok(ps[1], g), tok(tmp[3], g), tok(tmp[1], g), True, True)
            ins.then_inc(Pe.sem, 1)

        def l1gnn_act(act, ch):
            Pe, A, D = G1
            ln_act(act, G1)
            xnT_act(act, G1)
            act.wait_ge(Pe.sem, Pe.at("hT"))
            nc.scalar.activation(tmp[0], ps[1], ACT.Identity, bias=C("g1b")).then_inc(A.sem, 1)
            act.wait_ge(Pe.sem, Pe.at("h"))
            nc.scalar.copy(tmp[1], ps[2]).then_inc(A.sem, 1)
            act.wait_ge(Pe.sem, Pe.at("hA"))
            nc.scalar.copy(tmp[2], ps[3]).then_inc(A.sem, 1)
            act.wait_ge(D.sem, D.at("e"))
            for g in range(GRAPHS):
                ins = nc.scalar.activation(tok(tmp[3], g), tok(tmp[4], g), ACT.Exp, bias=col4[0][:, g:g + 1],
                                           accum_out=col4[1][:, g:g + 1])
            ins.then_inc(A.sem, 1)
            act.wait_ge(Pe.sem, Pe.at("hp"))
            nc.scalar.activation(tmp[5], ps[1], ACT.Relu).then_inc(A.sem, 1)
            act.wait_ge(D.sem, D.at("logit"))
            nc.scalar.activation(col4[3], col4[2], ACT.Sigmoid, bias=C("gateb")).then_inc(A.sem, 1)

        def l1gnn_dve(dve, ch, fill):
            Pe, A, D = G1
            ln_dve(dve, ch, G1, x_cur, xn, fill)
            fill(4)
            ch.link(nc.vector.tensor_scalar(tmp[6], adjT, 0.0, None, ALU.is_gt))
            ch.link(nc.vector.tensor_scalar(tmp[5], tmp[6], -1.0, NEG, ALU.add, ALU.mult))
            fill(12)
            dve.wait_ge(Pe.sem, Pe.at("e"))
            ch.link(nc.vector.tensor_tensor(tmp[4], ps[4], tmp[6], ALU.mult))
            ch.link(nc.vector.tensor_tensor(tmp[4], tmp[4], tmp[5], ALU.add))
            nc.vector.tensor_reduce(col4[0], v4(tmp[4]), AXX, ALU.max, negate=True).then_inc(D.sem, 1)
            fill(4)
            dve.wait_ge(A.sem, A.at("exp"))
            ch.link(nc.vector.reciprocal(col4[2], col4[1]))
            for g in range(GRAPHS):
                ins = nc.vector.scalar_tensor_tensor(tok(tmp[3], g), tok(tmp[3], g), col4[2][:, g:g + 1],
                                                     tok(adjT, g), ALU.mult, ALU.mult)
            ins.then_inc(D.sem, 1)
            gw = C("gatew", 0, 256)
            ch.link(nc.vector.tensor_tensor(v4(tmp[6]), v4(xn), gw[:, 0:P].unsqueeze(1).to_broadcast([P, GRAPHS, P]),
                                            ALU.mult))
            dve.wait_ge(A.sem, A.at("hp"))
            ch.link(nc.vector.tensor_tensor(v4(tmp[4]), v4(tmp[5]),
                                            gw[:, P:2 * P].unsqueeze(1).to_broadcast([P, GRAPHS, P]), ALU.mult))
            ch.link(nc.vector.tensor_tensor(tmp[4], tmp[4], tmp[6], ALU.add))
            nc.vector.tensor_reduce(col4[2], v4(tmp[4]), AXX, ALU.add).then_inc(D.sem, 1)
            ch.link(nc.vector.tensor_tensor(tmp[6], xn, tmp[5], ALU.subtract))
            fill(2)
            dve.wait_ge(A.sem, A.at("coeff"))
            for g in range(GRAPHS):
                ins = nc.vector.scalar_tensor_tensor(tok(tmp[6], g), tok(tmp[6], g), col4[3][:, g:g + 1],
                                                     tok(tmp[5], g), ALU.mult, ALU.add)
            ch.link(ins)
            nc.vector.tensor_tensor(x_cur, x_cur, tmp[6], ALU.add).then_inc(D.sem, 1)
            dve.wait_ge(D.sem, D.at("x"))

        def l2gnn_pe(pe):
            Pe, A, D = G2
            ln_pe(pe, G2)
            pe.wait_ge(A.sem, A.at("xnT"))
            bias_row(ps[1], R("bv"), P)
            for g in range(GRAPHS):
                ins = mm(tok(ps[1], g), tok(xnT, g), W("g2v"), False, g == GRAPHS - 1)
            ins.then_inc(Pe.sem, 1)
            mm(ps[2], W("g2q"), xnT, True, True).then_inc(Pe.sem, 1)
            mm(ps[3], W("g2k"), xnT, True, True).then_inc(Pe.sem, 1)
            pe.wait_ge(A.sem, A.at("k"))
            for g in range(GRAPHS):
                ins = mm(tok(ps[4], g), tok(tmp[1], g), tok(tmp[2], g), True, True)
            ins.then_inc(Pe.sem, 1)
            pe.wait_ge(D.sem, D.at("p"))
            for g in range(GRAPHS):
                ins = nc.tensor.transpose(tok(ps[1], g), tok(tmp[3], g), ident)
            ins.then_inc(Pe.sem, 1)
            pe.wait_ge(A.sem, A.at("pT"))
            for g in range(GRAPHS):
                ins = mm(tok(ps[2], g), tok(tmp[0], g), tok(tmp[4], g), True, True)
            ins.then_inc(Pe.sem, 1)
            bias_row(ps[3], R("bo"), P)
            pe.wait_ge(A.sem, A.at("oT"))
            for g in range(GRAPHS):
                ins = mm(tok(ps[3], g), tok(tmp[1], g), W("g2o"), False, g == GRAPHS - 1)
            ins.then_inc(Pe.sem, 1)

        def l2gnn_act(act, ch):
            Pe, A, D = G2
            ln_act(act, G2)
            xnT_act(act, G2)
            act.wait_ge(Pe.sem, Pe.at("v"))
            nc.scalar.activation(tmp[0], ps[1], ACT.Relu).then_inc(A.sem, 1)
            act.wait_ge(Pe.sem, Pe.at("q"))
            nc.scalar.activation(tmp[1], ps[2], ACT.Relu, bias=C("g2bq")).then_inc(A.sem, 1)
            act.wait_ge(Pe.sem, Pe.at("k"))
            nc.scalar.activation(tmp[2], ps[3], ACT.Relu, bias=C("g2bk")).then_inc(A.sem, 1)
            act.wait_ge(D.sem, D.at("s"))
            for g in range(GRAPHS):
                ins = nc.scalar.activation(tok(tmp[3], g), tok(tmp[5], g), ACT.Exp, bias=col4[0][:, g:g + 1],
                                           accum_out=col4[1][:, g:g + 1])
            ins.then_inc(A.sem, 1)
            act.wait_ge(Pe.sem, Pe.at("pT"))
            nc.scalar.copy(tmp[4], ps[1]).then_inc(A.sem, 1)
            act.wait_ge(Pe.sem, Pe.at("oT"))
            nc.scalar.copy(tmp[1], ps[2]).then_inc(A.sem, 1)

        def l2gnn_dve(dve, ch, fill):
            Pe, A, D = G2
            ln_dve(dve, ch, G2, x_cur, xn, fill)
            fill(4)
            ch.link(nc.vector.tensor_scalar(tmp[6], adj_row, -1.0, NEG, ALU.add, ALU.mult))
            fill(14)
            dve.wait_ge(Pe.sem, Pe.at("s"))
            ch.link(nc.vector.tensor_tensor(tmp[5], ps[4], adj_row, ALU.mult))
            ch.link(nc.vector.tensor_tensor(tmp[5], tmp[5], tmp[6], ALU.add))
            nc.vector.tensor_reduce(col4[0], v4(tmp[5]), AXX, ALU.max, negate=True).then_inc(D.sem, 1)
            fill(3)
            dve.wait_ge(A.sem, A.at("exp"))
            ch.link(nc.vector.reciprocal(col4[2], col4[1]))
            nc.vector.tensor_tensor(v4(tmp[3]), v4(tmp[3]), col4[2].unsqueeze(2).to_broadcast([P, GRAPHS, P]),
                                    ALU.mult).then_inc(D.sem, 1)
            fill(14)
            dve.wait_ge(Pe.sem, Pe.at("y"))
            nc.vector.scalar_tensor_tensor(x_cur, ps[3], 0.0, x_cur, ALU.max, ALU.add).then_inc(D.sem, 1)
            dve.wait_ge(D.sem, D.at("x"))

        qpk = [tmp[0], tmp[1]]

        def search_pe(pe):
            Pe, A, D = PK
            ln_pe(pe, PK)
            pe.wait_ge(A.sem, A.at("xnT"))

            def queries(b):
                if b >= 2:
                    pe.wait_ge(A.sem, A.at(("q", b - 2)))
                mm(ps[b % 2], chunk(W("pkq"), b), xnT, True, True).then_inc(Pe.sem, 1)

            for b in range(8):
                queries(b)
                pe.wait_ge(A.sem, A.at(("q", b)))
                if b >= 1:
                    pe.wait_ge(A.sem, A.at(("sim", b - 1)))
                for g in range(GRAPHS):
                    for hh in range(2):
                        part = slice(hh * DK, (hh + 1) * DK)
                        ins = mm(chunk(ps[2 + hh], g), tok(qpk[b % 2], g)[part, :],
                                 chunk(W("keys"), b)[part, :], True, True)
                        if g == GRAPHS - 1:
                            ins.then_inc(Pe.sem, 1)

        def search_act(act, ch):
            Pe, A, D = PK
            ln_act(act, PK)
            xnT_act(act, PK)
            for b in range(8):
                act.wait_ge(Pe.sem, Pe.at(("q", b)))
                nc.scalar.copy(qpk[b % 2], ps[b % 2]).then_inc(A.sem, 1)
                if b >= 2:
                    act.wait_ge(D.sem, D.at(("top", b - 2)))
                for hh in range(2):
                    act.wait_ge(Pe.sem, Pe.at(("sim", b, hh)))
                    ins = nc.scalar.copy(simb[:, b % 2, 4 * hh:4 * hh + 4, :], v4(ps[2 + hh]))
                ins.then_inc(A.sem, 1)

        def search2_act(act, tail):
            Pe, A, D = PK
            for g in range(GRAPHS):
                if tail:
                    l3experts_act(act, (2 * g, 2 * g + 1))
                act.wait_ge(D.sem, D.at(("gap", g)))
                w = chunk(wgt_new, g, PER_TILE)
                nc.scalar.activation(w, w, ACT.Exp).then_inc(A.sem, 1)

        def search_dve(dve, ch, fill):
            Pe, A, D = PK
            ln_dve(dve, ch, PK, x_cur, xn, fill)
            fill(8)
            for b in range(8):
                p, hp = b // 4, b % 4
                dve.wait_ge(A.sem, A.at(("sim", b)))
                units = [(hh * 4 + g, g, hp * 2 + hh) for g in range(GRAPHS) for hh in range(2)]
                src = simb[:, b % 2]
                for u, g, h in units:
                    ins = nc.vector.max(score[:, g, p, h, 0:8], src[:, u, :])
                ch.link(ins)
                for u, g, h in units:
                    ins = nc.vector.match_replace(simr[:, u, :], score[:, g, p, h, 0:8], src[:, u, :], LOW)
                fill(3)
                ch.link(ins)
                for u, g, h in units:
                    ins = nc.vector.max(score[:, g, p, h, 8:16], simr[:, u, :])
                fill(3)
                ch.link(ins)
                for u, g, h in units:
                    nc.vector.max_index(place[:, g, p, h, 0:8], score[:, g, p, h, 0:8], src[:, u, :])
                fill(3)
                for u, g, h in units:
                    ins = nc.vector.max_index(place[:, g, p, h, 8:16], score[:, g, p, h, 8:16], simr[:, u, :])
                ins.then_inc(D.sem, 1)
                fill(3)
            dve.wait_ge(D.sem, D.at(("top", 7)))

        def search2_dve(dve, ch, fill, tail):
            Pe, A, D = PK
            nc.vector.tensor_copy(placef[:, :, 0], place[:, :, 0])
            ch.link(nc.vector.tensor_scalar(placef[:, :, 1], place[:, :, 1], float(NUM_KEYS), None, ALU.mult))
            for g in range(GRAPHS):
                for src, dst in ((score, cand), (placef, code)):
                    a, c = src[:, g, 0], src[:, g, 1]
                    for i in range(5):
                        n, o = ROW_LEN[i], ROW_OFF[i]
                        nc.vector.tensor_tensor(dst[:, :, o:o + n], a[:, :, i:i + 1].to_broadcast([P, HEADS, n]),
                                                c[:, :, 0:n], ALU.add)
                    o = ROW_OFF[5]
                    nc.vector.tensor_tensor(dst[:, :, o:o + 6].rearrange("p h (i j) -> p h i j", i=3),
                                            a[:, :, 5:8].unsqueeze(3).to_broadcast([P, HEADS, 3, 2]),
                                            c[:, :, 0:2].unsqueeze(2).to_broadcast([P, HEADS, 3, 2]), ALU.add)
                    o = ROW_OFF[8]
                    ins = nc.vector.tensor_tensor(dst[:, :, o:o + 8], a[:, :, 8:16],
                                                  c[:, :, 0:1].to_broadcast([P, HEADS, 8]), ALU.add)
                ch.link(ins)
                fill(2)
                nc.vector.tensor_tensor(code, code, rank_code.unsqueeze(1).to_broadcast([P, HEADS, CAND]), ALU.add)
                for h in range(HEADS):
                    ins = nc.vector.max(fscore[:, h, 0:8], cand[:, h, :])
                ch.link(ins)
                for h in range(HEADS):
                    ins = nc.vector.match_replace(candr[:, h, :], fscore[:, h, 0:8], cand[:, h, :], LOW)
                ch.link(ins)
                for h in range(HEADS):
                    ins = nc.vector.max(fscore[:, h, 8:16], candr[:, h, :])
                ch.link(ins)
                fill(2)
                nc.vector.tensor_tensor(chunk(wgt_new, g, PER_TILE).rearrange("p (h k) -> p h k", h=HEADS), fscore,
                                        fscore[:, :, 0:1].to_broadcast([P, HEADS, TOPK]), ALU.subtract)\
                    .then_inc(D.sem, 1)
                for h in range(HEADS):
                    nc.vector.max_index(pos[:, h, 0:8], fscore[:, h, 0:8], cand[:, h, :])
                    ins = nc.vector.max_index(pos[:, h, 8:16], fscore[:, h, 8:16], candr[:, h, :])
                ch.link(ins)
                fill(2)
                ch.link(nc.vector.tensor_scalar(posf, pos, float(CODE), None, ALU.mult))
                for q in range(HEADS // 2):
                    hs = slice(2 * q, 2 * q + 2)
                    ch.link(nc.vector.tensor_tensor(look, code[:, hs].unsqueeze(2).to_broadcast([P, 2, TOPK, CAND]),
                                                    posf[:, hs].unsqueeze(3).to_broadcast([P, 2, TOPK, CAND]),
                                                    ALU.subtract))
                    ch.link(nc.vector.tensor_reduce(fidx[:, hs], look, AXX, ALU.min, apply_absolute_value=True))
                    fill(3)
                    if tail and q % 2 == 1:
                        l3expert_dve(dve, 2 * g + q // 2)
                nc.vector.tensor_tensor(chunk(idx_new, g, PER_TILE).rearrange("p (h k) -> p h k", h=HEADS), fidx,
                                        head_base.unsqueeze(2).to_broadcast([P, HEADS, TOPK]), ALU.add)\
                    .then_inc(D.sem, 1)
                w = chunk(wgt_new, g, PER_TILE).rearrange("p (h k) -> p h k", h=HEADS)
                dve.wait_ge(A.sem, A.at(("w", g)))
                ch.link(nc.vector.tensor_reduce(wsum, w, AXX, ALU.add))
                ch.link(nc.vector.reciprocal(wsum, wsum))
                ch.link(nc.vector.tensor_tensor(w, w, wsum.unsqueeze(2).to_broadcast([P, HEADS, TOPK]), ALU.mult))

        def gather_pool(pool):
            for n in range(GRAPHS * PER_TILE):
                t, k, h = n // PER_TILE, n % PER_TILE // HEADS, n % HEADS
                if n >= RING:
                    pool.wait_ge(sums_done, n - RING + 1)
                c = t * PER_TILE + h * TOPK + k
                pool.indirect_dma_start(ring[:, n % RING, :], None, table_d,
                                        bass.IndirectOffsetOnAxis(idx_cur[:, c:c + 1], 0))\
                    .then_inc(ring_full[n % RING], 16)
            pool.wait_ge(sums_done, GRAPHS * PER_TILE)
            pool.dma_reset(range(ring_full[0].num, ring_full[-1].num + 1))

        def sum_dve(dve, n, old):
            t, k, h = n // PER_TILE, n % PER_TILE // HEADS, n % HEADS
            c = t * PER_TILE + h * TOPK + k
            w = wgt_cur[:, c:c + 1]
            acc = kv[:, t % 2, h, :]
            dve.wait_ge(ring_full[n % RING], 16 * (n // RING + 1))
            if k == 0:
                reader = t - 2 + old
                if reader >= 0 and t >= 1:
                    dve.wait_ge(AT[0].sem, AT[0].at("o1", reader))
                nc.vector.tensor_scalar(acc, ring[:, n % RING, :], w, None, ALU.mult).then_inc(sums_done, 1)
            else:
                dve.wait_ge(sums_done, n - HEADS + 1)
                nc.vector.scalar_tensor_tensor(acc, ring[:, n % RING, :], w, acc, ALU.mult, ALU.add)\
                    .then_inc(sums_done, 1)

        at_buf = [(at_q, at_k, at_s), (tmp[0], tmp[1], tmp[2])]
        at_bank = [(5, 6, 7), (1, 2, 3)]

        def attend_pe(pe, turn, t, xq, before):
            Pe, A, D = AT
            if turn >= 1:
                pe.wait_ge(D.sem, D.at("x", turn - 1))
            for steps_before, last in before:
                pe.wait_ge(steps_before.sem, steps_before.at(last))
            for f in range(2):
                q, k, _ = at_bank[f]
                for j in range(4):
                    ins = mm(chunk(ps[q], j), chunk(W("wq"), 4 * f + j), xq, True, True)
                ins.then_inc(Pe.sem, 1)
            if t is not None:
                pe.wait_ge(sums_done, (t + 1) * PER_TILE)
            slot = GRAPHS - 1 if t is None else t
            for f in range(2):
                for j in range(4):
                    ins = nc.tensor.transpose(chunk(ps[at_bank[f][1]], j), kv[:, slot % 2, 4 * f + j, 0:P], ident)
                ins.then_inc(Pe.sem, 1)
            for f in range(2):
                q, k, _ = at_buf[f]
                pe.wait_ge(A.sem, A.at(f"k{f}", turn))
                for j in range(4):
                    ins = mm(chunk(ps[at_bank[f][2]], j), chunk(q, j), chunk(k, j), True, True)
                ins.then_inc(Pe.sem, 1)
            for f in range(2):
                pe.wait_ge(D.sem, D.at(f"p{f}", turn))
                for j in range(4):
                    ins = nc.tensor.transpose(chunk(ps[at_bank[f][0]], j), chunk(at_buf[f][2], j), ident)
                ins.then_inc(Pe.sem, 1)
            for f in range(2):
                pe.wait_ge(A.sem, A.at(f"pT{f}", turn))
                for j in range(4):
                    ins = mm(chunk(ps[at_bank[f][1]], j), kv[:, slot % 2, 4 * f + j, P:2 * P], chunk(at_buf[f][0], j),
                             True, True)
                ins.then_inc(Pe.sem, 1)
            for f in range(2):
                pe.wait_ge(A.sem, A.at(f"o{f}", turn))
                for j in range(4):
                    h = 4 * f + j
                    ins = mm(ps[7][:, 0:P], chunk(at_buf[f][1], j), chunk(W("wo"), h), h == 0, h == HEADS - 1)
            ins.then_inc(Pe.sem, 1)

        def attend_act(act, turn):
            Pe, A, D = AT
            for f in range(2):
                act.wait_ge(Pe.sem, Pe.at(f"q{f}", turn))
                nc.scalar.mul(at_buf[f][0], ps[at_bank[f][0]], float(P) ** -0.5).then_inc(A.sem, 1)
            for f in range(2):
                act.wait_ge(Pe.sem, Pe.at(f"k{f}", turn))
                nc.scalar.copy(at_buf[f][1], ps[at_bank[f][1]]).then_inc(A.sem, 1)
            for f in range(2):
                w = at_buf[f][2]
                act.wait_ge(D.sem, D.at(f"s{f}", turn))
                for j in range(4):
                    h = 4 * f + j
                    ins = nc.scalar.activation(chunk(w, j), chunk(w, j), ACT.Exp, bias=at_max[:, h:h + 1],
                                               accum_out=at_sum[:, h:h + 1])
                ins.then_inc(A.sem, 1)
            for f in range(2):
                act.wait_ge(Pe.sem, Pe.at(f"pT{f}", turn))
                nc.scalar.copy(at_buf[f][0], ps[at_bank[f][0]]).then_inc(A.sem, 1)
            for f in range(2):
                act.wait_ge(Pe.sem, Pe.at(f"o{f}", turn))
                nc.scalar.copy(at_buf[f][1], ps[at_bank[f][1]]).then_inc(A.sem, 1)

        def attend_dve(dve, ch, turn, x, fill):
            Pe, A, D = AT
            fill(12)
            for f in range(2):
                w, hs = at_buf[f][2], slice(4 * f, 4 * f + 4)
                dve.wait_ge(Pe.sem, Pe.at(f"s{f}", turn))
                ch.link(nc.vector.tensor_tensor(v4(w), v4(ps[at_bank[f][2]]),
                                                causal.unsqueeze(1).to_broadcast([P, 4, P]), ALU.add))
                nc.vector.tensor_reduce(at_max[:, hs], v4(w), AXX, ALU.max, negate=True).then_inc(D.sem, 1)
                fill(1)
            for f in range(2):
                w, hs = at_buf[f][2], slice(4 * f, 4 * f + 4)
                dve.wait_ge(A.sem, A.at(f"e{f}", turn))
                ch.link(nc.vector.reciprocal(at_sum[:, hs], at_sum[:, hs]))
                nc.vector.tensor_tensor(v4(w), v4(w), at_sum[:, hs].unsqueeze(2).to_broadcast([P, 4, P]), ALU.mult)\
                    .then_inc(D.sem, 1)
                fill(1)
            fill(12)
            dve.wait_ge(Pe.sem, Pe.at("y", turn))
            nc.vector.tensor_tensor(x, x, ps[7][:, 0:P], ALU.add).then_inc(D.sem, 1)
            dve.wait_ge(D.sem, D.at("x", turn))

        def l3gnn_pe(pe):
            Pe, A, D = G3
            ln_pe(pe, G3)
            for g in range(GRAPHS):
                ins = mm(tok(ps[1], g), tok(xn, g), tok(adjT_old, g), True, True)
            ins.then_inc(Pe.sem, 1)
            pe.wait_ge(D.sem, D.at("h"))
            for b in range(2):
                mm(ps[2 + b], chunk(W("g3w1"), b), tmp[0], True, True).then_inc(Pe.sem, 1)
            bias_row(ps[4], R("g3b2"), P)
            pe.wait_ge(A.sem, A.at("h1"))
            for g in range(GRAPHS):
                for b in range(2):
                    ins = mm(tok(ps[4], g), tok(tmp[1 + b], g), chunk(W("g3w2"), b), False,
                             g == GRAPHS - 1 and b == 1)
            ins.then_inc(Pe.sem, 1)

        def l3gnn_act(act, ch):
            Pe, A, D = G3
            ln_act(act, G3)
            xnT_act(act, G3)
            for b in range(2):
                act.wait_ge(Pe.sem, Pe.at(f"h{b}"))
                nc.scalar.activation(tmp[1 + b], ps[2 + b], ACT.Relu, bias=C("g3b1", b)).then_inc(A.sem, 1)

        def l3gnn_dve(dve, ch, fill):
            Pe, A, D = G3
            ln_dve(dve, ch, G3, x_old, xn, fill)
            fill(3)
            dve.wait_ge(A.sem, A.at("xnT"))
            dve.wait_ge(Pe.sem, Pe.at("agg"))
            nc.vector.scalar_tensor_tensor(tmp[0], xnT, eps1[:, 0:1], ps[1], ALU.mult, ALU.add)\
                .then_inc(D.sem, 1)
            fill(4)
            dve.wait_ge(Pe.sem, Pe.at("y"))
            nc.vector.tensor_tensor(x_old, x_old, ps[4], ALU.add).then_inc(D.sem, 1)
            dve.wait_ge(D.sem, D.at("x"))

        with nc.Block() as block:
            @block.sync
            def _(sp):
                sp.dma_start(cols, cols_d).then_inc(setup_in, 16)
                sp.dma_start(rows, rows_d).then_inc(setup_in, 16)
                sp.dma_start(b2, b2_d).then_inc(setup_in, 16)
                sp.dma_start(wbig, wbig_d).then_inc(setup_in, 16)
                sp.wait_ge(setup_in, 64)

            @block.gpsimd
            def _(pool):
                pool.memset(ident, 0.0)
                pool.memset(causal, 0.0).then_inc(setup_pool, 1)
                pool.wait_ge(setup_pool, 1)
                pool.affine_select(out=ident, in_=ident, compare_op=ALU.not_equal, fill=1.0, base=0,
                                   pattern=[[-1, P]], channel_multiplier=1)
                pool.affine_select(out=causal, in_=causal, compare_op=ALU.is_ge, fill=LOW, base=0,
                                   pattern=[[-1, P]], channel_multiplier=1)
                pool.iota(iota8, [[1, 8]], base=0, channel_multiplier=0, allow_small_or_imprecise_dtypes=True)
                pool.iota(rank_code, [[1, CAND]], base=0, channel_multiplier=0, allow_small_or_imprecise_dtypes=True)
                pool.iota(head_base, [[1, HEADS]], base=0, channel_multiplier=0,
                          allow_small_or_imprecise_dtypes=True)
                pool.memset(ones, 1.0)
                pool.memset(eps_col, EPS)
                pool.memset(h1pad, 0.0).then_inc(setup_pool, 1)

            @block.vector
            def _(dve):
                ch = Chain(dve, dve_chain)
                dve.wait_ge(setup_in, 64)
                dve.wait_ge(setup_pool, 2)
                ch.link(nc.vector.tensor_scalar(rank_code, rank_code, float(CODE), None, ALU.mult))
                ch.link(nc.vector.tensor_scalar(head_base, head_base, float(NUM_KV), None, ALU.mult))
                ch.link(nc.vector.tensor_scalar(eps1, C("g3eps"), 1.0, None, ALU.add))
                nc.vector.tensor_tensor(gru_bias, C("bih", 0, 2), C("bhh", 0, 2), ALU.add).then_inc(dve_end, 1)
                dve.wait_ge(act_chain, 1)
                ch.link(nc.vector.reciprocal(bn_scale, bn_scale))
                for k, name in enumerate(("bn1", "bn2")):
                    s, d = bn_scale[:, k:k + 1], bn_shift[:, k:k + 1]
                    ch.link(nc.vector.tensor_tensor(s, s, C(name, 0), ALU.mult))
                    ch.link(nc.vector.tensor_tensor(d, s, C(name, 2), ALU.mult))
                    ch.link(nc.vector.tensor_tensor(d, C(name, 1), d, ALU.subtract))

            @block.scalar
            def _(act):
                act.wait_ge(setup_in, 64)
                act.wait_ge(setup_pool, 2)
                nc.scalar.activation(bn_scale[:, 0:1], C("bn1", 3), ACT.Sqrt, bias=eps_col[:, 0:1])
                nc.scalar.activation(bn_scale[:, 1:2], C("bn2", 3), ACT.Sqrt, bias=eps_col[:, 0:1])\
                    .then_inc(act_chain, 1)
        nums = [s.num for s in sems]
        assert max(nums) - min(nums) + 1 == len(nums)
        all_sems = range(min(nums), max(nums) + 1)
        nc.all_engine_barrier(sems_to_clear=all_sems)

        x_g = x_d.rearrange("(i g) n d -> i n g d", g=GRAPHS)
        adj_g = adj_d.rearrange("(i g) n m -> i n g m", g=GRAPHS)
        out_g = out_d.rearrange("(i g) n d -> i n g d", g=GRAPHS)

        STAGES = dict(search=[(PK[2], ("top", 7))], search2=[(PK[2], ("idx", GRAPHS - 1))], l3gnn=[(G3[2], "x")],
                      l3experts=[(F3[2], "x")], l0gnn=[(G0[2], "x")], l0ffn=[(F0[2], "x")], l1gnn=[(G1[2], "x")],
                      l1ffn=[(F1[2], "x")], l2gnn=[(G2[2], "x")])

        def one_pass(i, front, gather, tail):
            parts = [(tail, "last"), (front, "l0gnn"), (front, "l0ffn"), (front, "l1gnn"), (gather, 0), (front, "l1ffn"),
                     (front, "l2gnn"), (tail, "l3gnn"), (front, "search"), (gather, 1), (tail, "l3route"),
                     (front, "search2"), (tail and not front, "l3experts"), (gather, 2), (True, "keep")]
            order = [name for on, name in parts if on]
            turns = [st for st in order if st in ("last", 0, 1, 2)]

            def attention(n):
                st, before = order[n], STAGES.get(order[n - 1], []) if n else []
                if order[n - 1] == "search2" and tail:
                    before = before + STAGES["l3experts"]
                if st == "last":
                    return turns.index(st), None, xq_last, tok(x_old, GRAPHS - 1), before
                return turns.index(st), st, tok(xnT_mid, st), tok(x_mid, st), before

            total = GRAPHS * PER_TILE if gather else 0

            with nc.Block() as block:
                @block.sync
                def _(sp):
                    if front:
                        sp.dma_start(v4(x_cur), x_g[i]).then_inc(x_in, 16)
                        sp.dma_start(v4(adj_row), adj_g[i]).then_inc(adj_in, 16)
                    if tail:
                        sp.wait_ge(F3[2].sem, F3[2].at("x"))
                        sp.dma_start(out_g[i - 2], v4(x_old)).then_inc(x_out, 16)
                        sp.wait_ge(x_out, 16)

                @block.gpsimd
                def _(pool):
                    if gather:
                        gather_pool(pool)

                @block.tensor
                def _(pe):
                    for n, st in enumerate(order):
                        if st in turns:
                            turn, t, xq, _, before = attention(n)
                            attend_pe(pe, turn, t, xq, before)
                        elif st != "keep":
                            {"l3gnn": l3gnn_pe, "l3route": l3route_pe, "l3experts": l3experts_pe,
                             "search2": l3experts_pe if tail else lambda pe: None, "l0gnn": l0gnn_pe, "l0ffn": l0ffn_pe,
                             "l1gnn": l1gnn_pe, "l1ffn": l1ffn_pe, "l2gnn": l2gnn_pe, "search": search_pe}[st](pe)

                @block.scalar
                def _(act):
                    ch = Chain(act, act_chain)
                    for st in order:
                        if st in turns:
                            attend_act(act, turns.index(st))
                        elif st == "keep":
                            if gather:
                                act.wait_ge(AT[1].sem, AT[1].at("q1", len(turns) - 1))
                                ch.link(nc.scalar.copy(xq_last, tok(xnT_mid, GRAPHS - 1)))
                            if front:
                                act.wait_ge(PK[1].sem, PK[1].at("xnT"))
                                nc.scalar.copy(xnT_mid, xnT)
                        else:
                            {"l3gnn": l3gnn_act, "l3route": l3route_act,
                             "l3experts": lambda act, ch: l3experts_act(act),
                             "search2": lambda act, ch: search2_act(act, tail), "l0gnn": l0gnn_act, "l0ffn": l0ffn_act,
                             "l1gnn": l1gnn_act, "l1ffn": l1ffn_act, "l2gnn": l2gnn_act,
                             "search": search_act}[st](act, ch)
                    act.wait_ge(dve_end, 1)
                    if gather:
                        ch.link(nc.scalar.copy(adjT_old, adjT_mid))
                    if front:
                        nc.scalar.copy(adjT_mid, adjT)

                @block.vector
                def _(dve):
                    ch = Chain(dve, dve_chain)
                    due = [0.0]
                    done = [0]
                    free = [1 if tail else 2]

                    def sums(upto):
                        while done[0] < min(total, free[0] * PER_TILE, upto):
                            sum_dve(dve, done[0], tail)
                            done[0] += 1
                        due[0] = max(due[0], done[0])

                    def fill(n):
                        due[0] += n * PACE
                        sums(int(due[0]))

                    for n, st in enumerate(order):
                        if st in turns:
                            turn, t, _, x, _ = attention(n)
                            if t is not None:
                                sums((t + 1) * PER_TILE)
                            attend_dve(dve, ch, turn, x, fill)
                            free[0] += 1
                        elif st != "keep":
                            {"l3gnn": l3gnn_dve, "l3route": l3route_dve, "l3experts": l3experts_dve,
                             "search2": lambda dve, ch, fill: search2_dve(dve, ch, fill, tail), "l0gnn": l0gnn_dve, "l0ffn": l0ffn_dve,
                             "l1gnn": l1gnn_dve, "l1ffn": l1ffn_dve, "l2gnn": l2gnn_dve,
                             "search": search_dve}[st](dve, ch, fill)
                    sums(total)
                    if tail:
                        dve.wait_ge(x_out, 16)
                    if gather:
                        ch.link(nc.vector.tensor_copy(x_old, x_mid))
                    if front:
                        nc.vector.tensor_copy(x_mid, x_cur)
                        nc.vector.tensor_copy(idx_cur, idx_new)
                        nc.vector.tensor_copy(wgt_cur, wgt_new)
                    nc.vector.tensor_copy(rstd, std).then_inc(dve_end, 1)
            nc.all_engine_barrier(sems_to_clear=all_sems)

        one_pass(0, True, False, False)
        one_pass(1, True, True, False)
        with nc.Fori(2, GROUPS) as i:
            one_pass(i, True, True, True)
        one_pass(GROUPS, False, True, True)
        one_pass(GROUPS + 1, False, False, True)


def kernel(**inputs):
    import numpy as np
    import concourse.bacc as _bacc
    from concourse.bass_utils import run_bass_kernel_spmd as _run

    a = {k: np.asarray(v) for k, v in inputs.items()}

    def rows_first(w):
        e, k, n = w.shape
        return w.reshape(e, k // P, P, n).transpose(2, 0, 1, 3).reshape(P, -1)

    def pad(v, n=P):
        return np.concatenate([v, np.zeros((n - v.shape[0],) + v.shape[1:], v.dtype)])

    wih = a["L0_gnn_w_ih"].T
    parts = dict(
        c1=a["L0_gnn_conv1_w"][:, :, 0].T, c2=a["L0_gnn_conv2_w"].transpose(1, 2, 0).reshape(P, -1),
        wse=a["L0_gnn_w_se"].T, wmsg=a["L0_gnn_w_msg"].T, wih=np.concatenate([wih[:P], wih[P:]], 1),
        whh=a["L0_gnn_w_hh"].T, f0wg=a["L0_ffn_Wg"], f0w1=a["L0_ffn_W1"].transpose(1, 0, 2).reshape(P, -1),
        f0w2=rows_first(a["L0_ffn_W2"]), g1w=a["L1_gnn_W_w"].T, g1a=a["L1_gnn_A"], f1r1=a["L1_ffn_router_w1"],
        f1r2=pad(a["L1_ffn_router_w2"]), f1w1=rows_first(a["L1_ffn_expert_w1"]),
        f1w2=rows_first(a["L1_ffn_expert_w2"]), f1w3=rows_first(a["L1_ffn_expert_w3"]),
        g2v=a["L2_gnn_Wv"], g2k=a["L2_gnn_Wk"], g2q=a["L2_gnn_Wq"], g2o=a["L2_gnn_Wo"], pkq=a["L2_ffn_Wq_pk"],
        keys=a["L2_ffn_pk_keys"].transpose(0, 2, 3, 1).reshape(2, 4, 2, DK, P).transpose(2, 3, 0, 1, 4).reshape(P, -1),
        wq=a["L2_ffn_Wq"], wo=a["L2_ffn_Wo"].reshape(HEADS, P, P).transpose(1, 0, 2).reshape(P, -1),
        g3w1=a["L3_gnn_W1"], g3w2=rows_first(a["L3_gnn_W2"][None]), f3wr=a["L3_ffn_Wr"],
        f3w1=a["L3_ffn_W1"].transpose(1, 0, 2).reshape(P, -1), f3w2=rows_first(a["L3_ffn_W2"]))
    wbig = np.concatenate([parts[n] for n, _ in WEIGHTS], 1)
    colp = dict(
        bn1=np.stack([a[f"L0_gnn_bn1_{k}"] for k in "gbmv"], 1), bn2=np.stack([a[f"L0_gnn_bn2_{k}"] for k in "gbmv"], 1),
        bih=a["L0_gnn_b_ih"].reshape(3, P).T, bhh=a["L0_gnn_b_hh"].reshape(3, P).T,
        bse=pad(a["L0_gnn_b_se"])[:, None], f0b1=a["L0_ffn_b1"].reshape(16, P).T, g1b=a["L1_gnn_W_b"][:, None],
        f1rb1=pad(a["L1_ffn_router_b1"])[:, None], f1b1=a["L1_ffn_expert_b1"].T, f1b2=a["L1_ffn_expert_b2"].T,
        g2bk=a["L2_gnn_bk"][:, None], g2bq=a["L2_gnn_bq"][:, None],
        g3eps=np.broadcast_to(a["L3_gnn_eps"][None], (P, 1)), g3b1=a["L3_gnn_b1"].reshape(2, P).T,
        lng=a["L3_ffn_ln_g"].T, lnb=a["L3_ffn_ln_b"].T, f3b1=a["L3_ffn_b1"].reshape(32, P).T,
        gateb=np.broadcast_to(a["L1_gnn_gate_b"][None], (P, 1)), gatew=np.broadcast_to(a["L1_gnn_gate_w"], (P, 256)))
    cols = np.concatenate([colp[n] for n, _ in COLS], 1)
    rowp = dict(bmsg=a["L0_gnn_b_msg"], bg=a["L0_ffn_bg"], g1b=a["L1_gnn_W_b"], rb2=a["L1_ffn_router_b2"],
                bv=a["L2_gnn_bv"], bo=a["L2_gnn_bo"], g3b2=a["L3_gnn_b2"], br=a["L3_ffn_br"])
    rows = np.concatenate([rowp[n] for n, _ in ROWS])[None]
    b2 = np.concatenate([a["L0_ffn_b2"], pad(a["L1_ffn_expert_b3"], 8), a["L3_ffn_b2"]], 1)
    table = np.concatenate([a["L2_ffn_keys_table"], a["L2_ffn_values_table"]], 1)

    nc = _bacc.Bacc("TRN2", target_bir_lowering=False, num_devices=1)
    arrays, args = {}, []
    for name, arr in (("x", a["x"]), ("adj", a["adj"]), ("table", table), ("wbig", wbig), ("cols", cols),
                      ("rows", rows), ("b2", b2)):
        arr = np.ascontiguousarray(arr)
        arrays[f"in_{name}_dram"] = arr
        args.append(nc.dram_tensor(f"in_{name}_dram", arr.shape, mybir.dt.from_np(arr.dtype),
                                   kind="ExternalInput").ap())
    args.append(nc.dram_tensor("out_0_dram", a["x"].shape, F32, kind="ExternalOutput").ap())
    build(nc, *args)
    r = _run(nc, [arrays], core_ids=[0])
    return r.results[0]["out_0_dram"]
```

```python
from contextlib import ExitStack

import concourse.bass as bass
from concourse import mybir

F32 = mybir.dt.float32
U32 = mybir.dt.uint32
ALU = mybir.AluOpType
ACT = mybir.ActivationFunctionType
AXX = mybir.AxisListType.X

P = 128
B = 64
GRAPHS = 4
T = GRAPHS * P
GROUPS = B // GRAPHS
TAPS = 17
PAD = TAPS // 2
HEADS = 8
TOPK = 16
NUM_KEYS = 128
NUM_KV = NUM_KEYS ** 2
DK = 64
RING = 24
PER_TILE = HEADS * TOPK
NEG = 9.0e15
LOW = -3.0e38
PACE = 0.8
EPS = 1e-5
HALF = TOPK // 2
CAND_RECTS = [(0, 1, 0, 16), (1, 1, 0, 8), (2, 1, 0, 5), (3, 1, 0, 4), (4, 1, 0, 3), (5, 3, 0, 2), (8, 8, 0, 1)]
CODE_RECTS = [(0, 1, 0, 8), (1, 1, 0, 4), (2, 2, 0, 2), (4, 4, 0, 1),
              (0, 1, 8, 8), (1, 1, 4, 4), (2, 1, 2, 3), (3, 1, 2, 2), (4, 1, 1, 2), (5, 3, 1, 1), (8, 8, 0, 1)]


def pairs_of(rects):
    return [(i, j) for i0, ni, j0, nj in rects for i in range(i0, i0 + ni) for j in range(j0, j0 + nj)]


CAND = len(pairs_of(CAND_RECTS))
CAND_HALF = len([1 for i, j in pairs_of(CAND_RECTS) if (i + 1) * (j + 1) <= HALF])
CODE = 2 * NUM_KV

WEIGHTS = [("c1", P), ("c2", TAPS * P), ("wse", 3), ("wmsg", P), ("wih", 6 * P), ("whh", 3 * P),
           ("f0wg", 8), ("f0w1", 8 * 256), ("f0w2", 16 * P), ("g1w", P), ("g1a", P), ("f1r1", 64), ("f1r2", 6),
           ("f1w1", 6 * P), ("f1w2", 6 * P), ("f1w3", 6 * P), ("g2v", P), ("g2k", P), ("g2q", P), ("g2o", P),
           ("pkq", 1024), ("keys", 1024), ("wq", 1024), ("wo", 1024), ("g3w1", 256), ("g3w2", 256),
           ("f3wr", 8), ("f3w1", 8 * 512), ("f3w2", 32 * P)]
COLS = [("bn1", 4), ("bn2", 4), ("bih", 3), ("bhh", 3), ("bse", 1), ("f0b1", 16), ("g1b", 1), ("f1rb1", 1),
        ("f1b1", 6), ("f1b2", 6), ("g2bk", 1), ("g2bq", 1), ("g3eps", 1), ("g3b1", 2), ("lng", 8), ("lnb", 8),
        ("f3b1", 32), ("gateb", 1), ("gatew", 256), ("rank", CAND)]
ROWS = [("bmsg", P), ("bg", 8), ("g1b", P), ("rb2", 6), ("bv", P), ("bo", P), ("g3b2", P), ("br", 8)]


def offsets(parts):
    at, out = 0, {}
    for name, n in parts:
        out[name] = (at, n)
        at += n
    return out, at


class Steps:

    def __init__(self, sem, names):
        self.sem = sem
        self.value = {n: k + 1 for k, n in enumerate(names)}
        self.count = len(names)

    def at(self, name, turn=0):
        return self.value[name] + turn * self.count


def build(nc, x_d, adj_d, table_d, wbig_d, cols_d, rows_d, b2_d, out_d):
    woff, wn = offsets(WEIGHTS)
    coff, cn = offsets(COLS)
    roff, rn = offsets(ROWS)
    with ExitStack() as ctx:
        def sb(name, shape, dt=F32):
            return ctx.enter_context(nc.sbuf_tensor(name, shape, dt))[:]

        w_first = woff["f0wg"][0]
        weights_in = ctx.enter_context(nc.semaphore("weights_in"))
        sems = []

        def sem(name):
            sems.append(ctx.enter_context(nc.semaphore(name)))
            return sems[-1]

        wbig = sb("wbig", [P, wn])
        cols = sb("cols", [P, cn])
        b2 = sb("b2", [8, 3 * P])
        ident = sb("ident", [P, P])
        causal = sb("causal", [P, P])
        iota8 = sb("iota8", [P, 8])
        head_base = sb("head_base", [P, HEADS])
        ones = sb("ones", [P, P])
        rows = sb("rows", [1, rn])
        eps_col = sb("eps_col", [P, 1])
        bn_scale = sb("bn_scale", [P, 2])
        bn_shift = sb("bn_shift", [P, 2])
        gru_bias = sb("gru_bias", [P, 2])
        eps1 = sb("eps1", [P, 1])

        def W(name, a=0, n=None):
            o, size = woff[name]
            return wbig[:, o + a:o + (size if n is None else a + n)]

        def C(name, k=0, n=1):
            return cols[:, coff[name][0] + k:coff[name][0] + k + n]

        def R(name):
            o, n = roff[name]
            return rows[:, o:o + n]

        x_cur = sb("x_cur", [P, T])
        x_mid = sb("x_mid", [P, T])
        x_old = sb("x_old", [P, T])
        adj_row = sb("adj_row", [P, T])
        adjT = sb("adjT", [P, T])
        adjT_mid = sb("adjT_mid", [P, T])
        adjT_old = sb("adjT_old", [P, T])
        xn = sb("xn", [P, T])
        xnT = sb("xnT", [P, T])
        xnT_mid = sb("xnT_mid", [P, T])
        idx_cur = sb("idx_cur", [P, GRAPHS * PER_TILE], U32)
        wgt_cur = sb("wgt_cur", [P, GRAPHS * PER_TILE])
        ring = sb("ring", [P, RING, 2 * P])
        kv = sb("kv", [P, 2, HEADS, 2 * P])
        bn_st = sb("bn_st", [P, GRAPHS, 6])
        bn_mv = sb("bn_mv", [P, GRAPHS, 2])
        std = sb("std", [P, GRAPHS])
        rstd = sb("rstd", [P, GRAPHS])
        tmps = sb("tmps", [P, 7 * T])
        tmp = [tmps[:, k * T:(k + 1) * T] for k in range(7)]
        h1pad = sb("h1pad", [P, GRAPHS, P + 2 * PAD])
        sml = [sb(f"sml{k}", [P, GRAPHS, 8]) for k in range(5)]
        idx8 = sb("idx8", [P, GRAPHS, 8], U32)
        col4 = [sb(f"col4{k}", [P, GRAPHS]) for k in range(4)]
        expert_wT = sb("expert_wT", [8, T])
        coord, coord_sq, sq_row, coord_m2 = tmp[5][0:3, :], tmp[4][0:3, :], tmp[6][0:1, :], expert_wT[0:3, :]
        simb = sb("simb", [P, 2, 8, P])
        simr = tmps[:, 2 * T:4 * T].rearrange("p (u k) -> p u k", u=8)
        score = sb("score", [P, GRAPHS, 2, HEADS, TOPK])
        place = sb("place", [P, GRAPHS, 2, HEADS, TOPK], U32)
        placef = place.bitcast(F32)
        cand, code = (tmp[k][:, 0:HEADS * CAND].rearrange("p (h c) -> p h c", h=HEADS) for k in (4, 5))
        fscore, pos, posf, fidx = (tmp[6][:, k * PER_TILE:(k + 1) * PER_TILE].rearrange("p (h k) -> p h k", h=HEADS)
                                   for k in range(4))
        pos = pos.bitcast(U32)
        wsum = sb("wsum", [P, 2 * HEADS])
        simb_flat = simb.rearrange("p a b c -> p (a b c)")
        at_look = HEADS // 2 * HALF * CAND
        look_best = simb_flat[:, 0:HEADS * HALF * CAND_HALF].rearrange("p (h k c) -> p h k c", h=HEADS, k=HALF)
        look_rest = simb_flat[:, 0:at_look].rearrange("p (h k c) -> p h k c", h=HEADS // 2, k=HALF)
        candr = simb_flat[:, at_look:at_look + HEADS * CAND].rearrange("p (h c) -> p h c", h=HEADS)
        at_q = sb("at_q", [P, T])
        at_k = sb("at_k", [P, T])
        at_s = sb("at_s", [P, T])
        at_max = sb("at_max", [P, HEADS])
        at_sum = sb("at_sum", [P, HEADS])
        xq_last = sb("xq_last", [P, P])

        ps = [ctx.enter_context(nc.psum_tensor(f"ps{k}", [P, 512], F32))[:] for k in range(8)]

        setup_in = sem("setup_in")
        setup_pool = sem("setup_pool")
        x_in = sem("x_in")
        adj_in = sem("adj_in")
        x_out = sem("x_out")
        dve_chain = sem("dve_chain")
        act_chain = sem("act_chain")
        ring_full = [sem(f"ring_full{k}") for k in range(RING)]
        sums_done = sem("sums_done")

        def steps(stage, pe, act, dve):
            return tuple(Steps(sem(f"{stage}_{e}"), n) for e, n in (("pe", pe), ("act", act), ("dve", dve)))

        LN_P, LN_A, LN_D = ["xnT"], ["std", "xnT"], ["var", "xn"]
        G0 = steps("l0gnn", ["adjT", *LN_P, "h1", "s", "sq", "conv", "dist", "msg", "nmp", "gh", "r", "z", "gi", "o"],
                   ["adjT", *LN_A, "h1", "s", "sq", "xconv", "exp", "msg", "nmp", "r", "z", "n"],
                   [*LN_D, "s2", "conv", "A", "pre_n", "o", "x"])

        def blocks_of(experts, blocks):
            return [(e, b) for e in range(experts) for b in range(blocks)]

        def moe_steps(stage, route_pe, route_act, route_dve, experts, blocks, layers):
            ks = blocks_of(experts, blocks)
            normed = stage == "l3ffn"
            pe = [("route", r) for r in route_pe] + ["wT", "b"]
            pe += pe_order(ks) if layers == 2 else pe_order_3layers(experts)
            act = [("route", r) for r in route_act] + ["wT"]
            act += [("act", *k) for k in ks] if layers == 2 else act_order_3layers(experts)
            dve = [("route", r) for r in route_dve] + ["w"] + [("xe", 0), ("xe", 1)] * normed + ["b"]
            dve += dve_order(experts, normed)
            return steps(stage, [*LN_P, *pe], [*LN_A, *act], [*LN_D, *dve])

        def pe_order(ks):
            out = []
            for n in range(len(ks) + 1):
                if n < len(ks):
                    out.append(("h", *ks[n]))
                if n >= 1:
                    out.append(("acc", *ks[n - 1]))
            return out

        def pe_order_3layers(experts):
            out = []
            for n in range(experts + 2):
                if n < experts:
                    out.append(("h1", n))
                if 1 <= n <= experts:
                    out.append(("h2", n - 1))
                if n >= 2:
                    out.append(("acc", n - 2, 0))
            return out

        def act_order_3layers(experts):
            out = []
            for n in range(experts + 1):
                if n < experts:
                    out.append(("act1", n))
                if n >= 1:
                    out.append(("act", n - 1, 0))
            return out

        def dve_order(experts, normed):
            out = []
            for e in range(experts):
                out += [x_of(e, experts)] + [("xe", e + 2)] * (normed and e + 2 < experts)
            return out

        def x_of(e, experts):
            return ("x", e) if e < experts - 1 else "x"

        F0 = moe_steps("l0ffn", ["gate"], [], [], 8, 2, 2)
        F1 = moe_steps("l1ffn", ["rh", "gate"], ["rh", "exp", "exp2"], ["max", "gap"], 6, 1, 3)
        F3 = moe_steps("l3ffn", ["gate", "xn2T"], ["exp", "std2", "xn2T"], ["max", "var2", "xn2"], 8, 4, 2)
        G1 = steps("l1gnn", [*LN_P, "hT", "h", "hA", "e", "hp"], [*LN_A, "hT", "h", "hA", "exp", "hp", "coeff"],
                   [*LN_D, "e", "att", "logit", "x"])
        G2 = steps("l2gnn", [*LN_P, "v", "q", "k", "s", "pT", "oT", "y"], [*LN_A, "v", "q", "k", "exp", "pT", "oT"],
                   [*LN_D, "s", "p", "x"])
        blk = range(8)
        PK = steps("search", [*LN_P, *[n for b in blk for n in (("q", b), ("sim", b, 0), ("sim", b, 1))]],
                   [*LN_A, *[n for b in blk for n in (("q", b), ("sim", b))]],
                   [*LN_D, *[("top", b) for b in blk], "num"])
        EARLY = steps("early", [], ["w"], [(n, g) for g in (0, 1) for n in ("gap", "idx")])
        LATE = steps("late", [], [("w", 2), ("w", 3)], [(n, g) for g in (2, 3) for n in ("gap", "idx")])
        AT = steps("attend", ["q0", "q1", "k0", "k1", "s0", "s1", "pT0", "pT1", "o0", "o1", "y"],
                   ["q0", "q1", "k0", "k1", "e0", "e1", "pT0", "pT1", "o0", "o1"],
                   ["s0", "s1", "p0", "p1", "x"])
        G3 = steps("l3gnn", [*LN_P, "agg", "h0", "h1", "y"], [*LN_A, "h0", "h1"], [*LN_D, "h", "x"])

        def v4(ap):
            return ap.rearrange("p (g d) -> p g d", g=GRAPHS)

        def tok(ap, g):
            return ap[:, g * P:(g + 1) * P]

        class Chain:

            def __init__(self, eng, s):
                self.eng, self.sem, self.n = eng, s, 0

            def link(self, ins):
                ins.then_inc(self.sem, 1)
                self.n += 1
                self.eng.wait_ge(self.sem, self.n)

        def ln_dve(dve, ch, S, x, out, fill):
            Pe, A, D = S
            for g in range(GRAPHS):
                ins = nc.vector.bn_stats(bn_st[:, g, :], tok(x, g))
            ch.link(ins)
            for g in range(GRAPHS):
                ins = nc.vector.bn_aggr(bn_mv[:, g, :], bn_st[:, g, :])
            ins.then_inc(D.sem, 1)
            fill(4)
            dve.wait_ge(A.sem, A.at("std"))
            ch.link(nc.vector.reciprocal(rstd, std))
            for g in range(GRAPHS):
                ins = nc.vector.tensor_scalar(tok(out, g), tok(x, g), bn_mv[:, g, 0:1], rstd[:, g:g + 1],
                                              ALU.subtract, ALU.mult)
            ins.then_inc(D.sem, 1)
            dve.wait_ge(D.sem, D.at("xn"))

        def ln_act(act, S, var="var"):
            Pe, A, D = S
            act.wait_ge(D.sem, D.at(var))
            nc.scalar.activation(std, bn_mv[:, :, 1], ACT.Sqrt, bias=eps_col[:, 0:1]).then_inc(A.sem, 1)

        def xnT_act(act, S, to=xnT):
            Pe, A, D = S
            act.wait_ge(Pe.sem, Pe.at("xnT"))
            nc.scalar.copy(to, ps[0]).then_inc(A.sem, 1)

        def ln_pe(pe, S):
            Pe, A, D = S
            pe.wait_ge(D.sem, D.at("xn"))
            for g in range(GRAPHS):
                ins = nc.tensor.transpose(tok(ps[0], g), tok(xn, g), ident)
            ins.then_inc(Pe.sem, 1)

        def mm(out, lhsT, rhs, start, stop):
            return nc.tensor.matmul(out, lhsT, rhs, start=start, stop=stop, skip_group_check=True)

        def bias_row(out, row, n):
            return mm(out, ones[0:1, :], row.unsqueeze(1).to_broadcast([1, GRAPHS, n]), True, False)

        def chunk(ap, k, n=P):
            return ap[:, k * n:(k + 1) * n]

        def l0gnn_pe(pe):
            Pe, A, D = G0
            pe.wait_ge(adj_in, 16)
            for g in range(GRAPHS):
                ins = nc.tensor.transpose(tok(ps[1], g), tok(adj_row, g), ident)
            ins.then_inc(Pe.sem, 1)
            ln_pe(pe, G0)
            pe.wait_ge(A.sem, A.at("xnT"))
            mm(ps[1], W("c1"), xnT, True, True).then_inc(Pe.sem, 1)
            mm(ps[3][0:3, :], W("wse"), xnT, True, True).then_inc(Pe.sem, 1)
            pe.wait_ge(D.sem, D.at("s2"))
            mm(ps[4][0:1, :], ones[0:3, 0:1], coord_sq, True, True).then_inc(Pe.sem, 1)
            pe.wait_ge(A.sem, A.at("h1"))
            for k in range(TAPS):
                ins = mm(ps[2], chunk(W("c2"), k), h1pad[:, :, k:k + P], k == 0, k == TAPS - 1)
            ins.then_inc(Pe.sem, 1)
            pe.wait_ge(A.sem, A.at("sq"))
            for g in range(GRAPHS):
                mm(tok(ps[0], g), tok(sq_row, g), ones[0:1, :], True, False)
                mm(tok(ps[0], g), ones[0:1, :], tok(sq_row, g), False, False)
                ins = mm(tok(ps[0], g), tok(coord_m2, g), tok(coord, g), False, True)
            ins.then_inc(Pe.sem, 1)
            bias_row(ps[1], R("bmsg"), P)
            for g in range(GRAPHS):
                ins = mm(tok(ps[1], g), tok(xnT, g), W("wmsg"), False, g == GRAPHS - 1)
            ins.then_inc(Pe.sem, 1)
            pe.wait_ge(D.sem, D.at("A"))
            pe.wait_ge(A.sem, A.at("msg"))
            for g in range(GRAPHS):
                ins = mm(tok(ps[3], g), tok(tmp[2], g), tok(tmp[1], g), True, True)
            ins.then_inc(Pe.sem, 1)
            mm(ps[4], chunk(W("whh"), 2), xnT, True, True).then_inc(Pe.sem, 1)
            pe.wait_ge(A.sem, A.at("nmp"))
            for k, bank in enumerate((0, 1, 2)):
                mm(ps[bank], chunk(W("wih"), k), tmp[0], True, False)
                ins = mm(ps[bank], chunk(W("wih"), 3 + k), tmp[3], False, k == 2)
                if k < 2:
                    ins = mm(ps[bank], chunk(W("whh"), k), xnT, False, True)
                ins.then_inc(Pe.sem, 1)
            pe.wait_ge(D.sem, D.at("o"))
            for g in range(GRAPHS):
                ins = nc.tensor.transpose(tok(ps[3], g), tok(tmp[4], g), ident)
            ins.then_inc(Pe.sem, 1)

        def l0gnn_act(act, ch):
            Pe, A, D = G0
            act.wait_ge(Pe.sem, Pe.at("adjT"))
            nc.scalar.copy(adjT, ps[1]).then_inc(A.sem, 1)
            ln_act(act, G0)
            xnT_act(act, G0)
            act.wait_ge(Pe.sem, Pe.at("h1"))
            nc.scalar.activation(h1pad[:, :, PAD:PAD + P], v4(ps[1]), ACT.Relu, bias=bn_shift[:, 0:1],
                                 scale=bn_scale[:, 0:1]).then_inc(A.sem, 1)
            act.wait_ge(Pe.sem, Pe.at("s"))
            nc.scalar.activation(coord, ps[3][0:3, :], ACT.Identity, bias=C("bse")[0:3, :]).then_inc(A.sem, 1)
            act.wait_ge(Pe.sem, Pe.at("sq"))
            nc.scalar.copy(sq_row, ps[4][0:1, :]).then_inc(A.sem, 1)
            act.wait_ge(D.sem, D.at("conv"))
            nc.scalar.activation(tmp[0], tmp[0], ACT.Relu, bias=bn_shift[:, 1:2]).then_inc(A.sem, 1)
            act.wait_ge(Pe.sem, Pe.at("dist"))
            nc.scalar.activation(tmp[1], ps[0], ACT.Exp, scale=-1.0).then_inc(A.sem, 1)
            act.wait_ge(Pe.sem, Pe.at("msg"))
            nc.scalar.activation(tmp[2], ps[1], ACT.Relu).then_inc(A.sem, 1)
            act.wait_ge(Pe.sem, Pe.at("nmp"))
            nc.scalar.copy(tmp[3], ps[3]).then_inc(A.sem, 1)
            for k, name in enumerate("rz"):
                act.wait_ge(Pe.sem, Pe.at(name))
                nc.scalar.activation(tmp[4 + k], ps[k], ACT.Sigmoid, bias=gru_bias[:, k:k + 1])\
                    .then_inc(A.sem, 1)
            act.wait_ge(D.sem, D.at("pre_n"))
            nc.scalar.activation(tmp[6], tmp[6], ACT.Tanh, bias=C("bih", 2)).then_inc(A.sem, 1)

        def l0gnn_dve(dve, ch, fill):
            Pe, A, D = G0
            dve.wait_ge(x_in, 16)
            ln_dve(dve, ch, G0, x_cur, xn, fill)
            fill(6)
            dve.wait_ge(A.sem, A.at("s"))
            nc.vector.tensor_scalar(coord_m2, coord, -2.0, None, ALU.mult)
            nc.vector.tensor_tensor(coord_sq, coord, coord, ALU.mult).then_inc(D.sem, 1)
            fill(18)
            dve.wait_ge(Pe.sem, Pe.at("conv"))
            nc.vector.scalar_tensor_tensor(tmp[0], ps[2], bn_scale[:, 1:2], xnT, ALU.mult, ALU.add)\
                .then_inc(D.sem, 1)
            fill(9)
            dve.wait_ge(A.sem, A.at("exp"))
            nc.vector.tensor_tensor(tmp[1], tmp[1], adjT, ALU.mult).then_inc(D.sem, 1)
            fill(12)
            dve.wait_ge(A.sem, A.at("r"))
            dve.wait_ge(Pe.sem, Pe.at("gh"))
            ch.link(nc.vector.scalar_tensor_tensor(tmp[6], ps[4], C("bhh", 2), tmp[4], ALU.add, ALU.mult))
            dve.wait_ge(Pe.sem, Pe.at("gi"))
            nc.vector.tensor_tensor(tmp[6], ps[2], tmp[6], ALU.add).then_inc(D.sem, 1)
            fill(10)
            dve.wait_ge(A.sem, A.at("n"))
            ch.link(nc.vector.tensor_tensor(tmp[4], xnT, tmp[6], ALU.subtract))
            ch.link(nc.vector.tensor_tensor(tmp[4], tmp[5], tmp[4], ALU.mult))
            nc.vector.tensor_tensor(tmp[4], tmp[4], tmp[6], ALU.add).then_inc(D.sem, 1)
            fill(4)
            dve.wait_ge(Pe.sem, Pe.at("o"))
            nc.vector.tensor_tensor(x_cur, x_cur, ps[3], ALU.add).then_inc(D.sem, 1)
            dve.wait_ge(D.sem, D.at("x"))

        def gate_pe(w, n, row):
            mm(ps[1][:, 0:GRAPHS * n], ones[0:1, :], row.unsqueeze(1).to_broadcast([1, GRAPHS, n]), True, False)
            for g in range(GRAPHS):
                ins = mm(ps[1][:, g * n:(g + 1) * n], w(g)[0], w(g)[1], False, g == GRAPHS - 1)
            return ins

        def wT_pe(pe, S):
            Pe, A, D = S
            pe.wait_ge(D.sem, D.at("w"))
            for g in range(GRAPHS):
                ins = nc.tensor.transpose(tok(ps[2][0:8, :], g), sml[4][:, g, :], ident)
            ins.then_inc(Pe.sem, 1)
            pe.wait_ge(A.sem, A.at("wT"))

        def wT_act(act, S):
            Pe, A, D = S
            act.wait_ge(Pe.sem, Pe.at("wT"))
            nc.scalar.copy(expert_wT, ps[2][0:8, :]).then_inc(A.sem, 1)

        def bias_pe(pe, S, which, experts):
            Pe, A, D = S
            for g in range(GRAPHS):
                ins = mm(tok(ps[4], g), tok(expert_wT[0:experts, :], g), b2[0:experts, which * P:(which + 1) * P],
                         True, True)
            ins.then_inc(Pe.sem, 1)

        def acc_pe(pe, S, e, b, blocks, hidden, w2, experts):
            Pe, A, D = S
            pe.wait_ge(A.sem, A.at(("act", e, b)))
            if b == 0 and e >= 2:
                pe.wait_ge(D.sem, D.at(x_of(e - 2, experts)))
            for g in range(GRAPHS):
                ins = mm(tok(ps[2 + e % 2], g), tok(hidden, g), w2, b == 0 and g == 0, b == blocks - 1)
            ins.then_inc(Pe.sem, 1)

        def experts_pe(pe, S, experts, blocks, w1, w2, hidden, rhs):
            Pe, A, D = S
            ks = blocks_of(experts, blocks)
            for kind, e, b in pe_order(ks):
                n = ks.index((e, b))
                if kind == "h":
                    if n >= 2:
                        pe.wait_ge(A.sem, A.at(("act", *ks[n - 2])))
                    if rhs is not None and b == 0:
                        pe.wait_ge(D.sem, D.at(("xe", e)))
                    mm(ps[n % 2], chunk(w1, n), xnT if rhs is None else rhs[e % 2], True, True)\
                        .then_inc(Pe.sem, 1)
                else:
                    acc_pe(pe, S, e, b, blocks, hidden[n % 3], chunk(w2, n), experts)

        def experts_act(act, S, experts, blocks, bias, hidden, some=None):
            Pe, A, D = S
            ks = blocks_of(experts, blocks)
            for n, (e, b) in enumerate(ks):
                if some is not None and e not in some:
                    continue
                act.wait_ge(Pe.sem, Pe.at(("h", e, b)))
                if n >= 3:
                    act.wait_ge(Pe.sem, Pe.at(("acc", *ks[n - 3])))
                nc.scalar.activation(hidden[n % 3], ps[n % 2], ACT.Gelu, bias=C(bias, n)).then_inc(A.sem, 1)

        def expert_dve(dve, S, e, experts, blocks, x, xe=None, xT=None):
            Pe, A, D = S
            if e == 0:
                dve.wait_ge(Pe.sem, Pe.at("b"))
                nc.vector.tensor_tensor(x, x, ps[4], ALU.add).then_inc(D.sem, 1)
            dve.wait_ge(Pe.sem, Pe.at(("acc", e, blocks - 1)))
            dve.wait_ge(D.sem, D.at(x_of(e - 1, experts)) if e else D.at("b"))
            for g in range(GRAPHS):
                ins = nc.vector.scalar_tensor_tensor(tok(x, g), tok(ps[2 + e % 2], g), sml[4][:, g, e:e + 1],
                                                     tok(x, g), ALU.mult, ALU.add)
            ins.then_inc(D.sem, 1)
            if xe is not None and e + 2 < experts:
                expert_in_dve(dve, S, e + 2, blocks, xe, xT)

        def expert_in_dve(dve, S, e, blocks, xe, xT):
            Pe, A, D = S
            if e >= 2:
                dve.wait_ge(Pe.sem, Pe.at(("h", e - 2, blocks - 1)))
            nc.vector.tensor_scalar(xe[e % 2], xT, C("lng", e), C("lnb", e), ALU.mult, ALU.add)\
                .then_inc(D.sem, 1)

        def top2_dve(dve, ch, scores):
            for g in range(GRAPHS):
                ins = nc.vector.max(sml[1][:, g, :], scores[:, g, :])
            ch.link(ins)
            for g in range(GRAPHS):
                ins = nc.vector.max_index(idx8[:, g, :], sml[1][:, g, :], scores[:, g, :])
            ch.link(ins)
            ch.link(nc.vector.tensor_copy(sml[4], idx8))
            it = iota8.unsqueeze(1).to_broadcast([P, GRAPHS, 8])
            nc.vector.tensor_tensor(sml[2], sml[4][:, :, 0:1].to_broadcast([P, GRAPHS, 8]), it, ALU.is_equal)
            ch.link(nc.vector.tensor_tensor(sml[3], sml[4][:, :, 1:2].to_broadcast([P, GRAPHS, 8]), it, ALU.is_equal))

        def b8(ap):
            return ap.unsqueeze(2).to_broadcast([P, GRAPHS, 8])

        def l0ffn_pe(pe):
            Pe, A, D = F0
            ln_pe(pe, F0)
            pe.wait_ge(A.sem, A.at("xnT"))
            gate_pe(lambda g: (tok(xnT, g), W("f0wg")), 8, R("bg")).then_inc(Pe.sem, 1)
            wT_pe(pe, F0)
            bias_pe(pe, F0, 0, 8)
            experts_pe(pe, F0, 8, 2, W("f0w1"), W("f0w2"), tmp, None)

        def l0ffn_act(act, ch, late):
            ln_act(act, F0)
            xnT_act(act, F0)
            wT_act(act, F0)
            experts_act(act, F0, 8, 2, "f0b1", tmp)
            if late:
                weights_act(act, LATE, 2)

        def l0ffn_dve(dve, ch, fill, late):
            Pe, A, D = F0
            ln_dve(dve, ch, F0, x_cur, xn, fill)
            fill(8)
            dve.wait_ge(Pe.sem, Pe.at(("route", "gate")))
            ch.link(nc.vector.tensor_copy(sml[0], ps[1][:, 0:32].rearrange("p (g e) -> p g e", g=GRAPHS)))
            top2_dve(dve, ch, sml[0])
            nc.vector.tensor_tensor(sml[4], sml[2], sml[3], ALU.add).then_inc(D.sem, 1)
            if late:
                def experts_step(s):
                    if s == 0:
                        fill(4)
                    for e in (2 * s, 2 * s + 1):
                        expert_dve(dve, F0, e, 8, 2, x_cur)

                lookup_dve(dve, ch, fill, 2, LATE, experts_step)
                weights_dve(dve, ch, LATE, 2, 1)
            else:
                for e in range(8):
                    expert_dve(dve, F0, e, 8, 2, x_cur)
            dve.wait_ge(D.sem, D.at("x"))

        def l1ffn_pe(pe):
            Pe, A, D = F1
            ln_pe(pe, F1)
            pe.wait_ge(A.sem, A.at("xnT"))
            mm(ps[3][0:64, :], W("f1r1"), xnT, True, True).then_inc(Pe.sem, 1)
            pe.wait_ge(A.sem, A.at(("route", "rh")))
            gate_pe(lambda g: (tok(tmp[3][0:64, :], g), W("f1r2")[0:64, :]), 6, R("rb2")).then_inc(Pe.sem, 1)
            wT_pe(pe, F1)
            bias_pe(pe, F1, 1, 6)
            for item in pe_order_3layers(6):
                e = item[1]
                if item[0] == "h1":
                    if e >= 1:
                        pe.wait_ge(A.sem, A.at(("act1", e - 1)))
                    mm(ps[0], chunk(W("f1w1"), e), xnT, True, True).then_inc(Pe.sem, 1)
                elif item[0] == "h2":
                    pe.wait_ge(A.sem, A.at(("act1", e)))
                    if e >= 1:
                        pe.wait_ge(A.sem, A.at(("act", e - 1, 0)))
                    mm(ps[1], chunk(W("f1w2"), e), tmp[2 + e % 2], True, True).then_inc(Pe.sem, 1)
                else:
                    acc_pe(pe, F1, e, 0, 1, tmp[e % 2], chunk(W("f1w3"), e), 6)

        def l1ffn_act(act, ch, late):
            Pe, A, D = F1
            ln_act(act, F1)
            xnT_act(act, F1)
            act.wait_ge(Pe.sem, Pe.at(("route", "rh")))
            nc.scalar.activation(tmp[3][0:64, :], ps[3][0:64, :], ACT.Relu, bias=C("f1rb1")[0:64, :])\
                .then_inc(A.sem, 1)
            act.wait_ge(D.sem, D.at(("route", "max")))
            nc.scalar.activation(sml[1][:, :, 0:6], sml[1][:, :, 0:6], ACT.Exp).then_inc(A.sem, 1)
            act.wait_ge(D.sem, D.at(("route", "gap")))
            nc.scalar.activation(col4[1], col4[0], ACT.Exp).then_inc(A.sem, 1)
            wT_act(act, F1)
            for item in act_order_3layers(6):
                e = item[1]
                if item[0] == "act1":
                    act.wait_ge(Pe.sem, Pe.at(("h1", e)))
                    if e >= 2:
                        act.wait_ge(Pe.sem, Pe.at(("h2", e - 2)))
                    nc.scalar.activation(tmp[2 + e % 2], ps[0], ACT.Relu, bias=C("f1b1", e)).then_inc(A.sem, 1)
                else:
                    act.wait_ge(Pe.sem, Pe.at(("h2", e)))
                    if e >= 2:
                        act.wait_ge(Pe.sem, Pe.at(("acc", e - 2, 0)))
                    nc.scalar.activation(tmp[e % 2], ps[1], ACT.Relu, bias=C("f1b2", e)).then_inc(A.sem, 1)
            if late:
                weights_act(act, LATE, 3)

        def softmax6_dve(dve, ch, S, n, bank):
            Pe, A, D = S
            lg = bank[:, 0:GRAPHS * n].rearrange("p (g e) -> p g e", g=GRAPHS)
            nc.vector.memset(sml[0], -1.0)
            ch.link(nc.vector.tensor_reduce(col4[0], lg, AXX, ALU.max))
            nc.vector.tensor_tensor(sml[1][:, :, 0:n], lg, col4[0].unsqueeze(2).to_broadcast([P, GRAPHS, n]),
                                    ALU.subtract).then_inc(D.sem, 1)
            dve.wait_ge(A.sem, A.at(("route", "exp")))
            ch.link(nc.vector.tensor_reduce(col4[1], sml[1][:, :, 0:n], AXX, ALU.add))
            ch.link(nc.vector.reciprocal(col4[2], col4[1]))
            ch.link(nc.vector.tensor_tensor(sml[0][:, :, 0:n], sml[1][:, :, 0:n],
                                            col4[2].unsqueeze(2).to_broadcast([P, GRAPHS, n]), ALU.mult))

        def l1ffn_dve(dve, ch, fill, late):
            Pe, A, D = F1
            ln_dve(dve, ch, F1, x_cur, xn, fill)
            fill(8)
            dve.wait_ge(Pe.sem, Pe.at(("route", "gate")))
            softmax6_dve(dve, ch, F1, 6, ps[1])
            top2_dve(dve, ch, sml[0])
            nc.vector.tensor_tensor(col4[0], sml[1][:, :, 1], sml[1][:, :, 0], ALU.subtract).then_inc(D.sem, 1)
            dve.wait_ge(A.sem, A.at(("route", "exp2")))
            ch.link(nc.vector.tensor_scalar(col4[2], col4[1], 1.0, None, ALU.add))
            ch.link(nc.vector.reciprocal(col4[3], col4[2]))
            ch.link(nc.vector.tensor_tensor(col4[1], col4[1], col4[3], ALU.mult))
            nc.vector.tensor_tensor(sml[2], sml[2], b8(col4[3]), ALU.mult)
            ch.link(nc.vector.tensor_tensor(sml[3], sml[3], b8(col4[1]), ALU.mult))
            nc.vector.tensor_tensor(sml[4], sml[2], sml[3], ALU.add).then_inc(D.sem, 1)
            if late:
                def experts_step(s):
                    if s == 0:
                        fill(10)
                    for e in ((0, 1), (2, 3), (4,), (5,))[s]:
                        expert_dve(dve, F1, e, 6, 1, x_cur)

                lookup_dve(dve, ch, fill, 3, LATE, experts_step)
                weights_dve(dve, ch, LATE, 3, 1)
            else:
                for e in range(6):
                    expert_dve(dve, F1, e, 6, 1, x_cur)
            dve.wait_ge(D.sem, D.at("x"))

        l3T, l3_hidden, l3_in = tmp[3], [tmp[0], tmp[1], at_s], [at_q, at_k]

        def l3route_pe(pe):
            Pe, A, D = F3
            ln_pe(pe, F3)
            pe.wait_ge(A.sem, A.at("xnT"))
            gate_pe(lambda g: (tok(l3T, g), W("f3wr")), 8, R("br")).then_inc(Pe.sem, 1)
            pe.wait_ge(D.sem, D.at(("route", "xn2")))
            for g in range(GRAPHS):
                ins = nc.tensor.transpose(tok(ps[3], g), tok(tmp[5], g), ident)
            ins.then_inc(Pe.sem, 1)
            wT_pe(pe, F3)

        def l3experts_pe(pe):
            bias_pe(pe, F3, 2, 8)
            experts_pe(pe, F3, 8, 4, W("f3w1"), W("f3w2"), l3_hidden, l3_in)

        def l3route_act(act, ch):
            Pe, A, D = F3
            ln_act(act, F3)
            xnT_act(act, F3, l3T)
            act.wait_ge(D.sem, D.at(("route", "max")))
            nc.scalar.activation(sml[1], sml[1], ACT.Exp).then_inc(A.sem, 1)
            act.wait_ge(D.sem, D.at(("route", "var2")))
            nc.scalar.activation(std, bn_mv[:, :, 1], ACT.Sqrt, bias=eps_col[:, 0:1]).then_inc(A.sem, 1)
            act.wait_ge(Pe.sem, Pe.at(("route", "xn2T")))
            nc.scalar.copy(l3T, ps[3]).then_inc(A.sem, 1)
            wT_act(act, F3)

        def l3experts_act(act, some=None):
            experts_act(act, F3, 8, 4, "f3b1", l3_hidden, some)

        def l3route_dve(dve, ch, fill):
            Pe, A, D = F3
            ln_dve(dve, ch, F3, x_old, xn, fill)
            fill(4)
            dve.wait_ge(Pe.sem, Pe.at(("route", "gate")))
            softmax6_dve(dve, ch, F3, 8, ps[1])
            top2_dve(dve, ch, sml[0])
            fill(5)
            for g in range(GRAPHS):
                ins = nc.vector.bn_stats(bn_st[:, g, :], tok(xn, g))
            ch.link(ins)
            for g in range(GRAPHS):
                ins = nc.vector.bn_aggr(bn_mv[:, g, :], bn_st[:, g, :])
            ins.then_inc(D.sem, 1)
            ch.link(nc.vector.tensor_tensor(col4[0], sml[1][:, :, 0], sml[1][:, :, 1], ALU.add))
            ch.link(nc.vector.reciprocal(col4[1], col4[0]))
            ch.link(nc.vector.tensor_tensor(col4[2], sml[1][:, :, 0], col4[1], ALU.mult))
            ch.link(nc.vector.tensor_tensor(col4[3], sml[1][:, :, 1], col4[1], ALU.mult))
            dve.wait_ge(A.sem, A.at(("route", "std2")))
            ch.link(nc.vector.reciprocal(rstd, std))
            for g in range(GRAPHS):
                ins = nc.vector.tensor_scalar(tok(tmp[5], g), tok(xn, g), bn_mv[:, g, 0:1], rstd[:, g:g + 1],
                                              ALU.subtract, ALU.mult)
            ins.then_inc(D.sem, 1)
            fill(3)
            nc.vector.tensor_tensor(sml[2], sml[2], b8(col4[2]), ALU.mult)
            ch.link(nc.vector.tensor_tensor(sml[3], sml[3], b8(col4[3]), ALU.mult))
            nc.vector.tensor_tensor(sml[4], sml[2], sml[3], ALU.add).then_inc(D.sem, 1)
            fill(4)
            dve.wait_ge(A.sem, A.at(("route", "xn2T")))
            for e in range(2):
                expert_in_dve(dve, F3, e, 4, l3_in, l3T)

        def l3expert_dve(dve, e):
            expert_dve(dve, F3, e, 8, 4, x_old, l3_in, l3T)

        def l3experts_dve(dve, ch, fill):
            for e in range(8):
                fill(6.8)
                l3expert_dve(dve, e)

        def l1gnn_pe(pe):
            Pe, A, D = G1
            ln_pe(pe, G1)
            pe.wait_ge(A.sem, A.at("xnT"))
            mm(ps[1], W("g1w"), xnT, True, True).then_inc(Pe.sem, 1)
            bias_row(ps[2], R("g1b"), P)
            for g in range(GRAPHS):
                ins = mm(tok(ps[2], g), tok(xnT, g), W("g1w"), False, g == GRAPHS - 1)
            ins.then_inc(Pe.sem, 1)
            pe.wait_ge(A.sem, A.at("hT"))
            mm(ps[3], W("g1a"), tmp[0], True, True).then_inc(Pe.sem, 1)
            pe.wait_ge(A.sem, A.at("hA"))
            for g in range(GRAPHS):
                mm(tok(ps[4], g), tok(tmp[2], g), tok(tmp[0], g), True, False)
                ins = mm(tok(ps[4], g), tok(tmp[0], g), tok(tmp[2], g), False, True)
            ins.then_inc(Pe.sem, 1)
            pe.wait_ge(D.sem, D.at("att"))
            for g in range(GRAPHS):
                ins = mm(tok(ps[1], g), tok(tmp[3], g), tok(tmp[1], g), True, True)
            ins.then_inc(Pe.sem, 1)

        def l1gnn_act(act, ch):
            Pe, A, D = G1
            ln_act(act, G1)
            xnT_act(act, G1)
            act.wait_ge(Pe.sem, Pe.at("hT"))
            nc.scalar.activation(tmp[0], ps[1], ACT.Identity, bias=C("g1b")).then_inc(A.sem, 1)
            act.wait_ge(Pe.sem, Pe.at("h"))
            nc.scalar.copy(tmp[1], ps[2]).then_inc(A.sem, 1)
            act.wait_ge(Pe.sem, Pe.at("hA"))
            nc.scalar.copy(tmp[2], ps[3]).then_inc(A.sem, 1)
            act.wait_ge(D.sem, D.at("e"))
            for g in range(GRAPHS):
                ins = nc.scalar.activation(tok(tmp[3], g), tok(tmp[4], g), ACT.Exp, bias=col4[0][:, g:g + 1],
                                           accum_out=col4[1][:, g:g + 1])
            ins.then_inc(A.sem, 1)
            act.wait_ge(Pe.sem, Pe.at("hp"))
            nc.scalar.activation(tmp[5], ps[1], ACT.Relu).then_inc(A.sem, 1)
            act.wait_ge(D.sem, D.at("logit"))
            nc.scalar.activation(col4[3], col4[2], ACT.Sigmoid, bias=C("gateb")).then_inc(A.sem, 1)

        def l1gnn_dve(dve, ch, fill):
            Pe, A, D = G1
            ln_dve(dve, ch, G1, x_cur, xn, fill)
            fill(4)
            ch.link(nc.vector.tensor_scalar(tmp[6], adjT, 0.0, None, ALU.is_gt))
            ch.link(nc.vector.tensor_scalar(tmp[5], tmp[6], -1.0, NEG, ALU.add, ALU.mult))
            fill(18)
            dve.wait_ge(Pe.sem, Pe.at("e"))
            ch.link(nc.vector.tensor_tensor(tmp[4], ps[4], tmp[6], ALU.mult))
            ch.link(nc.vector.tensor_tensor(tmp[4], tmp[4], tmp[5], ALU.add))
            nc.vector.tensor_reduce(col4[0], v4(tmp[4]), AXX, ALU.max, negate=True).then_inc(D.sem, 1)
            fill(7)
            dve.wait_ge(A.sem, A.at("exp"))
            ch.link(nc.vector.reciprocal(col4[2], col4[1]))
            for g in range(GRAPHS):
                ins = nc.vector.scalar_tensor_tensor(tok(tmp[3], g), tok(tmp[3], g), col4[2][:, g:g + 1],
                                                     tok(adjT, g), ALU.mult, ALU.mult)
            ins.then_inc(D.sem, 1)
            gw = C("gatew", 0, 256)
            ch.link(nc.vector.tensor_tensor(v4(tmp[6]), v4(xn), gw[:, 0:P].unsqueeze(1).to_broadcast([P, GRAPHS, P]),
                                            ALU.mult))
            dve.wait_ge(A.sem, A.at("hp"))
            ch.link(nc.vector.tensor_tensor(v4(tmp[4]), v4(tmp[5]),
                                            gw[:, P:2 * P].unsqueeze(1).to_broadcast([P, GRAPHS, P]), ALU.mult))
            ch.link(nc.vector.tensor_tensor(tmp[4], tmp[4], tmp[6], ALU.add))
            nc.vector.tensor_reduce(col4[2], v4(tmp[4]), AXX, ALU.add).then_inc(D.sem, 1)
            ch.link(nc.vector.tensor_tensor(tmp[6], xn, tmp[5], ALU.subtract))
            fill(7)
            dve.wait_ge(A.sem, A.at("coeff"))
            for g in range(GRAPHS):
                ins = nc.vector.scalar_tensor_tensor(tok(tmp[6], g), tok(tmp[6], g), col4[3][:, g:g + 1],
                                                     tok(tmp[5], g), ALU.mult, ALU.add)
            ch.link(ins)
            nc.vector.tensor_tensor(x_cur, x_cur, tmp[6], ALU.add).then_inc(D.sem, 1)
            dve.wait_ge(D.sem, D.at("x"))

        def l2gnn_pe(pe):
            Pe, A, D = G2
            ln_pe(pe, G2)
            pe.wait_ge(A.sem, A.at("xnT"))
            bias_row(ps[1], R("bv"), P)
            for g in range(GRAPHS):
                ins = mm(tok(ps[1], g), tok(xnT, g), W("g2v"), False, g == GRAPHS - 1)
            ins.then_inc(Pe.sem, 1)
            mm(ps[2], W("g2q"), xnT, True, True).then_inc(Pe.sem, 1)
            mm(ps[3], W("g2k"), xnT, True, True).then_inc(Pe.sem, 1)
            pe.wait_ge(A.sem, A.at("k"))
            for g in range(GRAPHS):
                ins = mm(tok(ps[4], g), tok(tmp[1], g), tok(tmp[2], g), True, True)
            ins.then_inc(Pe.sem, 1)
            pe.wait_ge(D.sem, D.at("p"))
            for g in range(GRAPHS):
                ins = nc.tensor.transpose(tok(ps[1], g), tok(tmp[3], g), ident)
            ins.then_inc(Pe.sem, 1)
            pe.wait_ge(A.sem, A.at("pT"))
            for g in range(GRAPHS):
                ins = mm(tok(ps[2], g), tok(tmp[0], g), tok(tmp[4], g), True, True)
            ins.then_inc(Pe.sem, 1)
            bias_row(ps[3], R("bo"), P)
            pe.wait_ge(A.sem, A.at("oT"))
            for g in range(GRAPHS):
                ins = mm(tok(ps[3], g), tok(tmp[1], g), W("g2o"), False, g == GRAPHS - 1)
            ins.then_inc(Pe.sem, 1)

        def l2gnn_act(act, ch):
            Pe, A, D = G2
            ln_act(act, G2)
            xnT_act(act, G2)
            act.wait_ge(Pe.sem, Pe.at("v"))
            nc.scalar.activation(tmp[0], ps[1], ACT.Relu).then_inc(A.sem, 1)
            act.wait_ge(Pe.sem, Pe.at("q"))
            nc.scalar.activation(tmp[1], ps[2], ACT.Relu, bias=C("g2bq")).then_inc(A.sem, 1)
            act.wait_ge(Pe.sem, Pe.at("k"))
            nc.scalar.activation(tmp[2], ps[3], ACT.Relu, bias=C("g2bk")).then_inc(A.sem, 1)
            act.wait_ge(D.sem, D.at("s"))
            for g in range(GRAPHS):
                ins = nc.scalar.activation(tok(tmp[3], g), tok(tmp[5], g), ACT.Exp, bias=col4[0][:, g:g + 1],
                                           accum_out=col4[1][:, g:g + 1])
            ins.then_inc(A.sem, 1)
            act.wait_ge(Pe.sem, Pe.at("pT"))
            nc.scalar.copy(tmp[4], ps[1]).then_inc(A.sem, 1)
            act.wait_ge(Pe.sem, Pe.at("oT"))
            nc.scalar.copy(tmp[1], ps[2]).then_inc(A.sem, 1)

        def l2gnn_dve(dve, ch, fill):
            Pe, A, D = G2
            ln_dve(dve, ch, G2, x_cur, xn, fill)
            fill(4)
            ch.link(nc.vector.tensor_scalar(tmp[6], adj_row, -1.0, NEG, ALU.add, ALU.mult))
            fill(18)
            dve.wait_ge(Pe.sem, Pe.at("s"))
            ch.link(nc.vector.tensor_tensor(tmp[5], ps[4], adj_row, ALU.mult))
            ch.link(nc.vector.tensor_tensor(tmp[5], tmp[5], tmp[6], ALU.add))
            nc.vector.tensor_reduce(col4[0], v4(tmp[5]), AXX, ALU.max, negate=True).then_inc(D.sem, 1)
            fill(6)
            dve.wait_ge(A.sem, A.at("exp"))
            ch.link(nc.vector.reciprocal(col4[2], col4[1]))
            nc.vector.tensor_tensor(v4(tmp[3]), v4(tmp[3]), col4[2].unsqueeze(2).to_broadcast([P, GRAPHS, P]),
                                    ALU.mult).then_inc(D.sem, 1)
            fill(14)
            dve.wait_ge(Pe.sem, Pe.at("y"))
            nc.vector.scalar_tensor_tensor(x_cur, ps[3], 0.0, x_cur, ALU.max, ALU.add).then_inc(D.sem, 1)
            dve.wait_ge(D.sem, D.at("x"))

        qpk = [tmp[0], tmp[1]]

        def search_pe(pe):
            Pe, A, D = PK
            ln_pe(pe, PK)
            pe.wait_ge(A.sem, A.at("xnT"))

            def queries(b):
                if b >= 2:
                    pe.wait_ge(A.sem, A.at(("q", b - 2)))
                mm(ps[b % 2], chunk(W("pkq"), b), xnT, True, True).then_inc(Pe.sem, 1)

            for b in range(8):
                queries(b)
                pe.wait_ge(A.sem, A.at(("q", b)))
                if b >= 1:
                    pe.wait_ge(A.sem, A.at(("sim", b - 1)))
                for g in range(GRAPHS):
                    for hh in range(2):
                        part = slice(hh * DK, (hh + 1) * DK)
                        ins = mm(chunk(ps[2 + hh], g), tok(qpk[b % 2], g)[part, :],
                                 chunk(W("keys"), b)[part, :], True, True)
                        if g == GRAPHS - 1:
                            ins.then_inc(Pe.sem, 1)

        def search_act(act, ch):
            Pe, A, D = PK
            ln_act(act, PK)
            xnT_act(act, PK)
            for b in range(8):
                act.wait_ge(Pe.sem, Pe.at(("q", b)))
                nc.scalar.copy(qpk[b % 2], ps[b % 2]).then_inc(A.sem, 1)
                if b >= 2:
                    act.wait_ge(D.sem, D.at(("top", b - 2)))
                for hh in range(2):
                    act.wait_ge(Pe.sem, Pe.at(("sim", b, hh)))
                    ins = nc.scalar.copy(simb[:, b % 2, 4 * hh:4 * hh + 4, :], v4(ps[2 + hh]))
                ins.then_inc(A.sem, 1)

        def weights_act(act, S, g, graphs=1):
            Pe, A, D = S
            act.wait_ge(D.sem, D.at(("gap", g)))
            w = wgt_cur[:, (g + 1 - graphs) * PER_TILE:(g + 1) * PER_TILE]
            nc.scalar.activation(w, w, ACT.Exp).then_inc(A.sem, 1)

        def early_act(act, tail):
            if tail:
                l3experts_act(act)
            weights_act(act, EARLY, 1, 2)

        def search_dve(dve, ch, fill):
            Pe, A, D = PK
            ln_dve(dve, ch, PK, x_cur, xn, fill)
            fill(8)
            for b in range(8):
                p, hp = b // 4, b % 4
                dve.wait_ge(A.sem, A.at(("sim", b)))
                units = [(hh * 4 + g, g, hp * 2 + hh) for g in range(GRAPHS) for hh in range(2)]
                src = simb[:, b % 2]
                for u, g, h in units:
                    ins = nc.vector.max(score[:, g, p, h, 0:8], src[:, u, :])
                ch.link(ins)
                for u, g, h in units:
                    ins = nc.vector.match_replace(simr[:, u, :], score[:, g, p, h, 0:8], src[:, u, :], LOW)
                fill(5)
                ch.link(ins)
                for u, g, h in units:
                    ins = nc.vector.max(score[:, g, p, h, 8:16], simr[:, u, :])
                fill(3)
                ch.link(ins)
                for u, g, h in units:
                    nc.vector.max_index(place[:, g, p, h, 0:8], score[:, g, p, h, 0:8], src[:, u, :])
                fill(3)
                for u, g, h in units:
                    ins = nc.vector.max_index(place[:, g, p, h, 8:16], score[:, g, p, h, 8:16], simr[:, u, :])
                ins.then_inc(D.sem, 1)
                fill(3)
            dve.wait_ge(D.sem, D.at(("top", 7)))

        def sums_of_pairs(dst, rects, a, c):
            o = 0
            for i, ni, j, nj in rects:
                ins = nc.vector.tensor_tensor(dst[:, :, o:o + ni * nj].rearrange("p h (i j) -> p h i j", i=ni),
                                              a[:, :, i:i + ni].unsqueeze(3).to_broadcast([P, HEADS, ni, nj]),
                                              c[:, :, j:j + nj].unsqueeze(2).to_broadcast([P, HEADS, ni, nj]),
                                              ALU.add)
                o += ni * nj
            return ins

        def lookup_dve(dve, ch, fill, g, S, between=lambda s: None):
            Pe, A, D = S
            sums_of_pairs(cand, CAND_RECTS, score[:, g, 0], score[:, g, 1])
            ch.link(sums_of_pairs(code, CODE_RECTS, placef[:, g, 0], placef[:, g, 1]))
            fill(5)
            nc.vector.tensor_tensor(code, code, C("rank", 0, CAND).unsqueeze(1).to_broadcast([P, HEADS, CAND]),
                                    ALU.add)
            for h in range(HEADS):
                ins = nc.vector.max(fscore[:, h, 0:8], cand[:, h, :])
            ch.link(ins)
            for h in range(HEADS):
                ins = nc.vector.match_replace(candr[:, h, :], fscore[:, h, 0:8], cand[:, h, :], LOW)
            ch.link(ins)
            for h in range(HEADS):
                ins = nc.vector.max(fscore[:, h, 8:16], candr[:, h, :])
            ch.link(ins)
            fill(5)
            nc.vector.tensor_tensor(chunk(wgt_cur, g, PER_TILE).rearrange("p (h k) -> p h k", h=HEADS), fscore,
                                    fscore[:, :, 0:1].to_broadcast([P, HEADS, TOPK]), ALU.subtract)\
                .then_inc(D.sem, 1)
            between(0)
            for h in range(HEADS):
                nc.vector.max_index(pos[:, h, 0:8], fscore[:, h, 0:8], cand[:, h, :])
                ins = nc.vector.max_index(pos[:, h, 8:16], fscore[:, h, 8:16], candr[:, h, :])
            ch.link(ins)
            fill(7)
            ch.link(nc.vector.tensor_scalar(posf, pos, float(CODE), None, ALU.mult))
            everyone, first, second = slice(0, HEADS), slice(0, HEADS // 2), slice(HEADS // 2, HEADS)
            for s, (hs, ks, look, n) in enumerate(((everyone, slice(0, HALF), look_best, CAND_HALF),
                                                   (first, slice(HALF, TOPK), look_rest, CAND),
                                                   (second, slice(HALF, TOPK), look_rest, CAND))):
                shape = [P, hs.stop - hs.start, HALF, n]
                ch.link(nc.vector.tensor_tensor(look, code[:, hs, 0:n].unsqueeze(2).to_broadcast(shape),
                                                posf[:, hs, ks].unsqueeze(3).to_broadcast(shape), ALU.subtract))
                fill(3)
                ch.link(nc.vector.tensor_reduce(fidx[:, hs, ks], look, AXX, ALU.min, apply_absolute_value=True))
                fill(4)
                between(s + 1)
            nc.vector.tensor_tensor(chunk(idx_cur, g, PER_TILE).rearrange("p (h k) -> p h k", h=HEADS), fidx,
                                    head_base.unsqueeze(2).to_broadcast([P, HEADS, TOPK]), ALU.add)\
                .then_inc(D.sem, 1)

        def weights_dve(dve, ch, S, g, graphs):
            Pe, A, D = S
            w = wgt_cur[:, (g + 1 - graphs) * PER_TILE:(g + 1) * PER_TILE].rearrange("p (h k) -> p h k", k=TOPK)
            total = wsum[:, 0:graphs * HEADS]
            dve.wait_ge(A.sem, A.at("w" if graphs == 2 else ("w", g)))
            ch.link(nc.vector.tensor_reduce(total, w, AXX, ALU.add))
            ch.link(nc.vector.reciprocal(total, total))
            ch.link(nc.vector.tensor_tensor(w, w, total.unsqueeze(2).to_broadcast([P, graphs * HEADS, TOPK]), ALU.mult))

        def early_dve(dve, ch, fill, gather, tail):
            Pe, A, D = PK
            if gather:
                dve.wait_ge(sums_done, 2 * PER_TILE)
            nc.vector.tensor_copy(placef[:, :, 0], place[:, :, 0])
            nc.vector.tensor_scalar(placef[:, :, 1], place[:, :, 1], float(NUM_KEYS), None, ALU.mult)\
                .then_inc(D.sem, 1)
            dve.wait_ge(D.sem, D.at("num"))
            for g in (0, 1):
                def experts_step(s):
                    if tail:
                        fill(1)
                        l3expert_dve(dve, 4 * g + s)

                lookup_dve(dve, ch, fill, g, EARLY, experts_step)
            weights_dve(dve, ch, EARLY, 1, 2)

        def late_act(act, ch):
            for g in (2, 3):
                weights_act(act, LATE, g)

        def late_dve(dve, ch, fill):
            for g in (2, 3):
                lookup_dve(dve, ch, fill, g, LATE)
                weights_dve(dve, ch, LATE, g, 1)

        def gather_pool(pool):
            for n in range(GRAPHS * PER_TILE):
                t, k, h = n // PER_TILE, n % PER_TILE // HEADS, n % HEADS
                if n % PER_TILE == 0 and t >= 2:
                    pool.wait_ge(LATE[2].sem, LATE[2].at(("idx", t)))
                if n >= RING:
                    pool.wait_ge(sums_done, n - RING + 1)
                c = t * PER_TILE + h * TOPK + k
                pool.indirect_dma_start(ring[:, n % RING, :], None, table_d,
                                        bass.IndirectOffsetOnAxis(idx_cur[:, c:c + 1], 0))\
                    .then_inc(ring_full[n % RING], 16)
            pool.wait_ge(sums_done, GRAPHS * PER_TILE)
            pool.dma_reset(range(ring_full[0].num, ring_full[-1].num + 1))

        def sum_dve(dve, n, old):
            t, k, h = n // PER_TILE, n % PER_TILE // HEADS, n % HEADS
            c = t * PER_TILE + h * TOPK + k
            w = wgt_cur[:, c:c + 1]
            acc = kv[:, t % 2, h, :]
            dve.wait_ge(ring_full[n % RING], 16 * (n // RING + 1))
            if k == 0:
                reader = t - 2 + old
                if reader >= 0 and t >= 1:
                    dve.wait_ge(AT[0].sem, AT[0].at("o1", reader))
                nc.vector.tensor_scalar(acc, ring[:, n % RING, :], w, None, ALU.mult).then_inc(sums_done, 1)
            else:
                dve.wait_ge(sums_done, n - HEADS + 1)
                nc.vector.scalar_tensor_tensor(acc, ring[:, n % RING, :], w, acc, ALU.mult, ALU.add)\
                    .then_inc(sums_done, 1)

        at_buf = [(at_q, at_k, at_s), (tmp[0], tmp[1], tmp[2])]
        at_bank = [(5, 6, 7), (1, 2, 3)]

        def attend_pe(pe, turn, t, xq, before):
            Pe, A, D = AT
            if turn >= 1:
                pe.wait_ge(D.sem, D.at("x", turn - 1))
            for steps_before, last in before:
                pe.wait_ge(steps_before.sem, steps_before.at(last))
            for f in range(2):
                q, k, _ = at_bank[f]
                for j in range(4):
                    ins = mm(chunk(ps[q], j), chunk(W("wq"), 4 * f + j), xq, True, True)
                ins.then_inc(Pe.sem, 1)
            if t is not None:
                pe.wait_ge(sums_done, (t + 1) * PER_TILE)
            slot = GRAPHS - 1 if t is None else t
            for f in range(2):
                for j in range(4):
                    ins = nc.tensor.transpose(chunk(ps[at_bank[f][1]], j), kv[:, slot % 2, 4 * f + j, 0:P], ident)
                ins.then_inc(Pe.sem, 1)
            for f in range(2):
                q, k, _ = at_buf[f]
                pe.wait_ge(A.sem, A.at(f"k{f}", turn))
                for j in range(4):
                    ins = mm(chunk(ps[at_bank[f][2]], j), chunk(q, j), chunk(k, j), True, True)
                ins.then_inc(Pe.sem, 1)
            for f in range(2):
                pe.wait_ge(D.sem, D.at(f"p{f}", turn))
                for j in range(4):
                    ins = nc.tensor.transpose(chunk(ps[at_bank[f][0]], j), chunk(at_buf[f][2], j), ident)
                ins.then_inc(Pe.sem, 1)
            for f in range(2):
                pe.wait_ge(A.sem, A.at(f"pT{f}", turn))
                for j in range(4):
                    ins = mm(chunk(ps[at_bank[f][1]], j), kv[:, slot % 2, 4 * f + j, P:2 * P], chunk(at_buf[f][0], j),
                             True, True)
                ins.then_inc(Pe.sem, 1)
            for f in range(2):
                pe.wait_ge(A.sem, A.at(f"o{f}", turn))
                for j in range(4):
                    h = 4 * f + j
                    ins = mm(ps[7][:, 0:P], chunk(at_buf[f][1], j), chunk(W("wo"), h), h == 0, h == HEADS - 1)
            ins.then_inc(Pe.sem, 1)

        def attend_act(act, turn):
            Pe, A, D = AT
            for f in range(2):
                act.wait_ge(Pe.sem, Pe.at(f"q{f}", turn))
                nc.scalar.mul(at_buf[f][0], ps[at_bank[f][0]], float(P) ** -0.5).then_inc(A.sem, 1)
            for f in range(2):
                act.wait_ge(Pe.sem, Pe.at(f"k{f}", turn))
                nc.scalar.copy(at_buf[f][1], ps[at_bank[f][1]]).then_inc(A.sem, 1)
            for f in range(2):
                w = at_buf[f][2]
                act.wait_ge(D.sem, D.at(f"s{f}", turn))
                for j in range(4):
                    h = 4 * f + j
                    ins = nc.scalar.activation(chunk(w, j), chunk(w, j), ACT.Exp, bias=at_max[:, h:h + 1],
                                               accum_out=at_sum[:, h:h + 1])
                ins.then_inc(A.sem, 1)
            for f in range(2):
                act.wait_ge(Pe.sem, Pe.at(f"pT{f}", turn))
                nc.scalar.copy(at_buf[f][0], ps[at_bank[f][0]]).then_inc(A.sem, 1)
            for f in range(2):
                act.wait_ge(Pe.sem, Pe.at(f"o{f}", turn))
                nc.scalar.copy(at_buf[f][1], ps[at_bank[f][1]]).then_inc(A.sem, 1)

        def attend_dve(dve, ch, turn, x, fill):
            Pe, A, D = AT
            fill(10)
            for f in range(2):
                w, hs = at_buf[f][2], slice(4 * f, 4 * f + 4)
                dve.wait_ge(Pe.sem, Pe.at(f"s{f}", turn))
                ch.link(nc.vector.tensor_tensor(v4(w), v4(ps[at_bank[f][2]]),
                                                causal.unsqueeze(1).to_broadcast([P, 4, P]), ALU.add))
                nc.vector.tensor_reduce(at_max[:, hs], v4(w), AXX, ALU.max, negate=True).then_inc(D.sem, 1)
                fill(1)
            for f in range(2):
                w, hs = at_buf[f][2], slice(4 * f, 4 * f + 4)
                dve.wait_ge(A.sem, A.at(f"e{f}", turn))
                ch.link(nc.vector.reciprocal(at_sum[:, hs], at_sum[:, hs]))
                nc.vector.tensor_tensor(v4(w), v4(w), at_sum[:, hs].unsqueeze(2).to_broadcast([P, 4, P]), ALU.mult)\
                    .then_inc(D.sem, 1)
                fill(1)
            fill(12)
            dve.wait_ge(Pe.sem, Pe.at("y", turn))
            nc.vector.tensor_tensor(x, x, ps[7][:, 0:P], ALU.add).then_inc(D.sem, 1)
            dve.wait_ge(D.sem, D.at("x", turn))

        def l3gnn_pe(pe):
            Pe, A, D = G3
            ln_pe(pe, G3)
            for g in range(GRAPHS):
                ins = mm(tok(ps[1], g), tok(xn, g), tok(adjT_old, g), True, True)
            ins.then_inc(Pe.sem, 1)
            pe.wait_ge(D.sem, D.at("h"))
            for b in range(2):
                mm(ps[2 + b], chunk(W("g3w1"), b), tmp[0], True, True).then_inc(Pe.sem, 1)
            bias_row(ps[4], R("g3b2"), P)
            pe.wait_ge(A.sem, A.at("h1"))
            for g in range(GRAPHS):
                for b in range(2):
                    ins = mm(tok(ps[4], g), tok(tmp[1 + b], g), chunk(W("g3w2"), b), False,
                             g == GRAPHS - 1 and b == 1)
            ins.then_inc(Pe.sem, 1)

        def l3gnn_act(act, ch):
            Pe, A, D = G3
            ln_act(act, G3)
            xnT_act(act, G3)
            for b in range(2):
                act.wait_ge(Pe.sem, Pe.at(f"h{b}"))
                nc.scalar.activation(tmp[1 + b], ps[2 + b], ACT.Relu, bias=C("g3b1", b)).then_inc(A.sem, 1)

        def l3gnn_dve(dve, ch, fill):
            Pe, A, D = G3
            ln_dve(dve, ch, G3, x_old, xn, fill)
            fill(3)
            dve.wait_ge(A.sem, A.at("xnT"))
            dve.wait_ge(Pe.sem, Pe.at("agg"))
            nc.vector.scalar_tensor_tensor(tmp[0], xnT, eps1[:, 0:1], ps[1], ALU.mult, ALU.add)\
                .then_inc(D.sem, 1)
            fill(14)
            dve.wait_ge(Pe.sem, Pe.at("y"))
            nc.vector.tensor_tensor(x_old, x_old, ps[4], ALU.add).then_inc(D.sem, 1)
            dve.wait_ge(D.sem, D.at("x"))

        with nc.Block() as block:
            @block.sync
            def _(sp):
                sp.dma_start(cols, cols_d).then_inc(setup_in, 16)
                sp.dma_start(rows, rows_d).then_inc(setup_in, 16)
                sp.dma_start(b2, b2_d).then_inc(setup_in, 16)
                sp.dma_start(wbig[:, 0:w_first], wbig_d[:, 0:w_first]).then_inc(setup_in, 16)
                sp.wait_ge(setup_in, 64)

            @block.gpsimd
            def _(pool):
                pool.memset(ident, 0.0)
                pool.memset(causal, 0.0).then_inc(setup_pool, 1)
                pool.wait_ge(setup_pool, 1)
                pool.affine_select(out=ident, in_=ident, compare_op=ALU.not_equal, fill=1.0, base=0,
                                   pattern=[[-1, P]], channel_multiplier=1)
                pool.affine_select(out=causal, in_=causal, compare_op=ALU.is_ge, fill=LOW, base=0,
                                   pattern=[[-1, P]], channel_multiplier=1)
                pool.iota(iota8, [[1, 8]], base=0, channel_multiplier=0, allow_small_or_imprecise_dtypes=True)
                pool.iota(head_base, [[1, HEADS]], base=0, channel_multiplier=0,
                          allow_small_or_imprecise_dtypes=True)
                pool.memset(ones, 1.0)
                pool.memset(eps_col, EPS)
                pool.memset(h1pad, 0.0).then_inc(setup_pool, 1)

            @block.vector
            def _(dve):
                ch = Chain(dve, dve_chain)
                dve.wait_ge(setup_in, 64)
                dve.wait_ge(setup_pool, 2)
                ch.link(nc.vector.tensor_scalar(head_base, head_base, float(NUM_KV), None, ALU.mult))
                ch.link(nc.vector.tensor_scalar(eps1, C("g3eps"), 1.0, None, ALU.add))
                nc.vector.tensor_tensor(gru_bias, C("bih", 0, 2), C("bhh", 0, 2), ALU.add)
                dve.wait_ge(act_chain, 1)
                ch.link(nc.vector.reciprocal(bn_scale, bn_scale))
                for k, name in enumerate(("bn1", "bn2")):
                    s, d = bn_scale[:, k:k + 1], bn_shift[:, k:k + 1]
                    ch.link(nc.vector.tensor_tensor(s, s, C(name, 0), ALU.mult))
                    ch.link(nc.vector.tensor_tensor(d, s, C(name, 2), ALU.mult))
                    ch.link(nc.vector.tensor_tensor(d, C(name, 1), d, ALU.subtract))

            @block.scalar
            def _(act):
                act.wait_ge(setup_in, 64)
                act.wait_ge(setup_pool, 2)
                nc.scalar.activation(bn_scale[:, 0:1], C("bn1", 3), ACT.Sqrt, bias=eps_col[:, 0:1])
                nc.scalar.activation(bn_scale[:, 1:2], C("bn2", 3), ACT.Sqrt, bias=eps_col[:, 0:1])\
                    .then_inc(act_chain, 1)
        nums = [s.num for s in sems]
        assert max(nums) - min(nums) + 1 == len(nums)
        all_sems = range(min(nums), max(nums) + 1)
        nc.all_engine_barrier(sems_to_clear=all_sems)

        x_g = x_d.rearrange("(i g) n d -> i n g d", g=GRAPHS)
        adj_g = adj_d.rearrange("(i g) n m -> i n g m", g=GRAPHS)
        out_g = out_d.rearrange("(i g) n d -> i n g d", g=GRAPHS)

        STAGES = dict(search=[(PK[2], ("top", 7))], early=[(EARLY[2], ("idx", 1))], l3gnn=[(G3[2], "x")],
                      l3experts=[(F3[2], "x")], l0gnn=[(G0[2], "x")], l0ffn=[(F0[2], "x")], l1gnn=[(G1[2], "x")],
                      l1ffn=[(F1[2], "x")], l2gnn=[(G2[2], "x")])

        def one_pass(i, front, gather, tail):
            parts = [(tail, "last"), (front, "l0gnn"), (front, "l0ffn"), (gather and not front, "late"),
                     (front, "l1gnn"), (gather, 0), (front, "l1ffn"), (front, "l2gnn"),
                     (tail, "l3gnn"), (gather, 1), (front, "search"), (gather, 2), (tail, "l3route"), (front, "early"),
                     (tail and not front, "l3experts"), (True, "keep")]
            order = [name for on, name in parts if on]
            turns = [st for st in order if st in ("last", 0, 1, 2)]

            def attention(n):
                st, before = order[n], STAGES.get(order[n - 1], []) if n else []
                if order[n - 1] == "early" and tail:
                    before = before + STAGES["l3experts"]
                if st == "last":
                    return turns.index(st), None, xq_last, tok(x_old, GRAPHS - 1), before
                return turns.index(st), st, tok(xnT_mid, st), tok(x_mid, st), before

            total = GRAPHS * PER_TILE if gather else 0

            with nc.Block() as block:
                @block.sync
                def _(sp):
                    if front:
                        sp.dma_start(v4(x_cur), x_g[i]).then_inc(x_in, 16)
                        sp.dma_start(v4(adj_row), adj_g[i]).then_inc(adj_in, 16)
                        if not gather:
                            sp.dma_start(wbig[:, w_first:], wbig_d[:, w_first:]).then_inc(weights_in, 16)
                    if tail:
                        sp.wait_ge(F3[2].sem, F3[2].at("x"))
                        sp.dma_start(out_g[i - 2], v4(x_old)).then_inc(x_out, 16)
                        sp.wait_ge(x_out, 16)

                @block.gpsimd
                def _(pool):
                    if gather:
                        gather_pool(pool)

                @block.tensor
                def _(pe):
                    for n, st in enumerate(order):
                        if st == "l0ffn" and not gather:
                            pe.wait_ge(weights_in, 16)
                        if st in turns:
                            turn, t, xq, _, before = attention(n)
                            attend_pe(pe, turn, t, xq, before)
                        elif st not in ("keep", "late") and (st != "early" or tail):
                            {"l3gnn": l3gnn_pe, "l3route": l3route_pe, "l3experts": l3experts_pe,
                             "early": l3experts_pe, "l0gnn": l0gnn_pe, "l0ffn": l0ffn_pe,
                             "l1gnn": l1gnn_pe, "l1ffn": l1ffn_pe, "l2gnn": l2gnn_pe, "search": search_pe}[st](pe)

                @block.scalar
                def _(act):
                    ch = Chain(act, act_chain)
                    for st in order:
                        if st in turns:
                            attend_act(act, turns.index(st))
                        elif st == "keep":
                            if gather:
                                act.wait_ge(AT[1].sem, AT[1].at("q1", len(turns) - 1))
                                ch.link(nc.scalar.copy(xq_last, tok(xnT_mid, GRAPHS - 1)))
                            if front:
                                act.wait_ge(PK[1].sem, PK[1].at("xnT"))
                                nc.scalar.copy(xnT_mid, xnT)
                        else:
                            {"l3gnn": l3gnn_act, "l3route": l3route_act,
                             "l3experts": lambda act, ch: l3experts_act(act),
                             "early": lambda act, ch: early_act(act, tail), "late": late_act, "l0gnn": l0gnn_act,
                             "l0ffn": lambda act, ch: l0ffn_act(act, ch, gather), "l1gnn": l1gnn_act,
                             "l1ffn": lambda act, ch: l1ffn_act(act, ch, gather), "l2gnn": l2gnn_act,
                             "search": search_act}[st](act, ch)
                    if gather:
                        ch.link(nc.scalar.copy(adjT_old, adjT_mid))
                    if front:
                        nc.scalar.copy(adjT_mid, adjT)

                @block.vector
                def _(dve):
                    ch = Chain(dve, dve_chain)
                    due = [0.0]
                    done = [0]
                    free = [1 if tail else 2]

                    def sums(upto):
                        while done[0] < min(total, free[0] * PER_TILE, upto):
                            sum_dve(dve, done[0], tail)
                            done[0] += 1
                        due[0] = max(due[0], done[0])

                    def fill(n):
                        due[0] += n * PACE
                        sums(int(due[0]))

                    for n, st in enumerate(order):
                        if st in turns:
                            turn, t, _, x, _ = attention(n)
                            if t is not None:
                                sums((t + 1) * PER_TILE)
                            attend_dve(dve, ch, turn, x, fill)
                            free[0] += 1
                        elif st != "keep":
                            {"l3gnn": l3gnn_dve, "l3route": l3route_dve, "l3experts": l3experts_dve,
                             "early": lambda dve, ch, fill: early_dve(dve, ch, fill, gather, tail), "late": late_dve,
                             "l0gnn": l0gnn_dve, "l0ffn": lambda dve, ch, fill: l0ffn_dve(dve, ch, fill, gather),
                             "l1gnn": l1gnn_dve, "l1ffn": lambda dve, ch, fill: l1ffn_dve(dve, ch, fill, gather),
                             "l2gnn": l2gnn_dve,
                             "search": search_dve}[st](dve, ch, fill)
                    sums(total)
                    if tail:
                        dve.wait_ge(x_out, 16)
                    if gather:
                        ch.link(nc.vector.tensor_copy(x_old, x_mid))
                    if front:
                        nc.vector.tensor_copy(x_mid, x_cur)
            nc.all_engine_barrier(sems_to_clear=all_sems)

        one_pass(0, True, False, False)
        one_pass(1, True, True, False)
        with nc.Fori(2, GROUPS) as i:
            one_pass(i, True, True, True)
        one_pass(GROUPS, False, True, True)
        one_pass(GROUPS + 1, False, False, True)


def kernel(**inputs):
    import numpy as np
    import concourse.bacc as _bacc
    from concourse.bass_utils import run_bass_kernel_spmd as _run

    a = {k: np.asarray(v) for k, v in inputs.items()}

    def rows_first(w):
        e, k, n = w.shape
        return w.reshape(e, k // P, P, n).transpose(2, 0, 1, 3).reshape(P, -1)

    def pad(v, n=P):
        return np.concatenate([v, np.zeros((n - v.shape[0],) + v.shape[1:], v.dtype)])

    flat = {pair: n for n, pair in enumerate(pairs_of(CAND_RECTS))}
    rank = np.array([[CODE * flat[pair] for pair in pairs_of(CODE_RECTS)]], np.float32)
    wih = a["L0_gnn_w_ih"].T
    parts = dict(
        c1=a["L0_gnn_conv1_w"][:, :, 0].T, c2=a["L0_gnn_conv2_w"].transpose(1, 2, 0).reshape(P, -1),
        wse=a["L0_gnn_w_se"].T, wmsg=a["L0_gnn_w_msg"].T, wih=np.concatenate([wih[:P], wih[P:]], 1),
        whh=a["L0_gnn_w_hh"].T, f0wg=a["L0_ffn_Wg"], f0w1=a["L0_ffn_W1"].transpose(1, 0, 2).reshape(P, -1),
        f0w2=rows_first(a["L0_ffn_W2"]), g1w=a["L1_gnn_W_w"].T, g1a=a["L1_gnn_A"], f1r1=a["L1_ffn_router_w1"],
        f1r2=pad(a["L1_ffn_router_w2"]), f1w1=rows_first(a["L1_ffn_expert_w1"]),
        f1w2=rows_first(a["L1_ffn_expert_w2"]), f1w3=rows_first(a["L1_ffn_expert_w3"]),
        g2v=a["L2_gnn_Wv"], g2k=a["L2_gnn_Wk"], g2q=a["L2_gnn_Wq"], g2o=a["L2_gnn_Wo"], pkq=a["L2_ffn_Wq_pk"],
        keys=a["L2_ffn_pk_keys"].transpose(0, 2, 3, 1).reshape(2, 4, 2, DK, P).transpose(2, 3, 0, 1, 4).reshape(P, -1),
        wq=a["L2_ffn_Wq"], wo=a["L2_ffn_Wo"].reshape(HEADS, P, P).transpose(1, 0, 2).reshape(P, -1),
        g3w1=a["L3_gnn_W1"], g3w2=rows_first(a["L3_gnn_W2"][None]), f3wr=a["L3_ffn_Wr"],
        f3w1=a["L3_ffn_W1"].transpose(1, 0, 2).reshape(P, -1), f3w2=rows_first(a["L3_ffn_W2"]))
    wbig = np.concatenate([parts[n] for n, _ in WEIGHTS], 1)
    colp = dict(
        bn1=np.stack([a[f"L0_gnn_bn1_{k}"] for k in "gbmv"], 1),
        bn2=np.stack([a[f"L0_gnn_bn2_{k}"] for k in "gbmv"], 1),
        bih=a["L0_gnn_b_ih"].reshape(3, P).T, bhh=a["L0_gnn_b_hh"].reshape(3, P).T,
        bse=pad(a["L0_gnn_b_se"])[:, None], f0b1=a["L0_ffn_b1"].reshape(16, P).T, g1b=a["L1_gnn_W_b"][:, None],
        f1rb1=pad(a["L1_ffn_router_b1"])[:, None], f1b1=a["L1_ffn_expert_b1"].T, f1b2=a["L1_ffn_expert_b2"].T,
        g2bk=a["L2_gnn_bk"][:, None], g2bq=a["L2_gnn_bq"][:, None],
        g3eps=np.broadcast_to(a["L3_gnn_eps"][None], (P, 1)), g3b1=a["L3_gnn_b1"].reshape(2, P).T,
        lng=a["L3_ffn_ln_g"].T, lnb=a["L3_ffn_ln_b"].T, f3b1=a["L3_ffn_b1"].reshape(32, P).T,
        gateb=np.broadcast_to(a["L1_gnn_gate_b"][None], (P, 1)), rank=np.broadcast_to(rank, (P, CAND)),
        gatew=np.broadcast_to(a["L1_gnn_gate_w"], (P, 256)))
    cols = np.concatenate([colp[n] for n, _ in COLS], 1)
    rowp = dict(bmsg=a["L0_gnn_b_msg"], bg=a["L0_ffn_bg"], g1b=a["L1_gnn_W_b"], rb2=a["L1_ffn_router_b2"],
                bv=a["L2_gnn_bv"], bo=a["L2_gnn_bo"], g3b2=a["L3_gnn_b2"], br=a["L3_ffn_br"])
    rows = np.concatenate([rowp[n] for n, _ in ROWS])[None]
    b2 = np.concatenate([a["L0_ffn_b2"], pad(a["L1_ffn_expert_b3"], 8), a["L3_ffn_b2"]], 1)
    table = np.concatenate([a["L2_ffn_keys_table"], a["L2_ffn_values_table"]], 1)

    nc = _bacc.Bacc("TRN2", target_bir_lowering=False, num_devices=1)
    arrays, args = {}, []
    for name, arr in (("x", a["x"]), ("adj", a["adj"]), ("table", table), ("wbig", wbig), ("cols", cols),
                      ("rows", rows), ("b2", b2)):
        arr = np.ascontiguousarray(arr)
        arrays[f"in_{name}_dram"] = arr
        args.append(nc.dram_tensor(f"in_{name}_dram", arr.shape, mybir.dt.from_np(arr.dtype),
                                   kind="ExternalInput").ap())
    args.append(nc.dram_tensor("out_0_dram", a["x"].shape, F32, kind="ExternalOutput").ap())
    build(nc, *args)
    r = _run(nc, [arrays], core_ids=[0])
    return r.results[0]["out_0_dram"]
```
